# Optimizing a Trainium2 kernel written in Bass

```python
import numpy as np
import jax
import jax.numpy as jnp

def _softmax(x, axis=-1):
    return jax.nn.softmax(x, axis=axis)

def _gelu(x):
    return jax.nn.gelu(x, approximate=True)

def _silu(x):
    return jax.nn.silu(x)

def _sigmoid(x):
    return jax.nn.sigmoid(x)

def _layernorm(x, axis=-1, eps=1e-05):
    m = jnp.mean(x, axis=axis, keepdims=True)
    v = jnp.var(x, axis=axis, keepdims=True)
    return (x - m) / jnp.sqrt(v + eps)

def _scatter_add(tgt, idx, src, axis=0):
    return tgt.at[idx].add(src)

def _segment_sum(src, seg, n):
    return jax.ops.segment_sum(src, seg, n)
kernel_name = 'mk_adaln_d2_jaxref_r8_ca90e5'

def setup_inputs(seed: int=0):
    np.random.seed(seed)
    _w = jnp.asarray

    def _L0_attn_setup():
        import jax, jax.numpy as jnp
        import numpy as np
        HIDDEN = 128
        B, S = (8, 256)
        key = jax.random.key(seed)
        k1, k2, k3, k4 = jax.random.split(key, 4)
        gain = 1.2
        bound = gain * np.sqrt(6.0 / (HIDDEN + HIDDEN))
        return {'hidden_states': jax.random.normal(k1, (B, S, HIDDEN), dtype=jnp.float32), 'Wq': jax.random.uniform(k2, (HIDDEN, HIDDEN), jnp.float32, -bound, bound), 'bq': jnp.zeros((HIDDEN,), jnp.float32), 'Wv': jax.random.uniform(k3, (HIDDEN, HIDDEN), jnp.float32, -bound, bound), 'bv': jnp.zeros((HIDDEN,), jnp.float32), 'anomaly_matrix': jax.random.uniform(k4, (HIDDEN, HIDDEN), jnp.float32, -2.0, 2.0)}
    _L0_attn_in = _L0_attn_setup()

    def _L0_ffn_setup():
        import jax, jax.numpy as jnp
        import numpy as np
        D = 128
        H = 256
        E = 8
        TOP_K = 2
        N_SHARED = 1
        B, S = (2, 128)
        key = jax.random.key(seed)
        ks = jax.random.split(key, 12)
        sc = 0.02
        return {'hidden': jax.random.normal(ks[0], (B, S, D), jnp.float32), 'router_w': jax.random.normal(ks[1], (D, E), jnp.float32) * sc, 'router_b': jnp.zeros((E,), jnp.float32), 'sw1': jax.random.normal(ks[2], (D, H), jnp.float32) * sc, 'sb1': jnp.zeros((H,), jnp.float32), 'sw2': jax.random.normal(ks[3], (H, D), jnp.float32) * sc, 'sb2': jnp.zeros((D,), jnp.float32), 'rw1': jax.random.normal(ks[4], (E, D, H), jnp.float32) * sc, 'rb1': jnp.zeros((E, H), jnp.float32), 'rw2': jax.random.normal(ks[5], (E, H, D), jnp.float32) * sc, 'rb2': jnp.zeros((E, D), jnp.float32)}
    _L0_ffn_in = _L0_ffn_setup()
    _L0_c = _w((lambda *s: np.random.randn(*s).astype(np.float32) * 0.05)(8, 128))
    _L0_wmod = _w((lambda *s: np.random.randn(*s).astype(np.float32) * 0.05)(128, 6 * 128) * 128 ** (-0.5))

    def _L1_attn_setup():
        import jax, jax.numpy as jnp
        import numpy as np
        B, T, D, H = (4, 128, 128, 16)
        key = jax.random.key(seed)
        ks = jax.random.split(key, 7)
        x = jax.random.normal(ks[0], (B, T, D), dtype=jnp.float32)
        scale = 0.02
        Wq = jax.random.normal(ks[1], (D, D), dtype=jnp.float32) * scale
        Wk = jax.random.normal(ks[2], (D, D), dtype=jnp.float32) * scale
        Wv = jax.random.normal(ks[3], (D, D), dtype=jnp.float32) * scale
        bq = jax.random.normal(ks[4], (D,), dtype=jnp.float32) * scale
        bk = jax.random.normal(ks[5], (D,), dtype=jnp.float32) * scale
        bv = jax.random.normal(ks[6], (D,), dtype=jnp.float32) * scale
        temperature = jnp.ones((H, 1, 1), dtype=jnp.float32)
        return {'x': x, 'Wq': Wq, 'bq': bq, 'Wk': Wk, 'bk': bk, 'Wv': Wv, 'bv': bv, 'temperature': temperature}
    _L1_attn_in = _L1_attn_setup()

    def _L1_ffn_setup():
        import jax, jax.numpy as jnp
        import numpy as np
        B, S, H = (2, 512, 128)
        E, K, I = (8, 2, 176)
        key = jax.random.key(seed)
        ks = jax.random.split(key, 9)
        sc = 0.02
        return {'hidden_states': jax.random.normal(ks[0], (B, S, H), jnp.float32), 'gate_w': jax.random.normal(ks[1], (E, H), jnp.float32) * sc, 'w_gate': jax.random.normal(ks[2], (E, H, I), jnp.float32) * sc, 'w_up': jax.random.normal(ks[3], (E, H, I), jnp.float32) * sc, 'w_down': jax.random.normal(ks[4], (E, I, H), jnp.float32) * sc, 'sw_gate': jax.random.normal(ks[5], (H, I), jnp.float32) * sc, 'sw_up': jax.random.normal(ks[6], (H, I), jnp.float32) * sc, 'sw_down': jax.random.normal(ks[7], (I, H), jnp.float32) * sc, 'shared_gate_w': jax.random.normal(ks[8], (1, H), jnp.float32) * sc}
    _L1_ffn_in = _L1_ffn_setup()
    _L1_c = _w((lambda *s: np.random.randn(*s).astype(np.float32) * 0.05)(8, 128))
    _L1_wmod = _w((lambda *s: np.random.randn(*s).astype(np.float32) * 0.05)(128, 6 * 128) * 128 ** (-0.5))
    _d = {'L0_attn_hidden_states': _L0_attn_in['hidden_states'], 'L0_attn_Wq': _L0_attn_in['Wq'], 'L0_attn_bq': _L0_attn_in['bq'], 'L0_attn_Wv': _L0_attn_in['Wv'], 'L0_attn_bv': _L0_attn_in['bv'], 'L0_attn_anomaly_matrix': _L0_attn_in['anomaly_matrix'], 'L0_ffn_router_w': _L0_ffn_in['router_w'], 'L0_ffn_router_b': _L0_ffn_in['router_b'], 'L0_ffn_sw1': _L0_ffn_in['sw1'], 'L0_ffn_sb1': _L0_ffn_in['sb1'], 'L0_ffn_sw2': _L0_ffn_in['sw2'], 'L0_ffn_sb2': _L0_ffn_in['sb2'], 'L0_ffn_rw1': _L0_ffn_in['rw1'], 'L0_ffn_rb1': _L0_ffn_in['rb1'], 'L0_ffn_rw2': _L0_ffn_in['rw2'], 'L0_ffn_rb2': _L0_ffn_in['rb2'], 'L0_c': _L0_c, 'L0_wmod': _L0_wmod, 'L1_attn_Wq': _L1_attn_in['Wq'], 'L1_attn_bq': _L1_attn_in['bq'], 'L1_attn_Wk': _L1_attn_in['Wk'], 'L1_attn_bk': _L1_attn_in['bk'], 'L1_attn_Wv': _L1_attn_in['Wv'], 'L1_attn_bv': _L1_attn_in['bv'], 'L1_attn_temperature': _L1_attn_in['temperature'], 'L1_ffn_gate_w': _L1_ffn_in['gate_w'], 'L1_ffn_w_gate': _L1_ffn_in['w_gate'], 'L1_ffn_w_up': _L1_ffn_in['w_up'], 'L1_ffn_w_down': _L1_ffn_in['w_down'], 'L1_ffn_sw_gate': _L1_ffn_in['sw_gate'], 'L1_ffn_sw_up': _L1_ffn_in['sw_up'], 'L1_ffn_sw_down': _L1_ffn_in['sw_down'], 'L1_ffn_shared_gate_w': _L1_ffn_in['shared_gate_w'], 'L1_c': _L1_c, 'L1_wmod': _L1_wmod}
    _x0 = _d['L0_attn_hidden_states']
    _d['L0_attn_hidden_states'] = jax.random.normal(jax.random.fold_in(jax.random.key(seed), 1), (8, 256, 128), dtype=_x0.dtype)
    del _x0
    return _d

def reference(L0_attn_hidden_states, L0_attn_Wq, L0_attn_bq, L0_attn_Wv, L0_attn_bv, L0_attn_anomaly_matrix, L0_ffn_router_w, L0_ffn_router_b, L0_ffn_sw1, L0_ffn_sb1, L0_ffn_sw2, L0_ffn_sb2, L0_ffn_rw1, L0_ffn_rb1, L0_ffn_rw2, L0_ffn_rb2, L0_c, L0_wmod, L1_attn_Wq, L1_attn_bq, L1_attn_Wk, L1_attn_bk, L1_attn_Wv, L1_attn_bv, L1_attn_temperature, L1_ffn_gate_w, L1_ffn_w_gate, L1_ffn_w_up, L1_ffn_w_down, L1_ffn_sw_gate, L1_ffn_sw_up, L1_ffn_sw_down, L1_ffn_shared_gate_w, L1_c, L1_wmod):

    def _L0_attn_ref(hidden_states, Wq, bq, Wv, bv, anomaly_matrix):
        import jax, jax.numpy as jnp
        import numpy as np
        HIDDEN = 128
        B, S = (8, 256)
        input_norm = jnp.linalg.norm(hidden_states, axis=-1, keepdims=True)
        scaled = hidden_states / (input_norm + 1e-09)
        q = jnp.einsum('bsh,oh->bso', scaled, Wq) + bq
        v = jnp.einsum('bsh,oh->bso', scaled, Wv) + bv
        tq = jnp.einsum('bsh,hk->bsk', q, anomaly_matrix)
        scores = jnp.einsum('bsh,bth->bst', q, tq) / jnp.sqrt(jnp.float32(HIDDEN))
        probs = jax.nn.softmax(scores, axis=-1)
        ctx = jnp.einsum('bst,bth->bsh', probs, v)
        return ctx * input_norm

    def _L0_ffn_ref(hidden, router_w, router_b, sw1, sb1, sw2, sb2, rw1, rb1, rw2, rb2):
        import jax, jax.numpy as jnp
        import numpy as np
        D = 128
        H = 256
        E = 8
        TOP_K = 2
        N_SHARED = 1
        B, S = (2, 128)
        b, s, d = hidden.shape
        T = b * s
        flat = hidden.reshape(T, d)
        router_logits = flat @ router_w + router_b
        router_probs = jax.nn.softmax(router_logits, axis=-1)
        topk_probs, topk_idx = jax.lax.top_k(router_probs, TOP_K)
        weights = jnp.zeros_like(router_probs).at[jnp.arange(T)[:, None], topk_idx].add(topk_probs)
        sh = jax.nn.gelu(flat @ sw1 + sb1, approximate=False)
        shared_out = (sh @ sw2 + sb2) / N_SHARED
        h1 = jax.nn.gelu(jnp.einsum('td,edh->teh', flat, rw1) + rb1[None], approximate=False)
        expert_out = jnp.einsum('teh,ehd->ted', h1, rw2) + rb2[None]
        mixed = jnp.einsum('ted,te->td', expert_out, weights)
        return (shared_out + mixed).reshape(b, s, d)

    def _L1_attn_ref(x, Wq, bq, Wk, bk, Wv, bv, temperature):
        import jax, jax.numpy as jnp
        import numpy as np
        B, T, D, H = (4, 128, 128, 16)
        b, t, d = x.shape
        h = temperature.shape[0]
        dh = d // h
        q = (x @ Wq + bq).reshape(b, h, dh, t)
        k = (x @ Wk + bk).reshape(b, h, dh, t)
        v = (x @ Wv + bv).reshape(b, h, dh, t)
        attn = jnp.einsum('bhdt,bhds->bhts', k, v) * temperature
        attn = jax.nn.softmax(attn, axis=-1)
        out = jnp.einsum('bhdt,bhts->bhds', q, attn)
        return out.reshape(b, t, d)

    def _L1_ffn_ref(hidden_states, gate_w, w_gate, w_up, w_down, sw_gate, sw_up, sw_down, shared_gate_w):
        import jax, jax.numpy as jnp
        import numpy as np
        B, S, H = (2, 512, 128)
        E, K, I = (8, 2, 176)
        b, s, h = hidden_states.shape
        x = hidden_states.reshape(-1, h)
        logits = jnp.einsum('th,eh->te', x, gate_w)
        probs = jax.nn.softmax(logits.astype(jnp.float32), axis=-1)
        topk_w, topk_i = jax.lax.top_k(probs, K)
        topk_w = topk_w / jnp.sum(topk_w, axis=-1, keepdims=True)
        combine = jnp.sum(jax.nn.one_hot(topk_i, E, dtype=topk_w.dtype) * topk_w[..., None], axis=1)
        combine = combine.astype(x.dtype)
        g = jnp.einsum('th,ehi->eti', x, w_gate)
        u = jnp.einsum('th,ehi->eti', x, w_up)
        eo = jnp.einsum('eti,eih->eth', jax.nn.silu(g) * u, w_down)
        out = jnp.einsum('te,eth->th', combine, eo)
        sg = jax.nn.sigmoid(jnp.einsum('th,oh->to', x, shared_gate_w))
        so = jax.nn.silu(x @ sw_gate) * (x @ sw_up) @ sw_down
        out = out + sg * so
        return out.reshape(b, s, h)
    x = L0_attn_hidden_states
    mod = (_silu(L0_c) @ L0_wmod).reshape(L0_c.shape[0], 6, 1, -1)
    sa, ca, ga, sb, cb, gb = (mod[:, 0], mod[:, 1], mod[:, 2], mod[:, 3], mod[:, 4], mod[:, 5])
    ga = (2 * (ga >= 0) - 1) * jnp.maximum(jnp.abs(ga), 0.25)
    gb = (2 * (gb >= 0) - 1) * jnp.maximum(jnp.abs(gb), 0.25)
    h = _layernorm(x, axis=-1) * (1 + ca) + sa
    x = x + ga * _L0_attn_ref(h, L0_attn_Wq, L0_attn_bq, L0_attn_Wv, L0_attn_bv, L0_attn_anomaly_matrix)
    h = _layernorm(x, axis=-1) * (1 + cb) + sb
    x = x + gb * _L0_ffn_ref(h, L0_ffn_router_w, L0_ffn_router_b, L0_ffn_sw1, L0_ffn_sb1, L0_ffn_sw2, L0_ffn_sb2, L0_ffn_rw1, L0_ffn_rb1, L0_ffn_rw2, L0_ffn_rb2)
    mod = (_silu(L1_c) @ L1_wmod).reshape(L1_c.shape[0], 6, 1, -1)
    sa, ca, ga, sb, cb, gb = (mod[:, 0], mod[:, 1], mod[:, 2], mod[:, 3], mod[:, 4], mod[:, 5])
    ga = (2 * (ga >= 0) - 1) * jnp.maximum(jnp.abs(ga), 0.25)
    gb = (2 * (gb >= 0) - 1) * jnp.maximum(jnp.abs(gb), 0.25)
    h = _layernorm(x, axis=-1) * (1 + ca) + sa
    x = x + ga * _L1_attn_ref(h, L1_attn_Wq, L1_attn_bq, L1_attn_Wk, L1_attn_bk, L1_attn_Wv, L1_attn_bv, L1_attn_temperature)
    h = _layernorm(x, axis=-1) * (1 + cb) + sb
    x = x + gb * _L1_ffn_ref(h, L1_ffn_gate_w, L1_ffn_w_gate, L1_ffn_w_up, L1_ffn_w_down, L1_ffn_sw_gate, L1_ffn_sw_up, L1_ffn_sw_down, L1_ffn_shared_gate_w)
    return x

_drawn_inputs = setup_inputs


def setup_inputs(seed=0):
    import zlib

    import numpy as np

    out = dict(_drawn_inputs(seed))
    spreads = {'L0_attn_bq': (0.0, 0.8),
     'L0_attn_bv': (0.0, 0.1),
     'L0_ffn_router_b': (0.0, 0.8),
     'L0_ffn_sb1': (0.0, 0.8),
     'L0_ffn_sb2': (0.0, 0.297),
     'L0_ffn_rb1': (0.0, 0.8),
     'L0_ffn_rb2': (0.0, 0.8),
     'L1_attn_temperature': (1.0, 0.6)}
    factors = {'L0_attn_Wq': 8.0,
     'L0_attn_Wv': 3.048,
     'L0_attn_anomaly_matrix': 8.0,
     'L0_ffn_router_w': 8.0,
     'L0_ffn_sw1': 6.305,
     'L0_ffn_sw2': 5.774,
     'L0_ffn_rw1': 8.0,
     'L0_ffn_rw2': 8.0,
     'L1_attn_Wq': 8.0,
     'L1_attn_bq': 8.0,
     'L1_attn_Wk': 8.0,
     'L1_attn_bk': 8.0,
     'L1_attn_Wv': 8.0,
     'L1_attn_bv': 8.0,
     'L1_ffn_gate_w': 8.0,
     'L1_ffn_w_gate': 8.0,
     'L1_ffn_w_up': 8.0,
     'L1_ffn_w_down': 8.0,
     'L1_ffn_sw_gate': 8.0,
     'L1_ffn_sw_up': 8.0,
     'L1_ffn_sw_down': 8.0,
     'L1_ffn_shared_gate_w': 8.0,
     'L1_c': 8.0,
     'L1_wmod': 8.0}
    for name, (base, spread) in spreads.items():
        noise = np.random.default_rng([zlib.crc32(name.encode()), seed]).standard_normal(out[name].shape)
        drawn = base * np.exp(spread * noise) if base else spread * noise
        out[name] = jnp.asarray(drawn.astype(out[name].dtype))
    for name, factor in factors.items():
        out[name] = (out[name] * factor).astype(out[name].dtype)
    return out
```

```python
from contextlib import ExitStack

import concourse.bass as bass
from concourse import mybir

D = 128
B, S = 8, 256
TOK = B * S
NT = TOK // D
TPB = S // D
NP = B // 2
TPP = NT // NP
PT = TOK // NP
E = 8
H0 = 256
C0 = H0 // D
H1 = 176
F1 = (E + 1) * H1
CH1 = [(c, min(D, F1 - c)) for c in range(0, F1, D)]
HEADS, DH = 16, 8
HPG = 4
NG = B * HEADS // HPG
GPB = HEADS // HPG
GPP = NG // NP
GT = HPG * DH * 2
KVR = 4
EPS = 1e-5


def two_block_adaln(nc, a, out, scratch):
    fp32, fp32r = mybir.dt.float32, mybir.dt.float32r
    bf16, u32 = mybir.dt.bfloat16, mybir.dt.uint32
    ACT, ALU, AX = mybir.ActivationFunctionType, mybir.AluOpType, mybir.AxisListType

    with ExitStack() as ctx:
        def sb(name, shape, dt=fp32):
            return ctx.enter_context(nc.sbuf_tensor(name, shape, dt))

        def sem(name):
            return ctx.enter_context(nc.semaphore(name))

        X = sb("X", [128, NT, D])
        SC = sb("SC", [128, NT, D])
        XT = 2 * [sb(f"XT{k}", [128, TOK]) for k in range(2)]
        qT = sb("qT", [128, TOK])
        PR = sb("PR", [128, NT, S])
        with ExitStack() as early:
            def sb_early(name, shape, dt=fp32):
                return early.enter_context(nc.sbuf_tensor(name, shape, dt))

            tqT = sb_early("tqT", [128, TOK])
            V = sb_early("V", [128, NT, D])
            PRT = sb_early("PRT", [128, B, TPB, S])
        VS = sb("VS", [128, 2, GPP, S], fp32r)
        KS = sb("KS", [128, 2, GPP, S], fp32r)
        EX = PR[:, :, :].rearrange("p t s -> p (t s)").rearrange("p (r j n) -> p r j n", r=2, j=HPG)
        ident = sb("ident", [128, 128])
        identb = sb("identb", [128, 128], bf16)
        iota = sb("iota", [128, E])

        yT = sb("yT", [128, 2, PT])
        O = sb("O", [128, 2, GPB, S])

        w0q = sb("w0q", [128, D]); w0v = sb("w0v", [128, D]); w0a = sb("w0a", [128, D])
        b0q = sb("b0q", [128, 1]); b0v = sb("b0v", [128, D])
        rw0 = sb("rw0", [128, E]); rb0 = sb("rb0", [128, E])
        up0 = sb("up0", [128, E + 1, H0]); ub0 = sb("ub0", [128, E + 1, C0])
        dn0 = sb("dn0", [128, E + 1, C0, D]); db0 = sb("db0", [E + 1, D])
        w1q = sb("w1q", [128, D]); w1vk = sb("w1vk", [128, 2 * D]); b1q = sb("b1q", [128, 1])
        b1v = sb("b1v", [128, D]); b1k = sb("b1k", [128, D]); b1kt = sb("b1kt", [128, 2, D])
        temp = sb("temp", [128, 2])
        rw1 = sb("rw1", [128, E + 1])
        gate1 = up0[:, :, :].rearrange("p e h -> p (e h)")[:, 0:F1]
        up1 = dn0[:, :, :, :].rearrange("p e c d -> p (e c d)")[:, 0:F1]
        dn1 = sb("dn1", [128, len(CH1), D])
        wmod = sb("wmod", [128, 2, 6 * D])
        cT = sb("cT", [128, 2, B]); scT = sb("scT", [128, 2, B]); scB = PRT[:, 0:B // 2, :, :].rearrange("p b j (k d) -> p (b j k) d", d=D).rearrange("p (l b) d -> p l b d", l=2)
        sel0f = yT[0:3 * E, :, :].rearrange("p r n -> p (r n)"); sel0 = sb("sel0", [3 * E, E * D], bf16)
        sel1f = O[0:3 * (E + 1), :, :, :].rearrange("p r g n -> p (r g n)")[:, 0:F1]; sel1 = sb("sel1", [3 * (E + 1), F1], bf16)
        mrow = sb("mrow", [128, B, 3, D])
        mrow1 = sb("mrow1", [128, B, D])
        mcol = sb("mcol", [128, 2, 6, B])
        gtmp = tqT[:, 0:B * D].rearrange("p (b d) -> p b d", b=B)
        gtmc = sb("gtmc", [128, 2, 6, B])

        st = sb("st", [128, 4, NT, 6]); mv = sb("mv", [128, 4, NT, 2])
        ve = sb("ve", [128, 4, NT]); rstd = sb("rstd", [128, 4, NT])
        mhalf = sb("mhalf", [128, NT]); phalf = sb("phalf", [128, NT])
        sq = sb("sq", [128, D]); ss = sb("ss", [128, NT]); nrm = sb("nrm", [128, NT])
        rn = sb("rn", [128, NT])
        nm0 = sb("nm0", [128, NT]); nms0 = sb("nms0", [128, NT]); Z0 = sb("Z0", [128, NT])
        nz = sb("nz", [128, NT])
        ctmp = sb("ctmp", [128, TPB, D])
        lg = sb("lg", [128, 2, NT, E + 1]); ld = sb("ld", [128, 2, NT, E + 1])
        ex = sb("ex", [128, 2, NT, E + 1]); nmr = sb("nmr", [128, 2, NT])
        top = sb("top", [128, 2, NT, 8]); tix = sb("tix", [128, 2, NT, 8], u32)
        tif = sb("tif", [128, 2, NT, 2]); tden = sb("tden", [128, 2, NT]); trc = sb("trc", [128, 2, NT])
        tw = sb("tw", [128, 2, NT, 2]); oh = sb("oh", [128, 2, NT, 2, E])
        W = sb("W", [128, 2, NT, E + 1]); res = sb("res", [128, 2, NT, E + 1])
        WP = sb("WP", [128, 2, NT, 3 * (E + 1)], bf16)
        WPT = [sb(f"WPT{k}", [3 * (E + k), TOK], bf16) for k in range(2)]
        WT = qT[0:E + 1, :]

        act_out = wmod[:, :, :].rearrange("p l n -> p (l n)").rearrange("p (r n) -> p r n", r=3)
        gu = sb("gu", [128, 2, PT])
        hid = sb("hid", [128, 3, PT])

        kvf = sb("kvf", [128, 2, 2, D])
        kvs = sb("kvs", [128, KVR, 4, D], fp32r)
        nm1 = sb("nm1", [128, NG, HPG, 2]); Z1 = sb("Z1", [128, NG, HPG, 2])
        rz1 = sb("rz1", [128, NG, HPG, 2])
        qs4 = hid[:, 0, :].rearrange("p (r j h c d) -> p r j h c d", r=2, j=HPG, h=2, c=HPG)
        qs = hid[:, 1, 0:4 * HPG * DH].rearrange("p (r j h d) -> p r j h d", r=2, j=HPG, h=2)
        AO = SC

        P = ctx.enter_context(nc.psum_tensor("P", [128, 8, PT], fp32))

        names = ["ld_c", "ld_b", "ld_w0", "ld_f0", "ld_w1", "ld_f1", "silu_done", "scb_done",
                 "sel_done", "mod_ps", "mod_sb", "ve_ready", "rstd_ready", "ss_ready", "nrm_ready",
                 "xn_ready", "xt_ps", "xt_sb", "q0_ps", "q0_sb", "v0_ps", "v0_sb", "tq_ps", "tq_sb",
                 "s0_ps", "nm0_ready", "p0_ready", "pt_ps", "pt_sb", "c0_ps", "c0_read",
                 "r_ps", "rd_ready", "rex_ready", "r_read", "w_ready", "wt_ps", "wt_sb",
                 "up_ps", "act_ready", "bc_ps", "hid_ready", "hid_used", "y_ps", "y_sb", "z_ps",
                 "z_read", "g_ps", "u_ps", "gact_ready", "gact_used", "u_read", "q1_ps", "q1_sb", "kv_ps", "kv_read",
                 "kvs_ready", "s1_ps", "nm1_ready", "e1_ready", "qs_ready", "c1_ps",
                 "o1_ready", "v_step", "pool_const", "x_done"]
        s = {n: sem(n) for n in names}
        ld_x = [sem(f"ld_x{p}") for p in range(NP)]
        kv_out = [sem(f"kv_out{r}") for r in range(KVR)]
        kv_in = [sem(f"kv_in{p}") for p in range(NP)]
        ao_out = [sem(f"ao_out{b}") for b in range(B)]
        ao_in = [sem(f"ao_in{b}") for b in range(B)]
        stored = sem("stored")
        block = ctx.enter_context(nc.Block())

        def per_partition(v, n):
            return v.rearrange("(p n) -> p n", n=n)

        def tiles(p):
            return range(TPP * p, TPP * p + TPP)

        def cols(p):
            return slice(PT * p, PT * p + PT)

        N_LD = {"ld_c": 5, "ld_b": 4, "ld_w0": 7, "ld_f0": 7, "ld_w1": 6, "ld_f1": 9}

        @block.sync
        def _(sp):
            def load(dst, src, name):
                sp.dma_start(dst, src).then_inc(s[name], 16)

            load(cT[:, 0, :], a["c0T"], "ld_c")
            load(wmod[:, 0, :], a["L0_wmod"], "ld_c")
            for p in range(NP):
                sp.dma_start(X[:, TPP * p:TPP * p + TPP, :],
                             a["x"].rearrange("(t p) d -> p t d", p=128)[:, TPP * p:TPP * p + TPP, :]
                             ).then_inc(ld_x[p], 16)
                if p == 0:
                    load(cT[:, 1, :], a["c1T"], "ld_c")
                    load(ident[:, :], a["ident"], "ld_c")
                    load(wmod[:, 1, :], a["L1_wmod"], "ld_c")
            load(iota[:, :], a["iota"].partition_broadcast(128), "ld_b")
            load(sel0f[:, :], a["sel0"], "ld_b")
            load(sel1f[:, :], a["sel1"], "ld_b")
            load(rb0[:, :], a["L0_ffn_router_b"].partition_broadcast(128), "ld_b")
            load(w0q[:, :], a["WqT0"], "ld_w0")
            load(w0v[:, :], a["WvT0"], "ld_w0")
            load(w0a[:, :], a["L0_attn_anomaly_matrix"], "ld_w0")
            load(b0q[:, :], per_partition(a["L0_attn_bq"], 1), "ld_w0")
            load(b0v[:, :], a["L0_attn_bv"].partition_broadcast(128), "ld_w0")
            load(rw0[:, :], a["L0_ffn_router_w"], "ld_w0")
            load(b1v[:, :], a["L1_attn_bv"].partition_broadcast(128), "ld_w0")
            load(up0[:, 0:E, :], a["L0_ffn_rw1"].rearrange("e d h -> d e h"), "ld_f0")
            load(up0[:, E, :], a["L0_ffn_sw1"], "ld_f0")
            load(ub0[:, :, :], a["ub0T"].rearrange("p (e c) -> p e c", c=C0), "ld_f0")
            load(dn0[:, 0:E, :, :], a["L0_ffn_rw2"].rearrange("e (c p) d -> p e c d", p=128), "ld_f0")
            load(dn0[:, E, :, :], a["L0_ffn_sw2"].rearrange("(c p) d -> p c d", p=128), "ld_f0")
            load(db0[0:E, :], a["L0_ffn_rb2"], "ld_f0")
            load(db0[E:E + 1, :], a["L0_ffn_sb2"].rearrange("(o d) -> o d", o=1), "ld_f0")
            load(w1q[:, :], a["L1_attn_Wq"], "ld_w1")
            load(w1vk[:, 0:D], a["L1_attn_Wv"], "ld_w1")
            load(w1vk[:, D:2 * D], a["L1_attn_Wk"], "ld_w1")
            load(b1q[:, :], per_partition(a["L1_attn_bq"], 1), "ld_w1")
            load(b1k[:, :], a["L1_attn_bk"].partition_broadcast(128), "ld_w1")
            load(temp[:, :], a["tempT"], "ld_w1")

            def load_experts_1():
                sp.wait_ge(s["y_ps"], NP)
                load(rw1[:, 0:E], a["gate_wT"], "ld_f1")
                load(rw1[:, E:E + 1], a["shared_gateT"], "ld_f1")
                load(gate1[:, 0:E * H1].rearrange("p (e i) -> p e i", e=E), a["L1_ffn_w_gate"].rearrange("e d i -> d e i"), "ld_f1")
                load(gate1[:, E * H1:F1], a["L1_ffn_sw_gate"], "ld_f1")
                load(up1[:, 0:E * H1].rearrange("p (e i) -> p e i", e=E), a["L1_ffn_w_up"].rearrange("e d i -> d e i"), "ld_f1")
                load(up1[:, E * H1:F1], a["L1_ffn_sw_up"], "ld_f1")
                load(dn1[:, 0:E * H1 // D, :], a["L1_ffn_w_down"].rearrange("e i d -> (e i) d").rearrange("(c p) d -> p c d", p=128), "ld_f1")
                load(dn1[:, E * H1 // D, :], a["L1_ffn_sw_down"][0:D, :], "ld_f1")
                load(dn1[0:H1 - D, E * H1 // D + 1, :], a["L1_ffn_sw_down"][D:H1, :], "ld_f1")

            def kv_store(p):
                for t in tiles(p):
                    sp.wait_ge(s["kvs_ready"], t + 1)
                    sp.dma_start(scratch["kv"][:, t * D:(t + 1) * D, :].rearrange("o p c -> p o c"),
                                 kvs[:, t % KVR, :, :].bitcast(fp32)).then_inc(kv_out[t % KVR], 16)

            def kv_load(p, stored_pairs):
                for r in range(KVR):
                    sp.wait_ge(kv_out[r], 16 * TPP * stored_pairs // KVR)
                if p >= 2:
                    sp.wait_ge(s["s1_ps"], HPG * GPP * (p - 1))
                for dst, parts in ((VS, (0, 1, 0)), (KS, (2, 2, 3))):
                    for j in range(HPG):
                        for n, o in enumerate(parts):
                            src = scratch["kv"][o, cols(p), :].rearrange(
                                "(g j d h) c -> j d g (h c)", j=HPG, d=DH, h=2)[j]
                            sp.dma_start(dst[32 * j + DH * n:32 * j + DH * n + DH, p % 2, :, :].bitcast(fp32), src
                                         ).then_inc(kv_in[p], 16)

            def attention_out(b):
                sp.wait_ge(s["o1_ready"], GPB * (b + 1))
                for j in range(HPG):
                    dst = scratch["ao"][b * S:(b + 1) * S, :].rearrange(
                        "(g j d h) c -> j d g (h c)", j=HPG, d=DH, h=2)[j]
                    sp.dma_start(dst, O[32 * j:32 * j + DH, b % 2, :, :]).then_inc(ao_out[b], 16)
                sp.wait_ge(ao_out[b], 16 * HPG)
                sp.dma_start(AO[:, TPB * b:TPB * b + TPB, :],
                             scratch["ao"][b * S:(b + 1) * S, :].rearrange("(t p) c -> p t c", p=128)
                             ).then_inc(ao_in[b], 16)

            for p in range(2):
                kv_store(p)
                kv_load(p, p + 1)
            kv_store(2)
            kv_store(3)
            load_experts_1()
            for p in range(2, NP):
                kv_load(p, NP)
                attention_out(2 * p - 4)
                attention_out(2 * p - 3)
            attention_out(B - 4)
            attention_out(B - 3)
            attention_out(B - 2)
            attention_out(B - 1)
            for p in range(NP):
                sp.wait_ge(s["z_read"], NP + p + 1)
                sp.dma_start(out.rearrange("(t p) d -> p t d", p=128)[:, TPP * p:TPP * p + TPP, :],
                             X[:, TPP * p:TPP * p + TPP, :]).then_inc(stored, 16)
            sp.wait_ge(stored, 16 * NP)

        @block.gpsimd
        def _(pool):
            nc.gpsimd.memset(mhalf[:, :], -0.5).then_inc(s["pool_const"], 1)
            nc.gpsimd.memset(phalf[:, :], 0.5).then_inc(s["pool_const"], 1)
            pool.wait_ge(s["pool_const"], 2)

            def root(k, p):
                pool.wait_ge(s["ve_ready"], NP * k + p + 1)
                nc.gpsimd.tensor_tensor(rstd[:, k, tiles(p)[0]:tiles(p)[-1] + 1],
                                        ve[:, k, tiles(p)[0]:tiles(p)[-1] + 1],
                                        mhalf[:, 0:TPP], ALU.pow).then_inc(s["rstd_ready"], 1)

            for p in range(NP):
                root(0, p)
            for p in range(NP):
                pool.wait_ge(s["ss_ready"], p + 1)
                nc.gpsimd.tensor_tensor(nrm[:, TPP * p:TPP * p + TPP], ss[:, TPP * p:TPP * p + TPP],
                                        phalf[:, 0:TPP], ALU.pow).then_inc(s["nrm_ready"], 1)
            for k in range(1, 4):
                for p in range(NP):
                    root(k, p)

        @block.vector
        def _(dve):
            v = nc.vector
            step = [0]

            def link(ins):
                step[0] += 1
                ins.then_inc(s["v_step"], 1)
                dve.wait_ge(s["v_step"], step[0])

            def guard(dst, gate, tmp):
                v.tensor_scalar(tmp, gate, 0.0, 2.0, ALU.is_ge, ALU.mult)
                link(v.scalar_tensor_tensor(out=gate, in0=gate, scalar=-1.0, in1=gate, op0=ALU.mult, op1=ALU.max))
                link(v.tensor_scalar(gate, gate, 0.25, None, ALU.max))
                return v.scalar_tensor_tensor(out=dst, in0=tmp, scalar=-1.0, in1=gate,
                                              op0=ALU.add, op1=ALU.mult)

            def ln_stats(k, p):
                for t in tiles(p):
                    last = v.bn_stats(st[:, k, t, :], X[:, t, :])
                link(last)
                for t in tiles(p):
                    last = v.bn_aggr(mv[:, k, t, :], st[:, k, t, :])
                link(last)
                ts = slice(TPP * p, TPP * p + TPP)
                v.tensor_scalar(ve[:, k, ts], mv[:, k, ts, 1], EPS, None, ALU.add
                                ).then_inc(s["ve_ready"], 1)

            def ln_apply(k, p):
                dve.wait_ge(s["rstd_ready"], NP * k + p + 1)
                if k >= 1:
                    dve.wait_ge(s["xt_ps"], NP * (k - 1) + p + 1)
                for t in tiles(p):
                    last = v.tensor_scalar(SC[:, t, :], X[:, t, :], mv[:, k, t, 0:1],
                                           rstd[:, k, t:t + 1], ALU.subtract, ALU.mult)
                return last

            dve.wait_ge(s["silu_done"], 1)
            for l in range(2):
                last = v.tensor_copy(scB[:, l, :, :], scT[:, l, :].unsqueeze(2).broadcast_to([128, B, D]))
            last.then_inc(s["scb_done"], 1)
            for p in range(NP):
                dve.wait_ge(ld_x[p], 16)
                ln_stats(0, p)
            for b in range(B):
                dve.wait_ge(s["mod_ps"], b + 1)
                bank = P[:, b, 0:3 * D].rearrange("p (m d) -> p m d", m=3)
                v.tensor_copy(mrow[:, b, 0, :], bank[:, 0, :])
                v.tensor_scalar(mrow[:, b, 1, :], bank[:, 1, :], 1.0, None, ALU.add)
                link(v.tensor_copy(mrow[:, b, 2, :], bank[:, 2, :]))
                v.tensor_copy(mrow[:, b, 2, :], mrow[:, b, 2, :]).then_inc(s["mod_sb"], 1)
            link(v.tensor_scalar(sq[:, 0:1], mrow[:, 0, 2, 0:1], 1.0, None, ALU.mult))
            guard(mrow[:, :, 2, :], mrow[:, :, 2, :], gtmp[:, :, :])
            for h in range(2):
                dve.wait_ge(s["mod_ps"], B + h + 1)
                link(v.tensor_copy(mrow1[:, 4 * h:4 * h + 4, :],
                                   P[:, h, :].rearrange("p (b d) -> p b d", d=D)))
                v.tensor_copy(sq[:, 0:1], mrow1[:, 0, 0:1]).then_inc(s["mod_sb"], 1)
            dve.wait_ge(s["mod_ps"], B + 3)
            link(v.tensor_copy(mcol[:, :, :, :], P[:, 2, 0:12 * B].rearrange("p (l m b) -> p l m b", l=2, m=6)))
            v.tensor_copy(sq[:, 0:1], mcol[:, 0, 0, 0:1]).then_inc(s["mod_sb"], 1)
            link(guard(mrow1[:, :, :], mrow1[:, :, :], gtmp[:, :, :]))
            for m in (1, 4):
                v.tensor_scalar(mcol[:, :, m, :], mcol[:, :, m, :], 1.0, None, ALU.add)
            link(guard(mcol[:, :, 5, :], mcol[:, :, 5, :], gtmc[:, :, 5, :]))

            for p in range(NP):
                link(ln_apply(0, p))
                for b in (2 * p, 2 * p + 1):
                    ts = slice(TPB * b, TPB * b + TPB)
                    link(v.tensor_tensor(SC[:, ts, :], SC[:, ts, :],
                                         mrow[:, b, 1, :].unsqueeze(1).broadcast_to([128, TPB, D]), ALU.mult))
                    link(v.tensor_tensor(SC[:, ts, :], SC[:, ts, :],
                                         mrow[:, b, 0, :].unsqueeze(1).broadcast_to([128, TPB, D]), ALU.add))
                for t in tiles(p):
                    link(v.scalar_tensor_tensor(out=sq[:, :], in0=SC[:, t, :], scalar=1.0, in1=SC[:, t, :],
                                                op0=ALU.mult, op1=ALU.mult, accum_out=ss[:, t:t + 1]))
                v.tensor_copy(sq[:, 0:1], ss[:, 4 * p + 3:4 * p + 4]).then_inc(s["ss_ready"], 1)
            for p in range(NP):
                dve.wait_ge(s["nrm_ready"], p + 1)
                ts = slice(TPP * p, TPP * p + TPP)
                link(v.tensor_scalar(rn[:, ts], nrm[:, ts], 1e-9, None, ALU.add))
                link(v.reciprocal(rn[:, ts], rn[:, ts]))
                for t in tiles(p):
                    last = v.tensor_scalar(SC[:, t, :], SC[:, t, :], rn[:, t:t + 1], None, ALU.mult)
                last.then_inc(s["xn_ready"], 1)
            dve.wait_ge(s["ld_w0"], 16 * N_LD["ld_w0"])
            for p in range(NP):
                dve.wait_ge(s["v0_ps"], p + 1)
                v.tensor_tensor(V[:, TPP * p:TPP * p + TPP, :],
                                P[:, bank_v0[p], :].rearrange("p (t d) -> p t d", d=D),
                                b0v[:, :].unsqueeze(1).broadcast_to([128, TPP, D]), ALU.add).then_inc(s["v0_sb"], 1)
            for p in range(NP):
                dve.wait_ge(s["tq_ps"], p + 1)
                v.tensor_copy(tqT[:, cols(p)], P[:, bank_tq[p], :]).then_inc(s["tq_sb"], 1)
            for b in range(B):
                dve.wait_ge(s["s0_ps"], b + 1)
                ts = slice(TPB * b, TPB * b + TPB)
                link(v.reduce_max(nm0[:, ts], P[:, bank_s0[b], :].rearrange("p (i t) -> p i t", i=TPB), AX.X))
                v.tensor_scalar(nms0[:, ts], nm0[:, ts], -(D ** -0.5), None, ALU.mult).then_inc(s["nm0_ready"], 1)
            for b in range(B):
                dve.wait_ge(s["c0_ps"], b + 1)
                ts = slice(TPB * b, TPB * b + TPB)
                link(v.reciprocal(nz[:, ts], Z0[:, ts]))
                link(v.tensor_tensor(nz[:, ts], nz[:, ts], nrm[:, ts], ALU.mult))
                for i in range(TPB):
                    t = TPB * b + i
                    last = v.scalar_tensor_tensor(out=ctmp[:, i, :], in0=P[:, bank_c0[b], i * D:(i + 1) * D],
                                                  scalar=nz[:, t:t + 1], in1=mrow[:, b, 2, :],
                                                  op0=ALU.mult, op1=ALU.mult)
                link(last)
                v.tensor_tensor(X[:, ts, :], X[:, ts, :], ctmp[:, :, :], ALU.add).then_inc(s["c0_read"], 1)
                dve.wait_ge(s["c0_read"], b + 1)

            def router(l, p):
                n, n9 = NP * l + p, E + l
                ts = slice(TPP * p, TPP * p + TPP)
                dve.wait_ge(s["r_ps"], n + 1)
                R = P[:, bank_r[n], 0:TPP * n9].rearrange("p (t e) -> p t e", e=n9)
                if l == 0:
                    link(v.tensor_tensor(lg[:, l, ts, 0:E], R, rb0[:, :].unsqueeze(1).broadcast_to([128, TPP, E]), ALU.add))
                else:
                    link(v.tensor_copy(lg[:, l, ts, :], R))
                link(v.reduce_max(nmr[:, l, ts], lg[:, l, ts, 0:E], AX.X))
                if l == 1:
                    v.tensor_scalar(ld[:, l, ts, E], lg[:, l, ts, E], -1.0, None, ALU.mult)
                v.tensor_tensor(ld[:, l, ts, 0:E], lg[:, l, ts, 0:E],
                                nmr[:, l, ts].unsqueeze(2).broadcast_to([128, TPP, E]), ALU.subtract
                                ).then_inc(s["rd_ready"], 1)
                dve.wait_ge(s["rex_ready"], n + 1)
                for t in tiles(p):
                    last = v.max(top[:, l, t, :], ex[:, l, t, 0:E])
                link(last)
                if l == 0:
                    v.memset(W[:, l, ts, E], 1.0)
                    v.reduce_sum(tden[:, l, ts], ex[:, l, ts, 0:E], AX.X)
                else:
                    v.tensor_scalar(res[:, l, ts, E], ex[:, l, ts, E], 1.0, None, ALU.add)
                    v.reduce_sum(tden[:, l, ts], top[:, l, ts, 0:2], AX.X)
                for t in tiles(p):
                    last = v.max_index(tix[:, l, t, :], top[:, l, t, :], ex[:, l, t, 0:E])
                link(last)
                link(v.tensor_copy(tif[:, l, ts, :], tix[:, l, ts, 0:2]))
                if l == 1:
                    v.reciprocal(W[:, l, ts, E], res[:, l, ts, E])
                link(v.reciprocal(trc[:, l, ts], tden[:, l, ts]))
                link(v.tensor_tensor(tw[:, l, ts, :], top[:, l, ts, 0:2],
                                     trc[:, l, ts].unsqueeze(2).broadcast_to([128, TPP, 2]), ALU.mult))
                for k in range(2):
                    last = v.tensor_tensor(oh[:, l, ts, k, :], iota[:, :].unsqueeze(1).broadcast_to([128, TPP, E]),
                                           tif[:, l, ts, k].unsqueeze(2).broadcast_to([128, TPP, E]), ALU.is_equal)
                link(last)
                for k in range(2):
                    last = v.tensor_tensor(oh[:, l, ts, k, :], oh[:, l, ts, k, :],
                                           tw[:, l, ts, k].unsqueeze(2).broadcast_to([128, TPP, E]), ALU.mult)
                link(last)
                link(v.tensor_tensor(W[:, l, ts, 0:E], oh[:, l, ts, 0, :], oh[:, l, ts, 1, :], ALU.add))
                link(v.tensor_copy(WP[:, l, ts, 0:n9], W[:, l, ts, 0:n9]))
                link(v.tensor_tensor(res[:, l, ts, 0:n9], W[:, l, ts, 0:n9], WP[:, l, ts, 0:n9], ALU.subtract))
                link(v.tensor_copy(WP[:, l, ts, n9:2 * n9], res[:, l, ts, 0:n9]))
                v.tensor_tensor(WP[:, l, ts, 2 * n9:3 * n9], res[:, l, ts, 0:n9], WP[:, l, ts, n9:2 * n9],
                                ALU.subtract).then_inc(s["w_ready"], 1)

            def modulate(k, p):
                l, m = ((0, 3), (1, 0), (1, 3))[k - 1]
                n = NP * k + p
                dve.wait_ge(s["xt_ps"], n + 1)
                for h in range(2):
                    b = 2 * p + h
                    last = v.tensor_scalar(XT[k][:, b * S:(b + 1) * S], P[:, bank_xt[n], h * S:(h + 1) * S],
                                           mcol[:, l, m + 1, b:b + 1], mcol[:, l, m, b:b + 1], ALU.mult, ALU.add)
                last.then_inc(s["xt_sb"], 1)

            dve.wait_ge(s["ld_b"], 16 * N_LD["ld_b"])
            v.tensor_copy(sel0[:, :], sel0f[:, :])
            v.tensor_copy(sel1[:, :], sel1f[:, :]).then_inc(s["sel_done"], 1)
            for p in range(NP):
                ln_stats(1, p)
            for p in range(NP):
                ln_apply(1, p).then_inc(s["xn_ready"], 1)
            for p in range(NP):
                modulate(1, p)
            for p in range(NP):
                router(0, p)

            def gate_experts(l, p):
                n = NP * l + p
                dve.wait_ge(s["y_ps"], n + 1)
                if n >= 2:
                    dve.wait_ge(s["z_ps"], n - 1)
                for h in range(2):
                    b = 2 * p + h
                    last = v.tensor_scalar(yT[:, n % 2, h * S:(h + 1) * S], P[:, bank_y[n], h * S:(h + 1) * S],
                                           mcol[:, l, 5, b:b + 1], None, ALU.mult)
                last.then_inc(s["y_sb"], 1)

            def add_experts(l, p):
                n = NP * l + p
                dve.wait_ge(s["z_ps"], n + 1)
                v.tensor_tensor(X[:, TPP * p:TPP * p + TPP, :], X[:, TPP * p:TPP * p + TPP, :],
                                P[:, bank_z[n], :].rearrange("p (t d) -> p t d", d=D), ALU.add
                                ).then_inc(s["z_read"], 1)
                dve.wait_ge(s["z_read"], n + 1)

            def kv(p):
                for t in tiles(p):
                    dve.wait_ge(s["kv_ps"], t // 2 + 1)
                    if t >= KVR:
                        dve.wait_ge(kv_out[t % KVR], 16 * (t // KVR))
                    ps = P[:, bank_kv[t // 2], (t % 2) * 2 * D:(t % 2) * 2 * D + 2 * D]
                    v.tensor_tensor(kvf[:, t % 2, 0, :], ps[:, 0:D], b1v[:, :], ALU.add)
                    link(v.scalar_tensor_tensor(out=kvf[:, t % 2, 1, :], in0=ps[:, D:2 * D],
                                                scalar=temp[:, t % 2:t % 2 + 1], in1=b1kt[:, t % 2, :],
                                                op0=ALU.mult, op1=ALU.add))
                    link(v.tensor_copy(kvs[:, t % KVR, 0:4:2, :], kvf[:, t % 2, :, :]))
                    v.tensor_tensor(kvs[:, t % KVR, 1:4:2, :], kvf[:, t % 2, :, :],
                                    kvs[:, t % KVR, 0:4:2, :].bitcast(fp32), ALU.subtract
                                    ).then_inc(s["kvs_ready"], 1)
                    dve.wait_ge(s["kvs_ready"], t + 1)

            for p in range(NP):
                for e in range(E):
                    for c in range(C0):
                        n = (p * E + e) * C0 + c
                        u = (p * (E + 1) + e) * C0 + c
                        dve.wait_ge(s["bc_ps"], p * E + e + 1)
                        dve.wait_ge(s["act_ready"], u + 1)
                        if n >= 3:
                            dve.wait_ge(s["hid_used"], n - 2)
                        v.tensor_tensor(hid[:, n % 3, :], act_out[:, u % 3, :], P[:, bank_bc(p * E + e), :],
                                        ALU.mult).then_inc(s["hid_ready"], 1)
                    if p >= 1 and e == 1:
                        gate_experts(0, p - 1)
                    if p >= 1 and e == 3:
                        add_experts(0, p - 1)
                        ln_stats(2, p - 1)
                    if p >= 1 and e == 4:
                        ln_apply(2, p - 1).then_inc(s["xn_ready"], 1)
                    if p >= 1 and e == 6:
                        modulate(2, p - 1)
            gate_experts(0, NP - 1)
            add_experts(0, NP - 1)
            ln_stats(2, NP - 1)
            ln_apply(2, NP - 1).then_inc(s["xn_ready"], 1)

            dve.wait_ge(s["ld_w1"], 16 * N_LD["ld_w1"])
            for i in range(2):
                last = v.tensor_scalar(b1kt[:, i, :], b1k[:, :], temp[:, i:i + 1], None, ALU.mult)
            link(last)
            kv(0)
            modulate(2, NP - 1)
            for p in range(1, NP):
                kv(p)

            def maxima(g):
                for h in range(HPG // 2):
                    dve.wait_ge(s["s1_ps"], HPG * g + 2 * h + 2)
                    v.tensor_reduce(nm1[:, g, 2 * h:2 * h + 2, :],
                                    P[:, 2 * h:2 * h + 2, :].rearrange("p j (h s) -> p (j h) s", h=2),
                                    AX.X, ALU.max, negate=True).then_inc(s["nm1_ready"], 1)

            def queries(g):
                dve.wait_ge(s["e1_ready"], HPG * (g + 1))
                dve.wait_ge(s["q1_sb"], g // GPP + 1)
                if g >= 2:
                    dve.wait_ge(s["c1_ps"], g - 1)
                link(v.reciprocal(rz1[:, g, :, :], Z1[:, g, :, :]))
                for h in range(2):
                    last = v.tensor_tensor(
                        qs[:, g % 2, :, h, :], qT1(g)[:, :, :, h],
                        rz1[:, g, :, h].unsqueeze(2).broadcast_to([128, HPG, DH]), ALU.mult)
                link(last)
                v.tensor_copy(qs4[:, g % 2, :, :, :, :].rearrange("p j h r d -> p (j h) r d"),
                              qs[:, g % 2, :, :, :].rearrange("p j h d -> p (j h) d").unsqueeze(2).broadcast_to([128, 2 * HPG, HPG, DH])
                              ).then_inc(s["qs_ready"], 1)

            def outputs(g):
                b = g // GPB
                dve.wait_ge(s["c1_ps"], g + 1)
                if b >= 2 and g % GPB == 0:
                    dve.wait_ge(ao_out[b - 2], 16 * HPG)
                v.tensor_copy(O[:, b % 2, g % GPB, :], P[:, 4 + g % 2, 0:S]).then_inc(s["o1_ready"], 1)

            def attention_residual(b):
                ts = slice(TPB * b, TPB * b + TPB)
                dve.wait_ge(ao_in[b], 16)
                link(v.tensor_tensor(AO[:, ts, :], AO[:, ts, :],
                                     mrow1[:, b, :].unsqueeze(1).broadcast_to([128, TPB, D]), ALU.mult))
                link(v.tensor_tensor(X[:, ts, :], X[:, ts, :], AO[:, ts, :], ALU.add))

            def qT1(g):
                return qT[:, GT * g:GT * g + GT].rearrange("p (j d h) -> p j d h", j=HPG, d=DH)

            maxima(0)
            for g in range(NG):
                if g + 1 < NG:
                    maxima(g + 1)
                queries(g)
                if g >= 1:
                    outputs(g - 1)
                if g % GPP == GPP - 1 and g > GPP:
                    for b in (2 * (g // GPP) - 2, 2 * (g // GPP) - 1):
                        attention_residual(b)
                    ln_stats(3, g // GPP - 1)
            outputs(NG - 1)
            for p in range(NP - 1):
                ln_apply(3, p).then_inc(s["xn_ready"], 1)
            for p in range(NP - 1):
                modulate(3, p)
            for p in range(NP - 1):
                router(1, p)

            NC = len(CH1)
            for p in range(NP):
                for c, (_, m) in enumerate(CH1):
                    n = p * NC + c
                    dve.wait_ge(s["u_ps"], n + 1)
                    dve.wait_ge(s["gact_ready"], n + 1)
                    link(v.tensor_tensor(gu[0:m, n % 2, :], act_out[0:m, n % 3, :], P[0:m, bank_u(n), :], ALU.mult))
                    v.tensor_copy(sq[0:1, 0:1], gu[0:1, n % 2, 0:1]).then_inc(s["u_read"], 1)
                    dve.wait_ge(s["bc_ps"], NP * E + n + 1)
                    if n >= 3:
                        dve.wait_ge(s["hid_used"], NP * E * C0 + n - 2)
                    v.tensor_tensor(hid[0:m, n % 3, :], gu[0:m, n % 2, :], P[0:m, bank_b1(n), :],
                                    ALU.mult).then_inc(s["hid_ready"], 1)
                    if p == 0 and c == 2:
                        for b in (B - 2, B - 1):
                            attention_residual(b)
                        ln_stats(3, NP - 1)
                        ln_apply(3, NP - 1).then_inc(s["xn_ready"], 1)
                    if p == 0 and c == 5:
                        modulate(3, NP - 1)
                    if p == 0 and c == 8:
                        router(1, NP - 1)
                    if p >= 1 and c == 3:
                        gate_experts(1, p - 1)
                    if p >= 1 and c == 7:
                        add_experts(1, p - 1)
            gate_experts(1, NP - 1)
            add_experts(1, NP - 1)

        @block.scalar
        def _(act):
            sc = nc.scalar
            act.wait_ge(s["ld_c"], 16 * N_LD["ld_c"])
            sc.activation(scT[:, :, :], cT[:, :, :], ACT.Silu).then_inc(s["silu_done"], 1)
            act.wait_ge(s["silu_done"], 1)
            sc.activation(identb[:, :], ident[:, :], ACT.Copy).then_inc(s["silu_done"], 1)
            for p in range(NP):
                act.wait_ge(s["xt_ps"], p + 1)
                sc.activation(XT[0][:, cols(p)], P[:, bank_xt[p], :], ACT.Copy).then_inc(s["xt_sb"], 1)
            act.wait_ge(s["ld_w0"], 16 * N_LD["ld_w0"])
            for p in range(NP):
                act.wait_ge(s["q0_ps"], p + 1)
                sc.activation(qT[:, cols(p)], P[:, bank_q0[p], :], ACT.Identity, bias=b0q[:, :]).then_inc(s["q0_sb"], 1)
            for b in range(B):
                act.wait_ge(s["nm0_ready"], b + 1)
                for i in range(TPB):
                    t = TPB * b + i
                    sc.activation(PR[:, t, :], P[:, bank_s0[b], i * S:(i + 1) * S], ACT.Exp,
                                  bias=nms0[:, t:t + 1], scale=D ** -0.5,
                                  accum_out=Z0[:, t:t + 1]).then_inc(s["p0_ready"], 1)
            for b in range(B):
                act.wait_ge(s["pt_ps"], b + 1)
                sc.activation(PRT[:, b, :, :], P[:, bank_pt[b], :].rearrange("p (j q) -> p j q", j=TPB),
                              ACT.Copy).then_inc(s["pt_sb"], 1)

            def router_exp(l, p):
                n = NP * l + p
                act.wait_ge(s["rd_ready"], n + 1)
                ts = slice(TPP * p, TPP * p + TPP)
                sc.activation(ex[:, l, ts, 0:E + l], ld[:, l, ts, 0:E + l], ACT.Exp).then_inc(s["rex_ready"], 1)

            def weights_transposed(l, p):
                n = NP * l + p
                act.wait_ge(s["wt_ps"], n + 1)
                r = 3 * (E + l)
                last = sc.activation(WPT[l][:, cols(p)], P[0:r, bank_wt[n], 0:PT // 2].bitcast(bf16), ACT.Copy)
                if l == 0:
                    last = sc.activation(WT[:, cols(p)], P[0:E + 1, bank_wt2[p], :], ACT.Copy)
                last.then_inc(s["wt_sb"], 1)

            for p in range(NP):
                router_exp(0, p)
            for p in range(NP):
                weights_transposed(0, p)
            act.wait_ge(s["ld_f0"], 16 * N_LD["ld_f0"])
            for p in range(NP):
                for e in range(E + 1):
                    for c in range(C0):
                        u = (p * (E + 1) + e) * C0 + c
                        act.wait_ge(s["up_ps"], u + 1)
                        if u >= 3:
                            pp, ee = (u - 3) // ((E + 1) * C0), (u - 3) // C0 % (E + 1)
                            if ee < E:
                                act.wait_ge(s["hid_ready"], pp * E * C0 + (u - 3) % ((E + 1) * C0) + 1)
                            else:
                                act.wait_ge(s["y_ps"], pp + 1)
                        sc.activation(act_out[:, u % 3, :], P[:, bank_up(u), :], ACT.Gelu,
                                      bias=ub0[:, e, c:c + 1]).then_inc(s["act_ready"], 1)
            act.wait_ge(s["ld_w1"], 16 * N_LD["ld_w1"])
            for p in range(NP):
                act.wait_ge(s["q1_ps"], p + 1)
                sc.activation(qT[:, cols(p)], P[:, bank_q1[p], :], ACT.Identity, bias=b1q[:, :]).then_inc(s["q1_sb"], 1)
            for g in range(NG):
                for j in range(HPG):
                    act.wait_ge(s["nm1_ready"], 2 * g + j // 2 + 1)
                    if g >= 2 and j == 0:
                        act.wait_ge(s["c1_ps"], g - 1)
                    for h in range(2):
                        last = sc.activation(EX[:, g % 2, j, h * S:(h + 1) * S], P[:, j, h * S:(h + 1) * S],
                                             ACT.Exp, bias=nm1[:, g, j, h:h + 1], accum_out=Z1[:, g, j, h:h + 1])
                    last.then_inc(s["e1_ready"], 1)
            for p in range(NP - 1):
                router_exp(1, p)
            for p in range(NP - 1):
                weights_transposed(1, p)
            NC = len(CH1)
            for p in range(NP):
                for c, (_, m) in enumerate(CH1):
                    n = p * NC + c
                    act.wait_ge(s["g_ps"], n + 1)
                    if n >= 3:
                        act.wait_ge(s["u_read"], n - 2)
                    if n < 3:
                        act.wait_ge(s["y_ps"], NP)
                        act.wait_ge(s["hid_ready"], NP * E * C0)
                    sc.activation(act_out[0:m, n % 3, :], P[0:m, bank_g(n), :], ACT.Silu).then_inc(s["gact_ready"], 1)
                    if p == 0 and c == 8:
                        router_exp(1, NP - 1)
                    if p == 0 and c == 10:
                        weights_transposed(1, NP - 1)

        @block.tensor
        def _(pe):
            mm = nc.tensor.matmul
            reader = {}

            def claim(bank, who, value):
                if bank in reader:
                    pe.wait_ge(*reader[bank])
                reader[bank] = (s[who], value)
                return P[:, bank, :]

            pe.wait_ge(s["scb_done"], 1)
            for b in range(B):
                claim(b, "mod_sb", b + 1)
                mm(P[:, b, 0:3 * D], scB[:, 0, b, :], wmod[:, 0, 0:3 * D], start=True, stop=True).then_inc(s["mod_ps"], 1)
            for h in range(2):
                claim(h, "mod_sb", B + h + 1)
                for i in range(4):
                    last = mm(P[:, h, i * D:(i + 1) * D], scB[:, 1, 4 * h + i, :], wmod[:, 1, 2 * D:3 * D],
                              start=True, stop=True)
                last.then_inc(s["mod_ps"], 1)
            claim(2, "mod_sb", B + 3)
            for l in range(2):
                for m in range(6):
                    last = mm(P[:, 2, (l * 6 + m) * B:(l * 6 + m + 1) * B], wmod[:, l, m * D:(m + 1) * D],
                              scT[:, l, :], start=True, stop=True)
            last.then_inc(s["mod_ps"], 1)

            def transpose_tokens(k, p):
                n = NP * k + p
                pe.wait_ge(s["xn_ready"], n + 1)
                claim(bank_xt[n], "xt_sb", n + 1)
                for i, t in enumerate(tiles(p)):
                    last = nc.tensor.transpose(P[:, bank_xt[n], i * D:(i + 1) * D], SC[:, t, :], ident[:, :])
                last.then_inc(s["xt_ps"], 1)

            for p in range(NP):
                transpose_tokens(0, p)
            pe.wait_ge(s["ld_w0"], 16 * N_LD["ld_w0"])
            for p in range(NP):
                pe.wait_ge(s["xt_sb"], p + 1)
                claim(bank_q0[p], "q0_sb", p + 1)
                mm(P[:, bank_q0[p], :], w0q[:, :], XT[0][:, cols(p)], start=True, stop=True).then_inc(s["q0_ps"], 1)
                claim(bank_v0[p], "v0_sb", p + 1)
                for i, t in enumerate(tiles(p)):
                    last = mm(P[:, bank_v0[p], i * D:(i + 1) * D], XT[0][:, t * D:(t + 1) * D], w0v[:, :],
                              start=True, stop=True)
                last.then_inc(s["v0_ps"], 1)
            for p in range(NP):
                pe.wait_ge(s["q0_sb"], p + 1)
                claim(bank_tq[p], "tq_sb", p + 1)
                mm(P[:, bank_tq[p], :], w0a[:, :], qT[:, cols(p)], start=True, stop=True).then_inc(s["tq_ps"], 1)
            for b in range(B):
                pe.wait_ge(s["tq_sb"], b // 2 + 1)
                claim(bank_s0[b], "p0_ready", TPB * (b + 1))
                for i in range(TPB):
                    t = TPB * b + i
                    last = mm(P[:, bank_s0[b], i * S:(i + 1) * S], qT[:, t * D:(t + 1) * D],
                              tqT[:, b * S:(b + 1) * S], start=True, stop=True)
                last.then_inc(s["s0_ps"], 1)
            for b in range(B):
                pe.wait_ge(s["p0_ready"], TPB * (b + 1))
                claim(bank_pt[b], "pt_sb", b + 1)
                for j in range(TPB):
                    for i in range(TPB):
                        last = nc.tensor.transpose(P[:, bank_pt[b], j * S + i * D:j * S + (i + 1) * D],
                                                   PR[:, TPB * b + i, j * D:(j + 1) * D], ident[:, :])
                last.then_inc(s["pt_ps"], 1)
            for b in range(B):
                pe.wait_ge(s["pt_sb"], b + 1)
                pe.wait_ge(s["v0_sb"], b // 2 + 1)
                claim(bank_c0[b], "c0_read", b + 1)
                for i in range(TPB):
                    for j in range(TPB):
                        last = mm(P[:, bank_c0[b], i * D:(i + 1) * D], PRT[:, b, j, i * D:(i + 1) * D],
                                  V[:, TPB * b + j, :], start=(j == 0), stop=(j == TPB - 1))
                last.then_inc(s["c0_ps"], 1)

            def route(l, p):
                n, n9 = NP * l + p, E + l
                k = 1 if l == 0 else 3
                pe.wait_ge(s["xt_sb"], NP * k + p + 1)
                claim(bank_r[n], "rd_ready", n + 1)
                for i, t in enumerate(tiles(p)):
                    last = mm(P[:, bank_r[n], i * n9:(i + 1) * n9], XT[k][:, t * D:(t + 1) * D],
                              (rw0, rw1)[l][:, :], start=True, stop=True)
                last.then_inc(s["r_ps"], 1)

            def weights_transposed(l, p):
                n, n9 = NP * l + p, E + l
                pe.wait_ge(s["w_ready"], n + 1)
                claim(bank_wt[n], "wt_sb", n + 1)
                for i, t in enumerate(tiles(p)):
                    last = nc.tensor.transpose(P[0:3 * n9, bank_wt[n], 0:PT // 2].bitcast(bf16)[:, i * D:(i + 1) * D],
                                               WP[:, l, t, 0:3 * n9], identb[:, :])
                if l == 0:
                    claim(bank_wt2[p], "wt_sb", n + 1)
                    for i, t in enumerate(tiles(p)):
                        last = nc.tensor.transpose(P[0:E + 1, bank_wt2[p], i * D:(i + 1) * D], W[:, 0, t, :], ident[:, :])
                last.then_inc(s["wt_ps"], 1)

            for p in range(NP):
                transpose_tokens(1, p)
            for p in range(NP):
                route(0, p)
            pe.wait_ge(s["silu_done"], 2)
            for p in range(NP):
                weights_transposed(0, p)

            def tokens_back(l, p):
                n = NP * l + p
                pe.wait_ge(s["y_sb"], n + 1)
                claim(bank_z[n], "z_read", n + 1)
                for i in range(TPP):
                    last = nc.tensor.transpose(P[:, bank_z[n], i * D:(i + 1) * D], yT[:, n % 2, i * D:(i + 1) * D],
                                               ident[:, :])
                last.then_inc(s["z_ps"], 1)

            pe.wait_ge(s["ld_f0"], 16 * N_LD["ld_f0"])
            pe.wait_ge(s["sel_done"], 1)
            LAG = 2

            def down0(u):
                p, e, c = u // ((E + 1) * C0), u // C0 % (E + 1), u % C0
                if e == 0 and c == 0:
                    pe.wait_ge(s["wt_sb"], p + 1)
                    claim(bank_y[p], "y_sb", p + 1)
                    mm(P[:, bank_y[p], :], db0[:, :], WT[:, cols(p)], start=True, stop=False)
                if e < E:
                    n = (p * E + e) * C0 + c
                    pe.wait_ge(s["hid_ready"], n + 1)
                    mm(P[:, bank_y[p], :], dn0[:, e, c, :], hid[:, n % 3, :], start=False, stop=False
                       ).then_inc(s["hid_used"], 1)
                else:
                    pe.wait_ge(s["act_ready"], u + 1)
                    last = mm(P[:, bank_y[p], :], dn0[:, e, c, :], act_out[:, u % 3, :], start=False,
                              stop=(c == C0 - 1))
                    if c == C0 - 1:
                        last.then_inc(s["y_ps"], 1)

            for p in range(NP):
                for e in range(E + 1):
                    for c in range(C0):
                        u = (p * (E + 1) + e) * C0 + c
                        claim(bank_up(u), "act_ready", u + 1)
                        mm(P[:, bank_up(u), :], up0[:, e, c * D:(c + 1) * D], XT[1][:, cols(p)],
                           start=True, stop=True).then_inc(s["up_ps"], 1)
                        if c == 0 and e < E:
                            m = p * E + e
                            claim(bank_bc(m), "hid_ready", (m + 1) * C0)
                            mm(P[:, bank_bc(m), :], sel0[:, e * D:(e + 1) * D], WPT[0][:, cols(p)],
                               start=True, stop=True).then_inc(s["bc_ps"], 1)
                        if u >= LAG:
                            down0(u - LAG)
                        if p >= 1 and (e, c) == (2, 1):
                            tokens_back(0, p - 1)
                        if p >= 1 and (e, c) == (6, 0):
                            transpose_tokens(2, p - 1)
            for u in range(NP * (E + 1) * C0 - LAG, NP * (E + 1) * C0):
                down0(u)
            tokens_back(0, NP - 1)

            pe.wait_ge(s["ld_w1"], 16 * N_LD["ld_w1"])

            def project1(p):
                pe.wait_ge(s["xt_sb"], NP * 2 + p + 1)
                claim(bank_q1[p], "q1_sb", p + 1)
                mm(P[:, bank_q1[p], :], w1q[:, :], XT[2][:, cols(p)], start=True, stop=True).then_inc(s["q1_ps"], 1)
                for h in range(2):
                    n = 2 * p + h
                    claim(bank_kv[n], "kvs_ready", 2 * n + 2)
                    for i in range(2):
                        t = 2 * n + i
                        last = mm(P[:, bank_kv[n], i * 2 * D:(i + 1) * 2 * D], XT[2][:, t * D:(t + 1) * D],
                                  w1vk[:, :], start=True, stop=True)
                    last.then_inc(s["kv_ps"], 1)

            project1(0)
            transpose_tokens(2, NP - 1)
            for p in range(1, NP):
                project1(p)

            def scores(g):
                p = g // GPP
                if g % GPP == 0:
                    pe.wait_ge(kv_in[p], 16 * 6 * HPG)
                for j in range(HPG):
                    claim(j, "e1_ready", HPG * g + j + 1)
                    for h in range(2):
                        last = mm(P[:, j, h * S:(h + 1) * S],
                                  KS[32 * j:32 * j + 3 * DH, p % 2, g % GPP, h * D:(h + 1) * D],
                                  VS[32 * j:32 * j + 3 * DH, p % 2, g % GPP, :], start=True, stop=True)
                    last.then_inc(s["s1_ps"], 1)

            def context(g):
                claim(4 + g % 2, "o1_ready", g + 1)
                pe.wait_ge(s["qs_ready"], g + 1)
                for h in range(2):
                    for j in range(HPG):
                        last = mm(P[32 * j:32 * j + 32, 4 + g % 2, 0:S],
                                  qs4[:, g % 2, j, h, :, :].rearrange("p r d -> p (r d)"),
                                  EX[:, g % 2, j, h * S:(h + 1) * S], start=(h == 0), stop=(h == 1))
                last.then_inc(s["c1_ps"], 1)

            scores(0)
            for g in range(NG):
                if g + 1 < NG:
                    scores(g + 1)
                context(g)
            pe.wait_ge(s["ld_f1"], 16 * N_LD["ld_f1"])
            for p in range(NP - 1):
                transpose_tokens(3, p)
            for p in range(NP - 1):
                route(1, p)
            for p in range(NP - 1):
                weights_transposed(1, p)

            NC = len(CH1)
            base = NP * E * C0

            def down1(n):
                p, c = n // NC, n % NC
                m = CH1[c][1]
                pe.wait_ge(s["hid_ready"], base + n + 1)
                if c == 0:
                    claim(bank_y[NP + p], "y_sb", NP + p + 1)
                last = mm(P[:, bank_y[NP + p], :], dn1[0:m, c, :], hid[0:m, n % 3, :],
                          start=(c == 0), stop=(c == NC - 1))
                last.then_inc(s["hid_used"], 1)
                if c == NC - 1:
                    pe.wait_ge(s["hid_used"], base + n + 1)
                    pe.sem_inc(s["y_ps"], 1)

            for p in range(NP):
                for c, (c0, m) in enumerate(CH1):
                    n = p * NC + c
                    if p == 0 and c == 0:
                        pass
                    claim(bank_g(n), "gact_ready", n + 1)
                    mm(P[0:m, bank_g(n), :], gate1[:, c0:c0 + m], XT[3][:, cols(p)], start=True, stop=True
                       ).then_inc(s["g_ps"], 1)
                    claim(bank_u(n), "u_read", n + 1)
                    mm(P[0:m, bank_u(n), :], up1[:, c0:c0 + m], XT[3][:, cols(p)], start=True, stop=True
                       ).then_inc(s["u_ps"], 1)
                    claim(bank_b1(n), "hid_ready", base + n + 1)
                    mm(P[0:m, bank_b1(n), :], sel1[:, c0:c0 + m], WPT[1][:, cols(p)], start=True, stop=True
                       ).then_inc(s["bc_ps"], 1)
                    if n >= LAG:
                        down1(n - LAG)
                    if p == 0 and c == 5:
                        transpose_tokens(3, NP - 1)
                    if p == 0 and c == 7:
                        route(1, NP - 1)
                    if p == 0 and c == 10:
                        weights_transposed(1, NP - 1)
                    if p >= 1 and c == 6:
                        tokens_back(1, p - 1)
            for n in range(NP * NC - LAG, NP * NC):
                down1(n)
            tokens_back(1, NP - 1)


bank_xt = [3, 4, 5, 6] + [0, 1, 2, 3] + [7, 7, 7, 7] + [0, 1, 2, 7]
bank_q0 = [7, 0, 1, 2]
bank_v0 = [3, 4, 5, 6]
bank_tq = [7, 0, 1, 2]
bank_s0 = [3, 4, 5, 6, 7, 0, 1, 2]
bank_pt = [3, 4, 5, 6, 7, 0, 1, 2]
bank_c0 = [3, 4, 5, 6, 7, 0, 1, 2]
bank_r = [4, 5, 6, 7] + [3, 4, 5, 7]
bank_wt = [0, 1, 2, 3] + [6, 0, 1, 7]
bank_wt2 = [4, 5, 6, 7]
bank_y = [5, 6, 5, 6] + [5, 6, 5, 6]
bank_z = [7] * 8
bank_q1 = [0, 1, 2, 3]
bank_kv = [4, 5, 6, 7, 0, 1, 2, 3]


def bank_up(u):
    return u % 3


def bank_bc(m):
    return 3 + m % 2


def bank_g(n):
    return n % 2


def bank_u(n):
    return 2


def bank_b1(n):
    return 3 + n % 2


_NAMED = ["L0_wmod", "L1_wmod", "L0_attn_anomaly_matrix", "L0_attn_bq", "L0_attn_bv",
          "L0_ffn_router_w", "L0_ffn_router_b", "L0_ffn_sw1", "L0_ffn_sw2", "L0_ffn_sb2",
          "L0_ffn_rw1", "L0_ffn_rw2", "L0_ffn_rb2", "L1_attn_Wq", "L1_attn_Wk", "L1_attn_Wv",
          "L1_attn_bq", "L1_attn_bk", "L1_attn_bv", "L1_ffn_w_gate", "L1_ffn_w_up",
          "L1_ffn_w_down", "L1_ffn_sw_gate", "L1_ffn_sw_up", "L1_ffn_sw_down"]


def kernel(**inputs):
    import numpy as np
    import concourse.bacc as bacc
    from concourse.bass_utils import run_bass_kernel_spmd as run

    arrays = {n: np.ascontiguousarray(inputs[n]) for n in _NAMED}

    def put(name, array):
        arrays[name] = np.ascontiguousarray(array)

    put("x", np.asarray(inputs["L0_attn_hidden_states"]).reshape(TOK, D))
    put("c0T", np.asarray(inputs["L0_c"]).T)
    put("c1T", np.asarray(inputs["L1_c"]).T)
    put("WqT0", np.asarray(inputs["L0_attn_Wq"]).T)
    put("WvT0", np.asarray(inputs["L0_attn_Wv"]).T)
    ub = np.concatenate([np.asarray(inputs["L0_ffn_rb1"]), np.asarray(inputs["L0_ffn_sb1"])[None]])
    put("ub0T", ub.reshape((E + 1) * C0, D).T)
    put("tempT", np.repeat(np.asarray(inputs["L1_attn_temperature"]).reshape(2, HEADS // 2), 2 * DH, axis=1).T)
    put("gate_wT", np.asarray(inputs["L1_ffn_gate_w"]).T)
    put("shared_gateT", np.asarray(inputs["L1_ffn_shared_gate_w"]).T)
    put("ident", np.eye(128, dtype=np.float32))
    put("iota", np.arange(E, dtype=np.float32))
    put("sel0", np.tile(np.repeat(np.eye(E, dtype=np.float32), D, axis=1), (3, 1)))
    put("sel1", np.tile(np.repeat(np.eye(E + 1, dtype=np.float32), H1, axis=1), (3, 1)))

    nc = bacc.Bacc("TRN2", target_bir_lowering=False, num_devices=1)
    aps = {n: nc.dram_tensor(f"in_{n}", v.shape, mybir.dt.float32, kind="ExternalInput").ap()
           for n, v in arrays.items()}
    out = nc.dram_tensor("out", (TOK, D), mybir.dt.float32, kind="ExternalOutput").ap()
    scratch = {"kv": nc.dram_tensor("kv_parts", (4, TOK, D), mybir.dt.float32, kind="Internal").ap(),
               "ao": nc.dram_tensor("attention_rows", (TOK, D), mybir.dt.float32, kind="Internal").ap()}
    two_block_adaln(nc, aps, out, scratch)
    r = run(nc, [{f"in_{n}": v for n, v in arrays.items()}], core_ids=[0])
    return r.results[0]["out"].reshape(B, S, D)
```

```python
from contextlib import ExitStack

import concourse.bass as bass
from concourse import mybir

D = 128
B, S = 8, 256
TOK = B * S
NT = TOK // D
TPB = S // D
NP = B // 2
TPP = NT // NP
PT = TOK // NP
E = 8
H0 = 256
C0 = H0 // D
H1 = 176
F1 = (E + 1) * H1
C1 = -(-F1 // D)
FP = C1 * D
HEADS, DH = 16, 8
HPG = 4
NG = B * HEADS // HPG
GPB = HEADS // HPG
GPP = NG // NP
GT = HPG * DH * 2
KVR = 4
LAG = 3
STEPS0 = (E + 1) * C0
EPS = 1e-5


def two_block_adaln(nc, a, out, scratch):
    fp32, fp32r = mybir.dt.float32, mybir.dt.float32r
    bf16, u32 = mybir.dt.bfloat16, mybir.dt.uint32
    ACT, ALU, AX = mybir.ActivationFunctionType, mybir.AluOpType, mybir.AxisListType

    with ExitStack() as ctx:
        def sb(name, shape, dt=fp32):
            return ctx.enter_context(nc.sbuf_tensor(name, shape, dt))

        def sem(name):
            return ctx.enter_context(nc.semaphore(name))

        X = sb("X", [128, NT, D])
        SC = sb("SC", [128, NT, D])
        AO = SC
        XT = sb("XT", [128, TOK])
        XH = sb("XH", [128, 2, PT], fp32r)
        XL = sb("XL", [128, 2, PT], fp32r)
        qT = sb("qT", [128, TOK])
        with ExitStack() as first:
            stage0 = first.enter_context(nc.sbuf_tensor("stage0", [128, 2 * STEPS0 * D], fp32))
        with ExitStack() as early:
            def sb_early(name, shape, dt=fp32):
                return early.enter_context(nc.sbuf_tensor(name, shape, dt))

            PR = sb_early("PR", [128, NT, S])
            PRT = sb_early("PRT", [128, B, TPB, S])
            tqT = sb_early("tqT", [128, TOK])
            V = sb_early("V", [128, NT, D])
            w0q = sb_early("w0q", [128, D]); w0v = sb_early("w0v", [128, D]); w0a = sb_early("w0a", [128, D])
            b0v = sb_early("b0v", [128, D])
            mrow0 = sb_early("mrow0", [128, B, D])
        EX = sb("EX", [128, 3, HPG, 2 * S])
        VS = sb("VS", [128, 2, GPP, S], fp32r)
        KS = sb("KS", [128, 2, GPP, S], fp32r)
        selstage = PRT[:, 2:B, :, :].rearrange("p b j q -> p (b j q)")[:, 0:E * D + FP]
        HH = tqT
        ident = sb("ident", [128, 128])
        identb = sb("identb", [128, 128], bf16)
        ones = sb("ones", [128, 128])
        iota = sb("iota", [128, E])
        yT = sb("yT", [128, 2, PT])
        O = sb("O", [128, 2, GPB, S])

        tmp = sb("tmp", [128, 4, PT])
        gu = tmp[:, 0:2, :]
        hidf = tmp[:, 2:4, :]
        hidh = sb("hidh", [128, 3, PT], fp32r)
        hidl = sb("hidl", [128, 3, PT], fp32r)
        stage1 = tmp[:, :, :].rearrange("p r n -> p (r n)")[:, 0:FP]

        b0q = sb("b0q", [128, 1])
        rw0 = sb("rw0", [128, E]); rb0 = sb("rb0", [128, E])
        ub0 = sb("ub0", [128, E + 1, C0]); sb2 = sb("sb2", [128, 1])
        db0 = tmp[0:3 * E, 2, 0:D]; dbr = tmp[0:3 * E, 2, D:2 * D]
        dbp = sb("dbp", [3 * E, 3, D], bf16)
        w1q = sb("w1q", [128, D]); w1vk = sb("w1vk", [128, 2 * D]); b1q = sb("b1q", [128, 1])
        b1v = sb("b1v", [128, D]); b1kt = sb("b1kt", [128, 2, D])
        temp = sb("temp", [128, 2])
        rw1 = sb("rw1", [128, E + 1])
        WH = sb("WH", [128, 3 * FP], fp32r)
        WL = sb("WL", [128, 3 * FP], fp32r)
        wmod = sb("wmod", [128, 2, 6 * D])
        act_out = wmod[:, :, :].rearrange("p l n -> p (l n)").rearrange("p (r n) -> p r n", r=3)
        cT = sb("cT", [128, 2, B]); scT = sb("scT", [128, 2, B])
        scB = O[:, :, :, :].rearrange("p r g n -> p (r g n)").rearrange("p (l b d) -> p l b d", l=2, b=B)
        sel0f = selstage[0:3 * E, 0:E * D]; sel0 = sb("sel0", [3 * E, E * D], bf16)
        sel1f = selstage[0:3 * (E + 1), E * D:]; sel1 = sb("sel1", [3 * (E + 1), FP], bf16)
        mrow1 = sb("mrow1", [128, B, D])
        mcol = sb("mcol", [128, 2, 6, B])
        gtmp = tqT[:, :].rearrange("p (l b d) -> p l b d", l=2, b=B)
        gtmc = sb("gtmc", [128, 2, B])

        st = sb("st", [128, NT, 6]); mv = sb("mv", [128, 4, NT, 2])
        ve = sb("ve", [128, 4, NT]); rstd = sb("rstd", [128, 4, NT])
        mhalf = sb("mhalf", [128, NT]); phalf = sb("phalf", [128, NT])
        dg = tmp[:, 0, :].rearrange("p (t d) -> p t d", d=D); ss = sb("ss", [128, NT]); nrm = sb("nrm", [128, NT])
        rn = sb("rn", [128, NT])
        nm0 = sb("nm0", [128, NT]); nms0 = sb("nms0", [128, NT]); Z0 = sb("Z0", [128, NT])
        nz = sb("nz", [128, NT])
        ctmp = tmp[:, 1, 0:TPB * D].rearrange("p (t d) -> p t d", d=D)
        RP = 2 * TPP
        lg = sb("lg", [128, RP, E + 1]); ld = sb("ld", [128, RP, E + 1]); ex = sb("ex", [128, RP, E + 1])
        nmr = sb("nmr", [128, RP]); top = sb("top", [128, RP, 8]); tix = sb("tix", [128, RP, 8], u32)
        tif = sb("tif", [128, RP, 2]); tden = sb("tden", [128, RP]); trc = sb("trc", [128, RP])
        tw = sb("tw", [128, RP, 2]); oh = sb("oh", [128, RP, 2, E])
        W = sb("W", [128, RP, E + 1]); res = sb("res", [128, RP, E + 1])
        WP = sb("WP", [128, RP, 3 * (E + 1)], bf16)
        WPT = sb("WPT", [3 * (E + 1), 2, PT], bf16)

        kvf = sb("kvf", [128, 2, 2, D])
        b1k = kvf[:, 0, 0, :]
        kvs = sb("kvs", [128, KVR, 4, D], fp32r)
        nm1 = sb("nm1", [128, 4, HPG, 2]); Z1 = sb("Z1", [128, 4, HPG, 2])
        rz1 = sb("rz1", [128, 4, HPG, 2])
        qs4 = sb("qs4", [128, 2, HPG, 2, HPG, DH])
        qs = tmp[:, 3, D:D + 2 * HPG * 2 * DH].rearrange("p (r j h d) -> p r j h d", r=2, j=HPG, h=2)

        P = ctx.enter_context(nc.psum_tensor("P", [128, 8, PT], fp32))

        names = ["ld_c", "ld_b", "ld_w0", "ld_f0", "ld_w1", "ld_r1", "silu_done", "identb_done",
                 "scb_done", "const_done", "mod_ps", "mod_sb", "mod_done", "ss_ps", "ss_ready",
                 "hh_ready", "nrm_ready", "dg_ready", "rn_ps",
                 "q0_ps", "q0_sb", "v0_ps", "v0_sb", "tq_ps", "tq_sb",
                 "s0_ps", "nm0_ready", "p0_ready", "pt_ps", "pt_sb", "c0_ps", "c0_read",
                 "w0_high", "w0_low", "zeroed", "stage_loaded", "w1_high", "w1_low",
                 "xh_ready", "xl_ready", "r_ps", "rd_ready", "rex_ready", "w_ready", "wt_ps", "wt_sb",
                 "up_ps", "act_ready", "bc_ps", "bc_read", "high_ready", "low_ready", "down_done",
                 "y_ps", "y_sb", "z_ps", "z_read", "g_ps", "u_ps", "gact_ready", "u_read",
                 "q1_ps", "q1_sb", "kv_ps",
                 "kvs_ready", "s1_ps", "nm1_ready", "e1_ready", "qs_ready", "c1_ps",
                 "o1_ready", "x_final", "v_step", "pool_const"]
        for k in range(4):
            names += [f"ve_ready{k}", f"rstd_ready{k}", f"xn_ready{k}", f"xt_ps{k}", f"xt_sb{k}"]
        s = {n: sem(n) for n in names}
        ld_x = [sem(f"ld_x{p}") for p in range(NP)]
        kv_out = [sem(f"kv_out{r}") for r in range(KVR)]
        kv_in = [sem(f"kv_in{p}") for p in range(NP)]
        ao_out = [sem(f"ao_out{b}") for b in range(B)]
        ao_in = [sem(f"ao_in{b}") for b in range(B)]
        stored = sem("stored")
        block = ctx.enter_context(nc.Block())

        def per_partition(v, n):
            return v.rearrange("(p n) -> p n", n=n)

        def tiles(p):
            return range(TPP * p, TPP * p + TPP)

        def half(p):
            return slice(TPP * (p % 2), TPP * (p % 2) + TPP)

        def cols(p):
            return slice(PT * p, PT * p + PT)

        N_LD = {"ld_c": 5, "ld_b": 9, "ld_w0": 7, "ld_f0": 4, "ld_w1": 6, "ld_r1": 2}

        @block.sync
        def _(sp):
            def load(dst, src, name):
                sp.dma_start(dst, src).then_inc(s[name], 16)

            load(cT[:, 0, :], a["c0T"], "ld_c")
            load(wmod[:, 0, :], a["L0_wmod"], "ld_c")
            for p in range(NP):
                sp.dma_start(X[:, TPP * p:TPP * p + TPP, :],
                             a["x"].rearrange("(t p) d -> p t d", p=128)[:, TPP * p:TPP * p + TPP, :]
                             ).then_inc(ld_x[p], 16)
                if p == 0:
                    load(cT[:, 1, :], a["c1T"], "ld_c")
                    load(ident[:, :], a["ident"], "ld_c")
                    load(wmod[:, 1, :], a["L1_wmod"], "ld_c")
            load(iota[:, :], a["iota"].partition_broadcast(128), "ld_b")
            load(sel0f[:, :], a["sel0"], "ld_b")
            load(sel1f[:, :], a["sel1"], "ld_b")
            load(rb0[:, :], a["L0_ffn_router_b"].partition_broadcast(128), "ld_b")
            load(ub0[:, :, :], a["ub0T"].rearrange("p (e c) -> p e c", c=C0), "ld_b")
            load(sb2[:, :], per_partition(a["L0_ffn_sb2"], 1), "ld_b")
            for n in range(3):
                load(db0[E * n:E * n + E, :], a["L0_ffn_rb2"], "ld_b")
            load(w0q[:, :], a["WqT0"], "ld_w0")
            load(w0v[:, :], a["WvT0"], "ld_w0")
            load(w0a[:, :], a["L0_attn_anomaly_matrix"], "ld_w0")
            load(b0q[:, :], per_partition(a["L0_attn_bq"], 1), "ld_w0")
            load(b0v[:, :], a["L0_attn_bv"].partition_broadcast(128), "ld_w0")
            load(rw0[:, :], a["L0_ffn_router_w"], "ld_w0")
            load(b1v[:, :], a["L1_attn_bv"].partition_broadcast(128), "ld_w0")
            ups = stage0[:, 0:STEPS0 * D].rearrange("p (e h) -> p e h", e=E + 1)
            downs = stage0[:, STEPS0 * D:].rearrange("p (e c d) -> p e c d", e=E + 1, c=C0)
            load(ups[:, 0:E, :], a["L0_ffn_rw1"].rearrange("e d h -> d e h"), "ld_f0")
            load(ups[:, E, :], a["L0_ffn_sw1"], "ld_f0")
            load(downs[:, 0:E, :, :], a["L0_ffn_rw2"].rearrange("e (c p) d -> p e c d", p=128), "ld_f0")
            load(downs[:, E, :, :], a["L0_ffn_sw2"].rearrange("(c p) d -> p c d", p=128), "ld_f0")
            load(w1q[:, :], a["L1_attn_Wq"], "ld_w1")
            load(w1vk[:, 0:D], a["L1_attn_Wv"], "ld_w1")
            load(w1vk[:, D:2 * D], a["L1_attn_Wk"], "ld_w1")
            load(b1q[:, :], per_partition(a["L1_attn_bq"], 1), "ld_w1")
            load(b1k, a["L1_attn_bk"].partition_broadcast(128), "ld_w1")
            load(temp[:, :], a["tempT"], "ld_w1")
            load(rw1[:, 0:E], a["gate_wT"], "ld_r1")
            load(rw1[:, E:E + 1], a["shared_gateT"], "ld_r1")

            def load_experts_1(w):
                sp.wait_ge(s["zeroed"], w + 1)
                if w < 2:
                    routed, shared = (("L1_ffn_w_gate", "L1_ffn_sw_gate"), ("L1_ffn_w_up", "L1_ffn_sw_up"))[w]
                    sp.dma_start(stage1[:, 0:E * H1].rearrange("p (e i) -> p e i", e=E),
                                 a[routed].rearrange("e d i -> d e i")).then_inc(s["stage_loaded"], 16)
                    sp.dma_start(stage1[:, E * H1:F1], a[shared]).then_inc(s["stage_loaded"], 16)
                else:
                    n = E * H1 // D
                    down = stage1.rearrange("p (c d) -> p c d", d=D)
                    sp.dma_start(down[:, 0:n, :],
                                 a["L1_ffn_w_down"].rearrange("e i d -> (e i) d").rearrange("(c p) d -> p c d", p=128)
                                 ).then_inc(s["stage_loaded"], 16)
                    sp.dma_start(down[:, n, :], a["L1_ffn_sw_down"][0:D, :]).then_inc(s["stage_loaded"], 16)
                    sp.dma_start(down[0:H1 - D, n + 1, :], a["L1_ffn_sw_down"][D:H1, :]
                                 ).then_inc(s["stage_loaded"], 16)

            def kv_store(p):
                for t in tiles(p):
                    sp.wait_ge(s["kvs_ready"], t + 1)
                    sp.dma_start(scratch["kv"][:, t * D:(t + 1) * D, :].rearrange("o p c -> p o c"),
                                 kvs[:, t % KVR, :, :].bitcast(fp32)).then_inc(kv_out[t % KVR], 16)

            def kv_load(p, stored_pairs):
                for r in range(KVR):
                    sp.wait_ge(kv_out[r], 16 * TPP * stored_pairs // KVR)
                if p >= 2:
                    sp.wait_ge(s["s1_ps"], HPG * GPP * (p - 1))
                for dst, parts in ((VS, (0, 1, 0)), (KS, (2, 2, 3))):
                    for j in range(HPG):
                        for n, o in enumerate(parts):
                            src = scratch["kv"][o, cols(p), :].rearrange(
                                "(g j d h) c -> j d g (h c)", j=HPG, d=DH, h=2)[j]
                            sp.dma_start(dst[32 * j + DH * n:32 * j + DH * n + DH, p % 2, :, :].bitcast(fp32), src
                                         ).then_inc(kv_in[p], 16)

            def attention_out(b):
                sp.wait_ge(s["o1_ready"], GPB * (b + 1))
                for j in range(HPG):
                    dst = scratch["ao"][b * S:(b + 1) * S, :].rearrange(
                        "(g j d h) c -> j d g (h c)", j=HPG, d=DH, h=2)[j]
                    sp.dma_start(dst, O[32 * j:32 * j + DH, b % 2, :, :]).then_inc(ao_out[b], 16)
                sp.wait_ge(ao_out[b], 16 * HPG)
                sp.dma_start(AO[:, TPB * b:TPB * b + TPB, :],
                             scratch["ao"][b * S:(b + 1) * S, :].rearrange("(t p) c -> p t c", p=128)
                             ).then_inc(ao_in[b], 16)

            for p in range(2):
                kv_store(p)
                kv_load(p, p + 1)
            kv_store(2)
            load_experts_1(0)
            kv_store(3)
            load_experts_1(1)
            for p in range(2, NP):
                kv_load(p, NP)
                if p == 3:
                    load_experts_1(2)
                attention_out(2 * p - 4)
                attention_out(2 * p - 3)
            attention_out(B - 4)
            attention_out(B - 3)
            attention_out(B - 2)
            attention_out(B - 1)
            for p in range(NP):
                sp.wait_ge(s["z_read"], NP + p + 1)
                sp.dma_start(out.rearrange("(t p) d -> p t d", p=128)[:, TPP * p:TPP * p + TPP, :],
                             X[:, TPP * p:TPP * p + TPP, :]).then_inc(stored, 16)
            sp.wait_ge(stored, 16 * NP)

        @block.gpsimd
        def _(pool):
            nc.gpsimd.memset(mhalf[:, :], -0.5).then_inc(s["pool_const"], 1)
            nc.gpsimd.memset(phalf[:, :], 0.5).then_inc(s["pool_const"], 1)
            nc.gpsimd.memset(ones[:, :], 1.0).then_inc(s["pool_const"], 1)
            pool.wait_ge(s["pool_const"], 3)

            def root(k, p):
                pool.wait_ge(s[f"ve_ready{k}"], p + 1)
                ts = slice(TPP * p, TPP * p + TPP)
                nc.gpsimd.tensor_tensor(rstd[:, k, ts], ve[:, k, ts], mhalf[:, 0:TPP], ALU.pow
                                        ).then_inc(s[f"rstd_ready{k}"], 1)

            for p in range(NP):
                root(0, p)
            for p in range(NP):
                pool.wait_ge(s["ss_ready"], p + 1)
                ts = slice(TPP * p, TPP * p + TPP)
                nc.gpsimd.tensor_tensor(nrm[:, ts], ss[:, ts], phalf[:, 0:TPP], ALU.pow
                                        ).then_inc(s["nrm_ready"], 1)
            pool.wait_ge(s["ld_f0"], 16 * N_LD["ld_f0"])
            for n in range(2 * STEPS0 // 4):
                pool.wait_ge(s["w0_high"], n + 1)
                c = slice(4 * D * n, 4 * D * n + 4 * D)
                nc.gpsimd.tensor_tensor(WL[:, c], stage0[:, c], WH[:, c].bitcast(fp32), ALU.subtract
                                        ).then_inc(s["w0_low"], 1)
            root(1, 0)
            for p in range(NP):
                if p + 1 < NP:
                    root(1, p + 1)
                if p >= 1:
                    root(2, p - 1)

            def clear(w):
                if w == 0:
                    pool.wait_ge(s["y_ps"], NP)
                    pool.wait_ge(s["low_ready"], NP * STEPS0)
                else:
                    pool.wait_ge(s["w1_low"], 2 * w)
                if w < 2:
                    nc.gpsimd.memset(stage1[:, F1:FP], 0.0).then_inc(s["zeroed"], 1)
                else:
                    nc.gpsimd.memset(stage1[:, FP - D:FP], 0.0).then_inc(s["zeroed"], 1)

            def split(w):
                pool.wait_ge(s["stage_loaded"], 16 * (2, 4, 7)[w])
                for h in range(2):
                    c = slice(h * FP // 2, (h + 1) * FP // 2)
                    d = slice(w * FP + h * FP // 2, w * FP + (h + 1) * FP // 2)
                    nc.gpsimd.tensor_copy(WH[:, d], stage1[:, c]).then_inc(s["w1_high"], 1)
                    pool.wait_ge(s["w1_high"], 2 * w + h + 1)
                    nc.gpsimd.tensor_tensor(WL[:, d], stage1[:, c], WH[:, d].bitcast(fp32), ALU.subtract
                                            ).then_inc(s["w1_low"], 1)

            clear(0)
            root(2, NP - 1)
            split(0)
            clear(1)
            split(1)
            root(3, 0)
            clear(2)
            split(2)
            for p in range(1, NP):
                root(3, p)

        @block.vector
        def _(dve):
            v = nc.vector
            step = [0]

            def link(ins):
                step[0] += 1
                ins.then_inc(s["v_step"], 1)
                dve.wait_ge(s["v_step"], step[0])

            def guard(dst, gate, tmp):
                v.tensor_scalar(tmp, gate, 0.0, 2.0, ALU.is_ge, ALU.mult)
                link(v.scalar_tensor_tensor(out=gate, in0=gate, scalar=-1.0, in1=gate, op0=ALU.mult, op1=ALU.max))
                link(v.tensor_scalar(gate, gate, 0.25, None, ALU.max))
                return v.scalar_tensor_tensor(out=dst, in0=tmp, scalar=-1.0, in1=gate,
                                              op0=ALU.add, op1=ALU.mult)

            def pair(p):
                return slice(TPP * p, TPP * p + TPP)

            def ln_stats(k, p):
                for t in tiles(p):
                    last = v.bn_stats(st[:, t, :], X[:, t, :])
                link(last)
                for t in tiles(p):
                    last = v.bn_aggr(mv[:, k, t, :], st[:, t, :])
                link(last)
                v.tensor_scalar(ve[:, k, pair(p)], mv[:, k, pair(p), 1], EPS, None, ALU.add
                                ).then_inc(s[f"ve_ready{k}"], 1)

            def ln_apply(k, p):
                dve.wait_ge(s[f"rstd_ready{k}"], p + 1)
                if k >= 1:
                    dve.wait_ge(s[f"xt_ps{k - 1}"], p + 1)
                for t in tiles(p):
                    last = v.tensor_scalar(SC[:, t, :], X[:, t, :], mv[:, k, t, 0:1],
                                           rstd[:, k, t:t + 1], ALU.subtract, ALU.mult)
                last.then_inc(s[f"xn_ready{k}"], 1)

            def modulate(k, p):
                l, m = ((0, 3), (1, 0), (1, 3))[k - 1]
                dve.wait_ge(s[f"xt_ps{k}"], p + 1)
                for h in range(2):
                    b = 2 * p + h
                    last = v.tensor_scalar(XT[:, b * S:(b + 1) * S], P[:, MISC, h * S:(h + 1) * S],
                                           mcol[:, l, m + 1, b:b + 1], mcol[:, l, m, b:b + 1], ALU.mult, ALU.add)
                last.then_inc(s[f"xt_sb{k}"], 1)

            def low_input(l, p):
                n = NP * l + p
                dve.wait_ge(s["xh_ready"], n + 1)
                v.tensor_tensor(XL[:, p % 2, :], XT[:, cols(p)], XH[:, p % 2, :].bitcast(fp32), ALU.subtract
                                ).then_inc(s["xl_ready"], 1)

            def router_logits(l, p):
                n, n9, ts = NP * l + p, E + l, half(p)
                dve.wait_ge(s["r_ps"], n + 1)
                R = P[:, MISC, 0:TPP * n9].rearrange("p (t e) -> p t e", e=n9)
                if l == 0:
                    link(v.tensor_tensor(lg[:, ts, 0:E], R, rb0[:, :].unsqueeze(1).broadcast_to([128, TPP, E]), ALU.add))
                else:
                    link(v.tensor_copy(lg[:, ts, :], R))
                link(v.reduce_max(nmr[:, ts], lg[:, ts, 0:E], AX.X))
                if l == 1:
                    v.tensor_scalar(ld[:, ts, E], lg[:, ts, E], -1.0, None, ALU.mult)
                v.tensor_tensor(ld[:, ts, 0:E], lg[:, ts, 0:E],
                                nmr[:, ts].unsqueeze(2).broadcast_to([128, TPP, E]), ALU.subtract
                                ).then_inc(s["rd_ready"], 1)

            def router_weights(l, p):
                n, n9, ts = NP * l + p, E + l, half(p)
                dve.wait_ge(s["rex_ready"], n + 1)
                for t in range(TPP * (p % 2), TPP * (p % 2) + TPP):
                    last = v.max(top[:, t, :], ex[:, t, 0:E])
                link(last)
                if l == 0:
                    v.reduce_sum(tden[:, ts], ex[:, ts, 0:E], AX.X)
                else:
                    v.tensor_scalar(res[:, ts, E], ex[:, ts, E], 1.0, None, ALU.add)
                    v.reduce_sum(tden[:, ts], top[:, ts, 0:2], AX.X)
                for t in range(TPP * (p % 2), TPP * (p % 2) + TPP):
                    last = v.max_index(tix[:, t, :], top[:, t, :], ex[:, t, 0:E])
                link(last)
                link(v.tensor_copy(tif[:, ts, :], tix[:, ts, 0:2]))
                if l == 1:
                    v.reciprocal(W[:, ts, E], res[:, ts, E])
                link(v.reciprocal(trc[:, ts], tden[:, ts]))
                for k in range(2):
                    last = v.tensor_tensor(oh[:, ts, k, :], iota[:, :].unsqueeze(1).broadcast_to([128, TPP, E]),
                                           tif[:, ts, k].unsqueeze(2).broadcast_to([128, TPP, E]), ALU.is_equal)
                link(v.tensor_tensor(tw[:, ts, :], top[:, ts, 0:2],
                                     trc[:, ts].unsqueeze(2).broadcast_to([128, TPP, 2]), ALU.mult))
                for k in range(2):
                    last = v.tensor_tensor(oh[:, ts, k, :], oh[:, ts, k, :],
                                           tw[:, ts, k].unsqueeze(2).broadcast_to([128, TPP, E]), ALU.mult)
                link(last)
                link(v.tensor_tensor(W[:, ts, 0:E], oh[:, ts, 0, :], oh[:, ts, 1, :], ALU.add))
                link(v.tensor_copy(WP[:, ts, 0:n9], W[:, ts, 0:n9]))
                link(v.tensor_tensor(res[:, ts, 0:n9], W[:, ts, 0:n9], WP[:, ts, 0:n9], ALU.subtract))
                link(v.tensor_copy(WP[:, ts, n9:2 * n9], res[:, ts, 0:n9]))
                v.tensor_tensor(WP[:, ts, 2 * n9:3 * n9], res[:, ts, 0:n9], WP[:, ts, n9:2 * n9],
                                ALU.subtract).then_inc(s["w_ready"], 1)

            def gate_experts(l, p):
                n = NP * l + p
                dve.wait_ge(s["y_ps"], n + 1)
                if n >= 2:
                    dve.wait_ge(s["z_ps"], n - 1)
                bank = bank_y0[p] if l == 0 else bank_y1
                for h in range(2):
                    b = 2 * p + h
                    last = v.tensor_scalar(yT[:, n % 2, h * S:(h + 1) * S], P[:, bank, h * S:(h + 1) * S],
                                           sb2[:, :] if l == 0 else 0.0, mcol[:, l, 5, b:b + 1], ALU.add, ALU.mult)
                last.then_inc(s["y_sb"], 1)

            def add_experts(l, p):
                n = NP * l + p
                dve.wait_ge(s["z_ps"], n + 1)
                v.tensor_tensor(X[:, pair(p), :], X[:, pair(p), :],
                                P[:, MISC, :].rearrange("p (t d) -> p t d", d=D), ALU.add
                                ).then_inc(s["z_read"], 1)
                dve.wait_ge(s["z_read"], n + 1)

            def kv(n):
                dve.wait_ge(s["kv_ps"], n + 1)
                for t in (2 * n, 2 * n + 1):
                    if t >= KVR:
                        dve.wait_ge(kv_out[t % KVR], 16 * (t // KVR))
                    ps = P[:, bank_kv(n), (t % 2) * 2 * D:(t % 2) * 2 * D + 2 * D]
                    v.tensor_tensor(kvf[:, t % 2, 0, :], ps[:, 0:D], b1v[:, :], ALU.add)
                    link(v.scalar_tensor_tensor(out=kvf[:, t % 2, 1, :], in0=ps[:, D:2 * D],
                                                scalar=temp[:, t % 2:t % 2 + 1], in1=b1kt[:, t % 2, :],
                                                op0=ALU.mult, op1=ALU.add))
                    link(v.tensor_copy(kvs[:, t % KVR, 0:4:2, :], kvf[:, t % 2, :, :]))
                    v.tensor_tensor(kvs[:, t % KVR, 1:4:2, :], kvf[:, t % 2, :, :],
                                    kvs[:, t % KVR, 0:4:2, :].bitcast(fp32), ALU.subtract
                                    ).then_inc(s["kvs_ready"], 1)

            for p in range(NP):
                dve.wait_ge(ld_x[p], 16)
                if p == 1:
                    dve.wait_ge(s["silu_done"], 1)
                    for l in range(2):
                        last = v.tensor_copy(scB[:, l, :, :], scT[:, l, :].unsqueeze(2).broadcast_to([128, B, D]))
                    last.then_inc(s["scb_done"], 1)
                ln_stats(0, p)
            for p in range(NP):
                ln_apply(0, p)
            dve.wait_ge(s["mod_ps"], 1)
            link(v.tensor_copy(mcol[:, :, :, :], P[:, 0, 0:12 * B].rearrange("p (l m b) -> p l m b", l=2, m=6)))
            v.tensor_copy(mcol[:, :, 0, 0:1], mcol[:, :, 0, 0:1]).then_inc(s["mod_sb"], 1)
            for m in (1, 4):
                last = v.tensor_scalar(mcol[:, :, m, :], mcol[:, :, m, :], 1.0, None, ALU.add)
            last.then_inc(s["mod_done"], 1)
            for h in range(4):
                dve.wait_ge(s["mod_ps"], h + 2)
                v.tensor_copy((mrow0, mrow1)[h // 2][:, 4 * (h % 2):4 * (h % 2) + 4, :],
                              P[:, h, :].rearrange("p (b d) -> p b d", d=D)).then_inc(s["mod_sb"], 1)

            dve.wait_ge(s["ld_b"], 16 * N_LD["ld_b"])
            v.tensor_copy(sel0[:, :], sel0f)
            v.tensor_copy(sel1[:, :], sel1f)
            link(v.tensor_copy(dbp[:, 0, :], db0[:, :]))
            link(v.tensor_tensor(dbr[:, :], db0[:, :], dbp[:, 0, :], ALU.subtract))
            link(v.tensor_copy(dbp[:, 1, :], dbr[:, :]))
            v.tensor_tensor(dbp[:, 2, :], dbr[:, :], dbp[:, 1, :], ALU.subtract).then_inc(s["const_done"], 1)

            def norms(p):
                dve.wait_ge(s["nrm_ready"], p + 1)
                link(v.tensor_scalar(rn[:, pair(p)], nrm[:, pair(p)], 1e-9, None, ALU.add))
                link(v.reciprocal(rn[:, pair(p)], rn[:, pair(p)]))
                if p >= 1:
                    dve.wait_ge(s["rn_ps"], p)
                for i, t in enumerate(tiles(p)):
                    last = v.tensor_scalar(dg[:, i, :], ident[:, :], rn[:, t:t + 1], None, ALU.mult)
                last.then_inc(s["dg_ready"], 1)

            for p in range(NP):
                dve.wait_ge(s["ss_ps"], p + 1)
                v.tensor_copy(ss[:, pair(p)], P[:, bank_ss[p], 0:TPP]).then_inc(s["ss_ready"], 1)
                if p >= 1:
                    norms(p - 1)
            norms(NP - 1)
            for p in range(NP):
                dve.wait_ge(s["rn_ps"], p + 1)
                v.tensor_tensor(XT[:, cols(p)], XT[:, cols(p)], P[:, bank_rn[p], :], ALU.mult
                                ).then_inc(s["xt_sb0"], 1)
            dve.wait_ge(s["mod_sb"], 5)
            for l, rows in enumerate((mrow0, mrow1)):
                rows = rows[:, :, :].rearrange("p b d -> p (b d)")
                link(guard(rows, rows, gtmp[:, l, :, :].rearrange("p b d -> p (b d)")))
            link(guard(mcol[:, :, 5, :], mcol[:, :, 5, :], gtmc[:, :, :]))
            dve.wait_ge(s["ld_w0"], 16 * N_LD["ld_w0"])
            for p in range(NP):
                dve.wait_ge(s["v0_ps"], p + 1)
                v.tensor_tensor(V[:, pair(p), :],
                                P[:, bank_v0[p], :].rearrange("p (t d) -> p t d", d=D),
                                b0v[:, :].unsqueeze(1).broadcast_to([128, TPP, D]), ALU.add).then_inc(s["v0_sb"], 1)
            for p in range(NP):
                dve.wait_ge(s["tq_ps"], p + 1)
                v.tensor_copy(tqT[:, cols(p)], P[:, bank_tq[p], :]).then_inc(s["tq_sb"], 1)
            for b in range(B):
                dve.wait_ge(s["s0_ps"], b + 1)
                ts = slice(TPB * b, TPB * b + TPB)
                link(v.reduce_max(nm0[:, ts], P[:, bank_s0[b], :].rearrange("p (i t) -> p i t", i=TPB), AX.X))
                v.tensor_scalar(nms0[:, ts], nm0[:, ts], -(D ** -0.5), None, ALU.mult).then_inc(s["nm0_ready"], 1)
            def context0(b):
                dve.wait_ge(s["c0_ps"], b + 1)
                ts = slice(TPB * b, TPB * b + TPB)
                link(v.reciprocal(nz[:, ts], Z0[:, ts]))
                link(v.tensor_tensor(nz[:, ts], nz[:, ts], nrm[:, ts], ALU.mult))
                for i in range(TPB):
                    t = TPB * b + i
                    last = v.scalar_tensor_tensor(out=ctmp[:, i, :], in0=P[:, bank_c0[b], i * D:(i + 1) * D],
                                                  scalar=nz[:, t:t + 1], in1=mrow0[:, b, :],
                                                  op0=ALU.mult, op1=ALU.mult)
                link(last)
                v.tensor_tensor(X[:, ts, :], X[:, ts, :], ctmp[:, :, :], ALU.add).then_inc(s["c0_read"], 1)
                dve.wait_ge(s["c0_read"], b + 1)

            context0(0)
            context0(1)
            ln_stats(1, 0)
            context0(2)
            ln_apply(1, 0)
            context0(3)
            modulate(1, 0)
            context0(4)
            low_input(0, 0)
            router_logits(0, 0)
            context0(5)
            router_weights(0, 0)
            context0(6)
            context0(7)

            def low_part(u, source):
                dve.wait_ge(s["high_ready"], u + 1)
                if u >= 3:
                    dve.wait_ge(s["down_done"], u - 2)
                v.tensor_tensor(hidl[:, u % 3, :], source, hidh[:, u % 3, :].bitcast(fp32), ALU.subtract
                                ).then_inc(s["low_ready"], 1)

            def hidden0(u):
                return act_out[:, u % 3, :] if u % STEPS0 >= E * C0 else hidf[:, u % 2, :]

            for u in range(NP * STEPS0):
                p, i = divmod(u, STEPS0)
                if i < E * C0:
                    dve.wait_ge(s["bc_ps"], p * E + i // C0 + 1)
                    dve.wait_ge(s["act_ready"], u + 1)
                    if u >= 2:
                        dve.wait_ge(s["low_ready"], u - 1)
                    v.tensor_tensor(hidf[:, u % 2, :], act_out[:, u % 3, :], P[:, bank_bc(p * E + i // C0), :],
                                    ALU.mult).then_inc(s["bc_read"], 1)
                if u >= 1:
                    low_part(u - 1, hidden0(u - 1))
                if p + 1 < NP:
                    if i == 0:
                        ln_stats(1, p + 1)
                    if i == 1:
                        ln_apply(1, p + 1)
                    if i == 4:
                        modulate(1, p + 1)
                    if i == 6:
                        low_input(0, p + 1)
                    if i == 8:
                        router_logits(0, p + 1)
                    if i == 10:
                        router_weights(0, p + 1)
                if p >= 1:
                    if i == 3:
                        gate_experts(0, p - 1)
                    if i == 6:
                        add_experts(0, p - 1)
                        ln_stats(2, p - 1)
                    if i == 7:
                        ln_apply(2, p - 1)
                    if i == 11:
                        modulate(2, p - 1)
                    if i == 15:
                        if p == 1:
                            dve.wait_ge(s["ld_w1"], 16 * N_LD["ld_w1"])
                            for k in range(2):
                                last = v.tensor_scalar(b1kt[:, k, :], b1k, temp[:, k:k + 1], None, ALU.mult)
                            link(last)
                        kv(2 * p - 2)
                    if i == 17:
                        kv(2 * p - 1)
            low_part(NP * STEPS0 - 1, hidden0(NP * STEPS0 - 1))

            def qT1(g):
                return qT[:, GT * g:GT * g + GT].rearrange("p (j d h) -> p j d h", j=HPG, d=DH)

            def maxima(g):
                for h in range(HPG // 2):
                    dve.wait_ge(s["s1_ps"], HPG * g + 2 * h + 2)
                    v.tensor_reduce(nm1[:, g % 4, 2 * h:2 * h + 2, :],
                                    P[:, 2 * h:2 * h + 2, :].rearrange("p j (h s) -> p (j h) s", h=2),
                                    AX.X, ALU.max, negate=True).then_inc(s["nm1_ready"], 1)

            def queries(g):
                dve.wait_ge(s["e1_ready"], HPG * (g + 1))
                dve.wait_ge(s["q1_sb"], g // GPP + 1)
                if g >= 2:
                    dve.wait_ge(s["c1_ps"], g - 1)
                link(v.reciprocal(rz1[:, g % 4, :, :], Z1[:, g % 4, :, :]))
                for h in range(2):
                    last = v.tensor_tensor(
                        qs[:, g % 2, :, h, :], qT1(g)[:, :, :, h],
                        rz1[:, g % 4, :, h].unsqueeze(2).broadcast_to([128, HPG, DH]), ALU.mult)
                link(last)
                v.tensor_copy(qs4[:, g % 2, :, :, :, :].rearrange("p j h r d -> p (j h) r d"),
                              qs[:, g % 2, :, :, :].rearrange("p j h d -> p (j h) d").unsqueeze(2).broadcast_to([128, 2 * HPG, HPG, DH])
                              ).then_inc(s["qs_ready"], 1)

            def outputs(g):
                b = g // GPB
                dve.wait_ge(s["c1_ps"], g + 1)
                if b >= 2 and g % GPB == 0:
                    dve.wait_ge(ao_out[b - 2], 16 * HPG)
                v.tensor_copy(O[:, b % 2, g % GPB, :], P[:, 4 + g % 2, 0:S]).then_inc(s["o1_ready"], 1)

            def attention_residual(b):
                ts = slice(TPB * b, TPB * b + TPB)
                dve.wait_ge(ao_in[b], 16)
                link(v.tensor_tensor(AO[:, ts, :], AO[:, ts, :],
                                     mrow1[:, b, :].unsqueeze(1).broadcast_to([128, TPB, D]), ALU.mult))
                link(v.tensor_tensor(X[:, ts, :], X[:, ts, :], AO[:, ts, :], ALU.add))

            maxima(0)
            gate_experts(0, NP - 1)
            for g in range(NG):
                if g + 1 < NG:
                    maxima(g + 1)
                queries(g)
                if g >= 2:
                    outputs(g - 2)
                if g == 1:
                    add_experts(0, NP - 1)
                    ln_stats(2, NP - 1)
                if g == 2:
                    ln_apply(2, NP - 1)
                if g == 4:
                    modulate(2, NP - 1)
                if g == 6:
                    kv(2 * NP - 2)
                if g == 7:
                    kv(2 * NP - 1)
                for p in range(2):
                    i = g - GPP * p
                    if i == 12:
                        attention_residual(2 * p)
                        attention_residual(2 * p + 1)
                        ln_stats(3, p)
                    if i == 13:
                        ln_apply(3, p)
                    if i == 14:
                        modulate(3, p)
                    if i == 15:
                        low_input(1, p)
                        router_logits(1, p)
                    if i == 16:
                        router_weights(1, p)
            outputs(NG - 2)
            outputs(NG - 1)

            base = NP * STEPS0
            for n in range(NP * C1):
                p, i = divmod(n, C1)
                dve.wait_ge(s["u_ps"], n + 1)
                dve.wait_ge(s["gact_ready"], n + 1)
                v.tensor_tensor(gu[:, n % 2, :], act_out[:, n % 3, :], P[:, bank_u(n), :], ALU.mult
                                ).then_inc(s["u_read"], 1)
                if n >= 1:
                    low_part(base + n - 1, hidf[:, (n - 1) % 2, :])
                dve.wait_ge(s["u_read"], n + 1)
                dve.wait_ge(s["bc_ps"], NP * E + n + 1)
                if n >= 2:
                    dve.wait_ge(s["low_ready"], base + n - 1)
                v.tensor_tensor(hidf[:, n % 2, :], gu[:, n % 2, :], P[:, bank_bc(n), :],
                                ALU.mult).then_inc(s["bc_read"], 1)
                if p == 0 and i in (2, 4):
                    for b in (2 + i, 3 + i):
                        attention_residual(b)
                if p in (1, 2):
                    if i == 0:
                        ln_stats(3, p + 1)
                    if i == 1:
                        ln_apply(3, p + 1)
                    if i == 3:
                        modulate(3, p + 1)
                    if i == 5:
                        low_input(1, p + 1)
                        router_logits(1, p + 1)
                    if i == 8:
                        router_weights(1, p + 1)
                if p >= 1:
                    if i == 2:
                        gate_experts(1, p - 1)
                    if i == 7:
                        add_experts(1, p - 1)
            low_part(base + NP * C1 - 1, hidf[:, (NP * C1 - 1) % 2, :])
            gate_experts(1, NP - 1)
            add_experts(1, NP - 1)

        @block.scalar
        def _(act):
            sc = nc.scalar
            act.wait_ge(s["ld_c"], 16 * N_LD["ld_c"])
            sc.activation(scT[:, :, :], cT[:, :, :], ACT.Silu).then_inc(s["silu_done"], 1)
            sc.activation(identb[:, :], ident[:, :], ACT.Copy).then_inc(s["identb_done"], 1)
            for p in range(NP):
                act.wait_ge(s["xt_ps0"], p + 1)
                act.wait_ge(s["mod_done"], 1)
                for h in range(2):
                    b = 2 * p + h
                    last = sc.activation(XT[:, b * S:(b + 1) * S], P[:, bank_xt0[p], h * S:(h + 1) * S],
                                         ACT.Identity, bias=mcol[:, 0, 0, b:b + 1], scale=mcol[:, 0, 1, b:b + 1])
                last.then_inc(s["hh_ready"], 1)
                act.wait_ge(s["hh_ready"], 2 * p + 1)
                sc.activation(HH[:, cols(p)], XT[:, cols(p)], ACT.Square).then_inc(s["hh_ready"], 1)

            def high_weights(n):
                c = slice(4 * D * n, 4 * D * n + 4 * D)
                sc.activation(WH[:, c], stage0[:, c], ACT.Copy).then_inc(s["w0_high"], 1)

            act.wait_ge(s["ld_f0"], 16 * N_LD["ld_f0"])
            for n in range(2 * STEPS0 // 4):
                high_weights(n)
            act.wait_ge(s["ld_w0"], 16 * N_LD["ld_w0"])
            for p in range(NP):
                act.wait_ge(s["q0_ps"], p + 1)
                sc.activation(qT[:, cols(p)], P[:, bank_q0[p], :], ACT.Identity, bias=b0q[:, :]).then_inc(s["q0_sb"], 1)
            act.wait_ge(s["const_done"], 1)
            act.wait_ge(s["w0_low"], 2 * STEPS0 // 4)
            for b in range(B):
                act.wait_ge(s["nm0_ready"], b + 1)
                for i in range(TPB):
                    t = TPB * b + i
                    sc.activation(PR[:, t, :], P[:, bank_s0[b], i * S:(i + 1) * S], ACT.Exp,
                                  bias=nms0[:, t:t + 1], scale=D ** -0.5,
                                  accum_out=Z0[:, t:t + 1]).then_inc(s["p0_ready"], 1)
            for b in range(B):
                act.wait_ge(s["pt_ps"], b + 1)
                sc.activation(PRT[:, b, :, :], P[:, bank_pt[b], :].rearrange("p (j q) -> p j q", j=TPB),
                              ACT.Copy).then_inc(s["pt_sb"], 1)

            def high_input(l, p):
                act.wait_ge(s[f"xt_sb{(1, 3)[l]}"], p + 1)
                if p >= 2:
                    act.wait_ge(s["y_ps"], NP * l + p - 1)
                sc.activation(XH[:, p % 2, :], XT[:, cols(p)], ACT.Copy).then_inc(s["xh_ready"], 1)

            def router_exp(l, p):
                act.wait_ge(s["rd_ready"], NP * l + p + 1)
                sc.activation(ex[:, half(p), 0:E + l], ld[:, half(p), 0:E + l], ACT.Exp).then_inc(s["rex_ready"], 1)

            def weights_out(l, p):
                n, r = NP * l + p, 3 * (E + l)
                act.wait_ge(s["wt_ps"], n + 1)
                sc.activation(WPT[0:r, p % 2, :], P[0:r, MISC, 0:PT // 2].bitcast(bf16), ACT.Copy
                              ).then_inc(s["wt_sb"], 1)

            def queries_out(p):
                act.wait_ge(s["q1_ps"], p + 1)
                sc.activation(qT[:, cols(p)], P[:, MISC, :], ACT.Identity, bias=b1q[:, :]).then_inc(s["q1_sb"], 1)

            def high_part(u, source):
                if u >= 3:
                    act.wait_ge(s["down_done"], u - 2)
                sc.activation(hidh[:, u % 3, :], source, ACT.Copy).then_inc(s["high_ready"], 1)

            high_input(0, 0)
            router_exp(0, 0)
            weights_out(0, 0)
            act.wait_ge(s["ld_b"], 16 * N_LD["ld_b"])
            act.wait_ge(s["ld_w1"], 16 * N_LD["ld_w1"])

            def high0(u):
                p, i = divmod(u, STEPS0)
                if i < E * C0:
                    act.wait_ge(s["bc_read"], p * E * C0 + i + 1)
                    high_part(u, hidf[:, u % 2, :])
                else:
                    act.wait_ge(s["act_ready"], u + 1)
                    high_part(u, act_out[:, u % 3, :])

            for u in range(NP * STEPS0):
                p, i = divmod(u, STEPS0)
                act.wait_ge(s["up_ps"], u + 1)
                if u >= 3:
                    pp, ii = divmod(u - 3, STEPS0)
                    if ii < E * C0:
                        act.wait_ge(s["bc_read"], pp * E * C0 + ii + 1)
                    else:
                        act.wait_ge(s["low_ready"], u - 2)
                sc.activation(act_out[:, u % 3, :], P[:, bank_up(u), :], ACT.Gelu,
                              bias=ub0[:, i // C0, i % C0:i % C0 + 1]).then_inc(s["act_ready"], 1)
                if u >= 1:
                    high0(u - 1)
                if p + 1 < NP:
                    if i == 5:
                        high_input(0, p + 1)
                    if i == 9:
                        router_exp(0, p + 1)
                    if i == 13:
                        weights_out(0, p + 1)
                if p >= 1 and i == 14:
                    queries_out(p - 1)
            high0(NP * STEPS0 - 1)

            for g in range(NG):
                for j in range(HPG):
                    act.wait_ge(s["nm1_ready"], 2 * g + j // 2 + 1)
                    if g >= 3 and j == 0:
                        act.wait_ge(s["c1_ps"], g - 2)
                    for h in range(2):
                        last = sc.activation(EX[:, g % 3, j, h * S:(h + 1) * S], P[:, j, h * S:(h + 1) * S],
                                             ACT.Exp, bias=nm1[:, g % 4, j, h:h + 1], accum_out=Z1[:, g % 4, j, h:h + 1])
                    last.then_inc(s["e1_ready"], 1)
                if g == 5:
                    queries_out(NP - 1)
                for p in range(2):
                    i = g - GPP * p
                    if i == 14:
                        high_input(1, p)
                    if i == 15:
                        router_exp(1, p)
                    if i == 17 or g == NG - 1 and i < 17 and p == 2:
                        weights_out(1, p)

            base = NP * STEPS0

            def high1(n):
                act.wait_ge(s["bc_read"], NP * E * C0 + n + 1)
                high_part(base + n, hidf[:, n % 2, :])

            for n in range(NP * C1):
                p, i = divmod(n, C1)
                act.wait_ge(s["g_ps"], n + 1)
                if n >= 3:
                    act.wait_ge(s["u_read"], n - 2)
                else:
                    act.wait_ge(s["low_ready"], base)
                sc.activation(act_out[:, n % 3, :], P[:, bank_g(n), :], ACT.Silu).then_inc(s["gact_ready"], 1)
                if n >= 1:
                    high1(n - 1)
                if p in (1, 2):
                    if i == 4:
                        high_input(1, p + 1)
                    if i == 6:
                        router_exp(1, p + 1)
                    if i == 10:
                        weights_out(1, p + 1)
            high1(NP * C1 - 1)

        @block.tensor
        def _(pe):
            mm = nc.tensor.matmul
            reader = {}

            def claim(bank, who, value):
                if bank in reader:
                    pe.wait_ge(*reader[bank])
                reader[bank] = (s[who], value)

            def split_mm(bank, w, m, xh, xl, start, stop):
                mm(P[:, bank, :], WH[:, w:w + m], xh, start=start, stop=False)
                mm(P[:, bank, :], WL[:, w:w + m], xh, start=False, stop=False)
                return mm(P[:, bank, :], WH[:, w:w + m], xl, start=False, stop=stop)

            pe.wait_ge(s["silu_done"], 1)
            claim(0, "mod_sb", 1)
            for l in range(2):
                for m in range(6):
                    last = mm(P[:, 0, (l * 6 + m) * B:(l * 6 + m + 1) * B], wmod[:, l, m * D:(m + 1) * D],
                              scT[:, l, :], start=True, stop=True)
            last.then_inc(s["mod_ps"], 1)

            def transpose_tokens(k, p, bank):
                pe.wait_ge(s[f"xn_ready{k}"], p + 1)
                claim(bank, f"xt_sb{k}", p + 1)
                for i, t in enumerate(tiles(p)):
                    last = nc.tensor.transpose(P[:, bank, i * D:(i + 1) * D], SC[:, t, :], ident[:, :])
                last.then_inc(s[f"xt_ps{k}"], 1)

            for p in range(NP):
                transpose_tokens(0, p, bank_xt0[p])
                reader[bank_xt0[p]] = (s["hh_ready"], 2 * p + 1)
            pe.wait_ge(s["scb_done"], 1)
            for h in range(4):
                claim(h, "mod_sb", h + 2)
                for i in range(4):
                    last = mm(P[:, h, i * D:(i + 1) * D], scB[:, h // 2, 4 * (h % 2) + i, :],
                              wmod[:, h // 2, 2 * D:3 * D], start=True, stop=True)
                last.then_inc(s["mod_ps"], 1)

            pe.wait_ge(s["pool_const"], 3)
            for p in range(NP):
                pe.wait_ge(s["hh_ready"], 2 * p + 2)
                claim(bank_ss[p], "ss_ready", p + 1)
                for i, t in enumerate(tiles(p)):
                    last = mm(P[:, bank_ss[p], i:i + 1], HH[:, t * D:(t + 1) * D], ones[:, 0:1], start=True, stop=True)
                last.then_inc(s["ss_ps"], 1)
            for p in range(NP):
                pe.wait_ge(s["dg_ready"], p + 1)
                claim(bank_rn[p], "xt_sb0", p + 1)
                mm(P[:, bank_rn[p], :], ones[:, :], dg[:, :, :].rearrange("p t d -> p (t d)"), start=True, stop=True
                   ).then_inc(s["rn_ps"], 1)
            pe.wait_ge(s["ld_w0"], 16 * N_LD["ld_w0"])
            for p in range(NP):
                pe.wait_ge(s["xt_sb0"], p + 1)
                claim(bank_q0[p], "q0_sb", p + 1)
                mm(P[:, bank_q0[p], :], w0q[:, :], XT[:, cols(p)], start=True, stop=True).then_inc(s["q0_ps"], 1)
                claim(bank_v0[p], "v0_sb", p + 1)
                for i, t in enumerate(tiles(p)):
                    last = mm(P[:, bank_v0[p], i * D:(i + 1) * D], XT[:, t * D:(t + 1) * D], w0v[:, :],
                              start=True, stop=True)
                last.then_inc(s["v0_ps"], 1)
            for p in range(NP):
                pe.wait_ge(s["q0_sb"], p + 1)
                claim(bank_tq[p], "tq_sb", p + 1)
                mm(P[:, bank_tq[p], :], w0a[:, :], qT[:, cols(p)], start=True, stop=True).then_inc(s["tq_ps"], 1)
            for b in range(B):
                pe.wait_ge(s["tq_sb"], b // 2 + 1)
                claim(bank_s0[b], "p0_ready", TPB * (b + 1))
                for i in range(TPB):
                    t = TPB * b + i
                    last = mm(P[:, bank_s0[b], i * S:(i + 1) * S], qT[:, t * D:(t + 1) * D],
                              tqT[:, b * S:(b + 1) * S], start=True, stop=True)
                last.then_inc(s["s0_ps"], 1)
            for b in range(B):
                pe.wait_ge(s["p0_ready"], TPB * (b + 1))
                claim(bank_pt[b], "pt_sb", b + 1)
                for j in range(TPB):
                    for i in range(TPB):
                        last = nc.tensor.transpose(P[:, bank_pt[b], j * S + i * D:j * S + (i + 1) * D],
                                                   PR[:, TPB * b + i, j * D:(j + 1) * D], ident[:, :])
                last.then_inc(s["pt_ps"], 1)
            for b in range(B):
                pe.wait_ge(s["pt_sb"], b + 1)
                pe.wait_ge(s["v0_sb"], b // 2 + 1)
                claim(bank_c0[b], "c0_read", b + 1)
                for i in range(TPB):
                    for j in range(TPB):
                        last = mm(P[:, bank_c0[b], i * D:(i + 1) * D], PRT[:, b, j, i * D:(i + 1) * D],
                                  V[:, TPB * b + j, :], start=(j == 0), stop=(j == TPB - 1))
                last.then_inc(s["c0_ps"], 1)

            def route(l, p):
                n, n9, k = NP * l + p, E + l, (1, 3)[l]
                pe.wait_ge(s[f"xt_sb{k}"], p + 1)
                claim(MISC, "rd_ready", n + 1)
                for i, t in enumerate(tiles(p)):
                    last = mm(P[:, MISC, i * n9:(i + 1) * n9], XT[:, t * D:(t + 1) * D],
                              (rw0, rw1)[l][:, :], start=True, stop=True)
                last.then_inc(s["r_ps"], 1)

            def weights_back(l, p):
                n, n9 = NP * l + p, E + l
                pe.wait_ge(s["w_ready"], n + 1)
                claim(MISC, "wt_sb", n + 1)
                for i, t in enumerate(tiles(p)):
                    last = nc.tensor.transpose(P[0:3 * n9, MISC, 0:PT // 2].bitcast(bf16)[:, i * D:(i + 1) * D],
                                               WP[:, TPP * (p % 2) + i, 0:3 * n9], identb[:, :])
                last.then_inc(s["wt_ps"], 1)

            def tokens_back(l, p):
                n = NP * l + p
                pe.wait_ge(s["y_sb"], n + 1)
                claim(MISC, "z_read", n + 1)
                for i in range(TPP):
                    last = nc.tensor.transpose(P[:, MISC, i * D:(i + 1) * D], yT[:, n % 2, i * D:(i + 1) * D],
                                               ident[:, :])
                last.then_inc(s["z_ps"], 1)

            def project_q(p):
                pe.wait_ge(s["xt_sb2"], p + 1)
                claim(MISC, "q1_sb", p + 1)
                mm(P[:, MISC, :], w1q[:, :], XT[:, cols(p)], start=True, stop=True).then_inc(s["q1_ps"], 1)

            def project_kv(n):
                claim(bank_kv(n), "kvs_ready", 2 * n + 2)
                for i in range(2):
                    t = 2 * n + i
                    last = mm(P[:, bank_kv(n), i * 2 * D:(i + 1) * 2 * D], XT[:, t * D:(t + 1) * D],
                              w1vk[:, :], start=True, stop=True)
                last.then_inc(s["kv_ps"], 1)

            transpose_tokens(1, 0, MISC)
            route(0, 0)
            pe.wait_ge(s["identb_done"], 1)
            weights_back(0, 0)

            pe.wait_ge(s["w0_low"], 2 * STEPS0 // 4)
            pe.wait_ge(s["const_done"], 1)
            pe.wait_ge(s["ld_w1"], 16 * N_LD["ld_w1"])

            def down0(u):
                p, i = divmod(u, STEPS0)
                if i == 0:
                    claim(bank_y0[p], "y_sb", p + 1)
                    for n in range(3):
                        mm(P[:, bank_y0[p], :], dbp[:, n, :], WPT[0:3 * E, p % 2, :], start=(n == 0), stop=False)
                pe.wait_ge(s["high_ready"], u + 1)
                pe.wait_ge(s["low_ready"], u + 1)
                last = split_mm(bank_y0[p], (STEPS0 + i) * D, D, hidh[:, u % 3, :], hidl[:, u % 3, :],
                                False, i == STEPS0 - 1)
                last.then_inc(s["down_done"], 1)
                if i == STEPS0 - 1:
                    pe.wait_ge(s["down_done"], u + 1)
                    pe.sem_inc(s["y_ps"], 1)

            for u in range(NP * STEPS0):
                p, i = divmod(u, STEPS0)
                if i == 0:
                    pe.wait_ge(s["xl_ready"], p + 1)
                    pe.wait_ge(s["wt_sb"], p + 1)
                claim(bank_up(u), "act_ready", u + 1)
                split_mm(bank_up(u), i * D, D, XH[:, p % 2, :], XL[:, p % 2, :], True, True
                         ).then_inc(s["up_ps"], 1)
                if i % C0 == 0 and i < E * C0:
                    m = p * E + i // C0
                    claim(bank_bc(m), "bc_read", (m + 1) * C0)
                    mm(P[:, bank_bc(m), :], sel0[:, i // C0 * D:(i // C0 + 1) * D], WPT[0:3 * E, p % 2, :],
                       start=True, stop=True).then_inc(s["bc_ps"], 1)
                if u >= LAG:
                    down0(u - LAG)
                if p + 1 < NP:
                    if i == 3:
                        transpose_tokens(1, p + 1, MISC)
                    if i == 7:
                        route(0, p + 1)
                    if i == 12:
                        weights_back(0, p + 1)
                if p >= 1:
                    if i == 5:
                        tokens_back(0, p - 1)
                    if i == 9:
                        transpose_tokens(2, p - 1, MISC)
                    if i == 14:
                        project_q(p - 1)
                    if i == 15:
                        project_kv(2 * p - 2)
                    if i == 17:
                        project_kv(2 * p - 1)
            for u in range(NP * STEPS0 - LAG, NP * STEPS0):
                down0(u)

            def scores(g):
                p = g // GPP
                if g % GPP == 0:
                    pe.wait_ge(kv_in[p], 16 * 6 * HPG)
                for j in range(HPG):
                    claim(j, "e1_ready", HPG * g + j + 1)
                    for h in range(2):
                        last = mm(P[:, j, h * S:(h + 1) * S],
                                  KS[32 * j:32 * j + 3 * DH, p % 2, g % GPP, h * D:(h + 1) * D],
                                  VS[32 * j:32 * j + 3 * DH, p % 2, g % GPP, :], start=True, stop=True)
                    last.then_inc(s["s1_ps"], 1)

            def context(g):
                claim(4 + g % 2, "o1_ready", g + 1)
                pe.wait_ge(s["qs_ready"], g + 1)
                for h in range(2):
                    for j in range(HPG):
                        last = mm(P[32 * j:32 * j + 32, 4 + g % 2, 0:S],
                                  qs4[:, g % 2, j, h, :, :].rearrange("p r d -> p (r d)"),
                                  EX[:, g % 3, j, h * S:(h + 1) * S], start=(h == 0), stop=(h == 1))
                last.then_inc(s["c1_ps"], 1)

            scores(0)
            for g in range(NG):
                if g + 1 < NG:
                    scores(g + 1)
                if g >= 1:
                    context(g - 1)
                if g == 1:
                    tokens_back(0, NP - 1)
                if g == 3:
                    transpose_tokens(2, NP - 1, MISC)
                if g == 5:
                    project_q(NP - 1)
                if g == 6:
                    project_kv(2 * NP - 2)
                    project_kv(2 * NP - 1)
                if g == 9:
                    pe.wait_ge(s["ld_r1"], 16 * N_LD["ld_r1"])
                for p in range(2):
                    i = g - GPP * p
                    if i == 14:
                        transpose_tokens(3, p, MISC)
                    if i == 15:
                        route(1, p)
                    if i == 17:
                        weights_back(1, p)
            context(NG - 1)

            base = NP * STEPS0
            pe.wait_ge(s["w1_low"], 6)

            def down1(n):
                p, i = divmod(n, C1)
                u = base + n
                if i == 0:
                    claim(bank_y1, "y_sb", NP + p + 1)
                pe.wait_ge(s["high_ready"], u + 1)
                pe.wait_ge(s["low_ready"], u + 1)
                last = split_mm(bank_y1, 2 * FP + i * D, D, hidh[:, u % 3, :], hidl[:, u % 3, :],
                                i == 0, i == C1 - 1)
                last.then_inc(s["down_done"], 1)
                if i == C1 - 1:
                    pe.wait_ge(s["down_done"], u + 1)
                    pe.sem_inc(s["y_ps"], 1)

            for n in range(NP * C1):
                p, i = divmod(n, C1)
                if i == 0:
                    pe.wait_ge(s["xl_ready"], NP + p + 1)
                    pe.wait_ge(s["wt_sb"], NP + p + 1)
                claim(bank_g(n), "gact_ready", n + 1)
                split_mm(bank_g(n), i * D, D, XH[:, p % 2, :], XL[:, p % 2, :], True, True).then_inc(s["g_ps"], 1)
                claim(bank_u(n), "u_read", n + 1)
                split_mm(bank_u(n), FP + i * D, D, XH[:, p % 2, :], XL[:, p % 2, :], True, True).then_inc(s["u_ps"], 1)
                claim(bank_bc(n), "bc_read", NP * E * C0 + n + 1)
                mm(P[:, bank_bc(n), :], sel1[:, i * D:(i + 1) * D], WPT[:, p % 2, :], start=True, stop=True
                   ).then_inc(s["bc_ps"], 1)
                if n >= LAG:
                    down1(n - LAG)
                if p in (1, 2):
                    if i == 2:
                        transpose_tokens(3, p + 1, MISC)
                    if i == 4:
                        route(1, p + 1)
                    if i == 9:
                        weights_back(1, p + 1)
                if p >= 1 and i == 6:
                    tokens_back(1, p - 1)
            for n in range(NP * C1 - LAG, NP * C1):
                down1(n)
            tokens_back(1, NP - 1)


def bank_kv(n):
    return 7 if n < 2 * NP - 2 else 13 - n


bank_xt0 = [4, 5, 6, 7]
bank_ss = [0, 1, 2, 3]
bank_rn = [4, 5, 6, 7]
bank_q0 = [0, 1, 2, 3]
bank_v0 = [4, 5, 6, 7]
bank_tq = [0, 1, 2, 3]
bank_s0 = [4, 5, 6, 7, 0, 1, 2, 3]
bank_pt = [4, 5, 6, 7, 0, 1, 2, 3]
bank_c0 = [7, 0, 1, 2, 3, 4, 5, 6]
MISC = 7
MISC2 = 6
bank_y0 = [5, 6, 5, 6]
bank_y1 = 5


def bank_up(u):
    return u % 3


def bank_bc(m):
    return 3 + m % 2


def bank_g(n):
    return n % 2


def bank_u(n):
    return (2, 6)[n % 2]


_NAMED = ["L0_wmod", "L1_wmod", "L0_attn_anomaly_matrix", "L0_attn_bq", "L0_attn_bv",
          "L0_ffn_router_w", "L0_ffn_router_b", "L0_ffn_sw1", "L0_ffn_sw2", "L0_ffn_sb2",
          "L0_ffn_rw1", "L0_ffn_rw2", "L0_ffn_rb2", "L1_attn_Wq", "L1_attn_Wk", "L1_attn_Wv",
          "L1_attn_bq", "L1_attn_bk", "L1_attn_bv", "L1_ffn_w_gate", "L1_ffn_w_up",
          "L1_ffn_w_down", "L1_ffn_sw_gate", "L1_ffn_sw_up", "L1_ffn_sw_down"]


def kernel(**inputs):
    import numpy as np
    import concourse.bacc as bacc
    from concourse.bass_utils import run_bass_kernel_spmd as run

    arrays = {n: np.ascontiguousarray(inputs[n]) for n in _NAMED}

    def put(name, array):
        arrays[name] = np.ascontiguousarray(array)

    put("x", np.asarray(inputs["L0_attn_hidden_states"]).reshape(TOK, D))
    put("c0T", np.asarray(inputs["L0_c"]).T)
    put("c1T", np.asarray(inputs["L1_c"]).T)
    put("WqT0", np.asarray(inputs["L0_attn_Wq"]).T)
    put("WvT0", np.asarray(inputs["L0_attn_Wv"]).T)
    ub = np.concatenate([np.asarray(inputs["L0_ffn_rb1"]), np.asarray(inputs["L0_ffn_sb1"])[None]])
    put("ub0T", ub.reshape((E + 1) * C0, D).T)
    put("tempT", np.repeat(np.asarray(inputs["L1_attn_temperature"]).reshape(2, HEADS // 2), 2 * DH, axis=1).T)
    put("gate_wT", np.asarray(inputs["L1_ffn_gate_w"]).T)
    put("shared_gateT", np.asarray(inputs["L1_ffn_shared_gate_w"]).T)
    put("ident", np.eye(128, dtype=np.float32))
    put("iota", np.arange(E, dtype=np.float32))
    put("sel0", np.tile(np.repeat(np.eye(E, dtype=np.float32), D, axis=1), (3, 1)))
    sel1 = np.tile(np.repeat(np.eye(E + 1, dtype=np.float32), H1, axis=1), (3, 1))
    put("sel1", np.pad(sel1, ((0, 0), (0, FP - F1))))

    nc = bacc.Bacc("TRN2", target_bir_lowering=False, num_devices=1)
    aps = {n: nc.dram_tensor(f"in_{n}", v.shape, mybir.dt.float32, kind="ExternalInput").ap()
           for n, v in arrays.items()}
    out = nc.dram_tensor("out", (TOK, D), mybir.dt.float32, kind="ExternalOutput").ap()
    scratch = {"kv": nc.dram_tensor("kv_parts", (4, TOK, D), mybir.dt.float32, kind="Internal").ap(),
               "ao": nc.dram_tensor("attention_rows", (TOK, D), mybir.dt.float32, kind="Internal").ap()}
    two_block_adaln(nc, aps, out, scratch)
    r = run(nc, [{f"in_{n}": v for n, v in arrays.items()}], core_ids=[0])
    return r.results[0]["out"].reshape(B, S, D)
```

```python
from contextlib import ExitStack

import concourse.bass as bass
from concourse import mybir

D = 128
B, S = 8, 256
TOK = B * S
NT = TOK // D
TPB = S // D
NP = B // 2
TPP = NT // NP
PT = TOK // NP
E = 8
H0 = 256
C0 = H0 // D
H1 = 176
F1 = (E + 1) * H1
C1 = -(-F1 // D)
FP = C1 * D
HEADS, DH = 16, 8
HPG = 4
NG = B * HEADS // HPG
GPB = HEADS // HPG
GPP = NG // NP
GT = HPG * DH * 2
KVR = 4
LAG = 4
STEPS0 = (E + 1) * C0
EPS = 1e-5


def two_block_adaln(nc, a, out, scratch):
    fp32, fp32r = mybir.dt.float32, mybir.dt.float32r
    bf16, u32 = mybir.dt.bfloat16, mybir.dt.uint32
    ACT, ALU, AX = mybir.ActivationFunctionType, mybir.AluOpType, mybir.AxisListType

    with ExitStack() as ctx:
        def sb(name, shape, dt=fp32):
            return ctx.enter_context(nc.sbuf_tensor(name, shape, dt))

        def sem(name):
            return ctx.enter_context(nc.semaphore(name))

        X = sb("X", [128, NT, D])
        SC = sb("SC", [128, NT, D])
        AO = SC
        XT = sb("XT", [128, TOK])
        XH = sb("XH", [128, 2, PT], fp32r)
        XL = sb("XL", [128, 2, PT], fp32r)
        qT = sb("qT", [128, TOK])
        with ExitStack() as early:
            def sb_early(name, shape, dt=fp32):
                return early.enter_context(nc.sbuf_tensor(name, shape, dt))

            PR = sb_early("PR", [128, NT, S])
            PRT = sb_early("PRT", [128, B, TPB, S])
            tqT = sb_early("tqT", [128, TOK])
            V = sb_early("V", [128, NT, D])
            w0q = sb_early("w0q", [128, D]); w0v = sb_early("w0v", [128, D]); w0a = sb_early("w0a", [128, D])
            b0v = sb_early("b0v", [128, D])
            mrow0 = sb_early("mrow0", [128, B, D])
        EX = sb("EX", [128, 3, HPG, 2 * S])
        VS = sb("VS", [128, 2, GPP, S], fp32r)
        KS = sb("KS", [128, 2, GPP, S], fp32r)
        HH = tqT
        ident = sb("ident", [128, 128])
        identb = sb("identb", [128, 128], bf16)
        ones = sb("ones", [128, 128])
        iota = sb("iota", [128, E])
        yT = sb("yT", [128, 2, PT])

        tmp = sb("tmp", [128, 4, PT])
        gu = tmp[:, 0:2, :]
        hidf = tmp[:, 2:4, :]
        hidf0 = tmp
        with ExitStack() as first:
            stage0 = first.enter_context(nc.sbuf_tensor("stage0", [128, 2 * STEPS0 * D], fp32))
        with ExitStack() as between:
            EX3 = between.enter_context(nc.sbuf_tensor("EX3", [128, HPG, 2 * S], fp32))
        hidh = sb("hidh", [128, 3, PT], fp32r)
        hidl = sb("hidl", [128, 3, PT], fp32r)
        O = sb("O", [128, 2, GPB, S])

        def ex1(g, j):
            return EX[:, g % 4, j, :] if g % 4 < 3 else EX3[:, j, :]
        stage1 = tmp[:, :, :].rearrange("p r n -> p (r n)")[:, 0:FP]

        b0q = sb("b0q", [128, 1])
        rw0 = sb("rw0", [128, E]); rb0 = sb("rb0", [128, E])
        ub0 = sb("ub0", [128, E + 1, C0]); sb2 = sb("sb2", [128, 1])
        db0 = tmp[0:3 * E, 2, 0:D]; dbr = tmp[0:3 * E, 2, D:2 * D]
        dbp = sb("dbp", [3 * E, 3, D], bf16)
        w1q = sb("w1q", [128, D]); w1vk = sb("w1vk", [128, 2 * D]); b1q = sb("b1q", [128, 1])
        b1v = sb("b1v", [128, D]); b1kt = sb("b1kt", [128, 2, D])
        temp = sb("temp", [128, 2])
        rw1 = sb("rw1", [128, E + 1])
        WH = sb("WH", [128, 3 * FP], fp32r)
        WL = sb("WL", [128, 3 * FP], fp32r)
        wmod = sb("wmod", [128, 2, 6 * D])
        act_out = wmod[:, :, :].rearrange("p l n -> p (l n)").rearrange("p (r n) -> p r n", r=3)
        cT = sb("cT", [128, 2, B]); scT = sb("scT", [128, 2, B])
        sel0f = yT[0:3 * E, :, :].rearrange("p r n -> p (r n)"); sel0 = sb("sel0", [3 * E, E * D], bf16)
        sel1 = sb("sel1", [3 * (E + 1), FP], bf16)
        mrow1 = sb("mrow1", [128, B, D])
        mcol = sb("mcol", [128, 2, 6, B])
        gtmc = sb("gtmc", [128, 2, B])

        st = sb("st", [128, NT, 6]); mv = sb("mv", [128, 4, NT, 2])
        ve = sb("ve", [128, 4, NT]); rstd = sb("rstd", [128, 4, NT])
        mhalf = sb("mhalf", [128, NT]); phalf = sb("phalf", [128, NT])
        dg = tmp[:, 0:4:3, :].rearrange("p r (t d) -> p r t d", d=D); ss = sb("ss", [128, NT]); nrm = sb("nrm", [128, NT])
        rn = sb("rn", [128, NT])
        nm0 = sb("nm0", [128, NT]); nms0 = sb("nms0", [128, NT]); Z0 = sb("Z0", [128, NT])
        nz = sb("nz", [128, NT])
        ctmp = tmp[:, 1, :].rearrange("p (r t d) -> p r t d", r=2, d=D)
        RP = 2 * TPP
        lg = sb("lg", [128, RP, E + 1]); ld = sb("ld", [128, RP, E + 1]); ex = sb("ex", [128, RP, E + 1])
        nmr = sb("nmr", [128, RP]); top = sb("top", [128, RP, 8]); tix = sb("tix", [128, RP, 8], u32)
        tif = sb("tif", [128, RP, 2]); tden = sb("tden", [128, RP]); trc = sb("trc", [128, RP])
        tw = sb("tw", [128, RP, 2]); oh = sb("oh", [128, RP, 2, E])
        W = sb("W", [128, RP, E + 1]); res = sb("res", [128, RP, E + 1])
        WP = sb("WP", [128, RP, 3 * (E + 1)], bf16)
        WPT = sb("WPT", [3 * (E + 1), 2, PT], bf16)

        kvf = sb("kvf", [128, 2, 2, D])
        b1k = kvf[:, 0, 0, :]
        kvs = sb("kvs", [128, KVR, 4, D], fp32r)
        sel1f = kvs[0:3 * (E + 1), :, :, :].rearrange("p r o d -> p (r o d)")[:, 0:FP]
        nm1 = sb("nm1", [128, 4, HPG, 2]); Z1 = sb("Z1", [128, 4, HPG, 2])
        rz1 = sb("rz1", [128, 4, HPG, 2])
        qs4 = sb("qs4", [128, 2, HPG, 2, HPG, DH])

        P = ctx.enter_context(nc.psum_tensor("P", [128, 8, PT], fp32))

        names = ["ld_c", "ld_b", "ld_w0", "ld_f0", "ld_w1", "ld_r1", "ld_m1", "silu_done", "identb_done",
                 "const_done", "sel_done", "mod_ps", "mod_sb", "mod_done", "gates_ready", "gate_ps", "gate_sb",
                 "ss_ps", "ss_ready",
                 "hh_ready", "nrm_ready", "dg_ready", "rn_ps",
                 "q0_ps", "q0_sb", "v0_ps", "v0_sb", "tq_ps", "tq_sb",
                 "s0_ps", "nm0_ready", "p0_ready", "pt_ps", "pt_sb", "c0_ps", "c0_read", "x0_ready",
                 "w0_high", "w0_low", "zeroed", "stage_loaded", "w1_high", "w1_low",
                 "xh_ready", "xl_ready", "r_ps", "rd_ready", "rex_ready", "w_ready", "wt_ps", "wt_sb",
                 "up_ps", "act_ready", "bc_ps", "bc_read", "high_ready", "low_ready", "down_done",
                 "y_sb", "z_ps", "z_read", "g_ps", "u_ps", "gact_ready", "u_read",
                 "q1_ps", "q1_sb", "kv_ps",
                 "kvs_ready", "s1_ps", "nm1_ready", "e1_ready", "rz_ready", "qs_ready", "c1_ps",
                 "o1_ready", "gated", "x1_ready", "v_step", "pool_const"]
        for k in range(4):
            names += [f"ve_ready{k}", f"rstd_ready{k}", f"xn_ready{k}", f"xt_ps{k}", f"xt_sb{k}"]
        s = {n: sem(n) for n in names}
        ld_x = [sem(f"ld_x{p}") for p in range(NP)]
        kv_out = [sem(f"kv_out{r}") for r in range(KVR)]
        kv_in = [sem(f"kv_in{p}") for p in range(NP)]
        ao_out = [sem(f"ao_out{b}") for b in range(B)]
        ao_in = [sem(f"ao_in{b}") for b in range(B)]
        stored = sem("stored")
        block = ctx.enter_context(nc.Block())

        def per_partition(v, n):
            return v.rearrange("(p n) -> p n", n=n)

        def tiles(p):
            return range(TPP * p, TPP * p + TPP)

        def half(p):
            return slice(TPP * (p % 2), TPP * (p % 2) + TPP)

        def summed(n):
            return min(n, NP) * STEPS0 + max(n - NP, 0) * C1

        def cols(p):
            return slice(PT * p, PT * p + PT)

        N_LD = {"ld_c": 3, "ld_m1": 2, "ld_b": 9, "ld_w0": 7, "ld_f0": 4, "ld_w1": 6, "ld_r1": 2}

        @block.sync
        def _(sp):
            def load(dst, src, name):
                sp.dma_start(dst, src).then_inc(s[name], 16)

            for p in range(NP):
                sp.dma_start(X[:, TPP * p:TPP * p + TPP, :],
                             a["x"].rearrange("(t p) d -> p t d", p=128)[:, TPP * p:TPP * p + TPP, :]
                             ).then_inc(ld_x[p], 16)
                if p == 0:
                    load(cT[:, 0, :], a["c0T"], "ld_c")
                    load(wmod[:, 0, :], a["L0_wmod"], "ld_c")
                    load(ident[:, :], a["ident"], "ld_c")
                if p == 1:
                    load(cT[:, 1, :], a["c1T"], "ld_m1")
                    load(wmod[:, 1, :], a["L1_wmod"], "ld_m1")
            load(iota[:, :], a["iota"].partition_broadcast(128), "ld_b")
            load(sel0f[:, :], a["sel0"], "ld_b")
            load(sel1f.bitcast(fp32), a["sel1"], "ld_b")
            load(rb0[:, :], a["L0_ffn_router_b"].partition_broadcast(128), "ld_b")
            load(ub0[:, :, :], a["ub0T"].rearrange("p (e c) -> p e c", c=C0), "ld_b")
            load(sb2[:, :], per_partition(a["L0_ffn_sb2"], 1), "ld_b")
            for n in range(3):
                load(db0[E * n:E * n + E, :], a["L0_ffn_rb2"], "ld_b")
            load(w0q[:, :], a["WqT0"], "ld_w0")
            load(w0v[:, :], a["WvT0"], "ld_w0")
            load(w0a[:, :], a["L0_attn_anomaly_matrix"], "ld_w0")
            load(b0q[:, :], per_partition(a["L0_attn_bq"], 1), "ld_w0")
            load(b0v[:, :], a["L0_attn_bv"].partition_broadcast(128), "ld_w0")
            load(rw0[:, :], a["L0_ffn_router_w"], "ld_w0")
            load(b1v[:, :], a["L1_attn_bv"].partition_broadcast(128), "ld_w0")
            ups = stage0[:, 0:STEPS0 * D].rearrange("p (e h) -> p e h", e=E + 1)
            downs = stage0[:, STEPS0 * D:].rearrange("p (e c d) -> p e c d", e=E + 1, c=C0)
            load(ups[:, 0:E, :], a["L0_ffn_rw1"].rearrange("e d h -> d e h"), "ld_f0")
            load(ups[:, E, :], a["L0_ffn_sw1"], "ld_f0")
            load(downs[:, 0:E, :, :], a["L0_ffn_rw2"].rearrange("e (c p) d -> p e c d", p=128), "ld_f0")
            load(downs[:, E, :, :], a["L0_ffn_sw2"].rearrange("(c p) d -> p c d", p=128), "ld_f0")
            load(w1q[:, :], a["L1_attn_Wq"], "ld_w1")
            load(w1vk[:, 0:D], a["L1_attn_Wv"], "ld_w1")
            load(w1vk[:, D:2 * D], a["L1_attn_Wk"], "ld_w1")
            load(b1q[:, :], per_partition(a["L1_attn_bq"], 1), "ld_w1")
            load(b1k, a["L1_attn_bk"].partition_broadcast(128), "ld_w1")
            load(temp[:, :], a["tempT"], "ld_w1")
            load(rw1[:, 0:E], a["gate_wT"], "ld_r1")
            load(rw1[:, E:E + 1], a["shared_gateT"], "ld_r1")

            def load_experts_1(w):
                sp.wait_ge(s["zeroed"], w + 1)
                if w < 2:
                    routed, shared = (("L1_ffn_w_gate", "L1_ffn_sw_gate"), ("L1_ffn_w_up", "L1_ffn_sw_up"))[w]
                    sp.dma_start(stage1[:, 0:E * H1].rearrange("p (e i) -> p e i", e=E),
                                 a[routed].rearrange("e d i -> d e i")).then_inc(s["stage_loaded"], 16)
                    sp.dma_start(stage1[:, E * H1:F1], a[shared]).then_inc(s["stage_loaded"], 16)
                else:
                    n = E * H1 // D
                    down = stage1.rearrange("p (c d) -> p c d", d=D)
                    sp.dma_start(down[:, 0:n, :],
                                 a["L1_ffn_w_down"].rearrange("e i d -> (e i) d").rearrange("(c p) d -> p c d", p=128)
                                 ).then_inc(s["stage_loaded"], 16)
                    sp.dma_start(down[:, n, :], a["L1_ffn_sw_down"][0:D, :]).then_inc(s["stage_loaded"], 16)
                    sp.dma_start(down[0:H1 - D, n + 1, :], a["L1_ffn_sw_down"][D:H1, :]
                                 ).then_inc(s["stage_loaded"], 16)

            def kv_store(p):
                for t in tiles(p):
                    sp.wait_ge(s["kvs_ready"], t + 1)
                    sp.dma_start(scratch["kv"][:, t * D:(t + 1) * D, :].rearrange("o p c -> p o c"),
                                 kvs[:, t % KVR, :, :].bitcast(fp32)).then_inc(kv_out[t % KVR], 16)

            def kv_load(p, stored_pairs):
                for r in range(KVR):
                    sp.wait_ge(kv_out[r], 16 * TPP * stored_pairs // KVR)
                if p >= 2:
                    sp.wait_ge(s["s1_ps"], HPG * GPP * (p - 1))
                for dst, parts in ((VS, (0, 1, 0)), (KS, (2, 2, 3))):
                    for j in range(HPG):
                        for n, o in enumerate(parts):
                            src = scratch["kv"][o, cols(p), :].rearrange(
                                "(g j d h) c -> j d g (h c)", j=HPG, d=DH, h=2)[j]
                            sp.dma_start(dst[32 * j + DH * n:32 * j + DH * n + DH, p % 2, :, :].bitcast(fp32), src
                                         ).then_inc(kv_in[p], 16)

            def attention_out(b):
                sp.wait_ge(s["o1_ready"], GPB * (b + 1))
                for j in range(HPG):
                    dst = scratch["ao"][b * S:(b + 1) * S, :].rearrange(
                        "(g j d h) c -> j d g (h c)", j=HPG, d=DH, h=2)[j]
                    sp.dma_start(dst, O[32 * j:32 * j + DH, b % 2, :, :]).then_inc(ao_out[b], 16)
                sp.wait_ge(ao_out[b], 16 * HPG)
                sp.dma_start(AO[:, TPB * b:TPB * b + TPB, :],
                             scratch["ao"][b * S:(b + 1) * S, :].rearrange("(t p) c -> p t c", p=128)
                             ).then_inc(ao_in[b], 16)

            for p in range(2):
                kv_store(p)
                kv_load(p, p + 1)
            kv_store(2)
            load_experts_1(0)
            attention_out(0)
            kv_load(2, 3)
            load_experts_1(1)
            attention_out(1)
            kv_store(3)
            kv_load(3, NP)
            attention_out(2)
            load_experts_1(2)
            attention_out(3)
            attention_out(B - 4)
            attention_out(B - 3)
            attention_out(B - 2)
            attention_out(B - 1)
            for p in range(NP):
                sp.wait_ge(s["z_read"], NP + p + 1)
                sp.dma_start(out.rearrange("(t p) d -> p t d", p=128)[:, TPP * p:TPP * p + TPP, :],
                             X[:, TPP * p:TPP * p + TPP, :]).then_inc(stored, 16)
            sp.wait_ge(stored, 16 * NP)

        @block.gpsimd
        def _(pool):
            nc.gpsimd.memset(mhalf[:, :], -0.5).then_inc(s["pool_const"], 1)
            nc.gpsimd.memset(phalf[:, :], 0.5).then_inc(s["pool_const"], 1)
            nc.gpsimd.memset(ones[:, :], 1.0).then_inc(s["pool_const"], 1)
            pool.wait_ge(s["pool_const"], 3)

            def root(k, p):
                pool.wait_ge(s[f"ve_ready{k}"], p + 1)
                ts = slice(TPP * p, TPP * p + TPP)
                nc.gpsimd.tensor_tensor(rstd[:, k, ts], ve[:, k, ts], mhalf[:, 0:TPP], ALU.pow
                                        ).then_inc(s[f"rstd_ready{k}"], 1)

            def norm(p):
                pool.wait_ge(s["ss_ready"], p + 1)
                ts = slice(TPP * p, TPP * p + TPP)
                nc.gpsimd.tensor_tensor(nrm[:, ts], ss[:, ts], phalf[:, 0:TPP], ALU.pow
                                        ).then_inc(s["nrm_ready"], 1)

            def add_attention0(b):
                pool.wait_ge(s["c0_read"], b + 1)
                ts = slice(TPB * b, TPB * b + TPB)
                nc.gpsimd.tensor_tensor(X[:, ts, :], X[:, ts, :], ctmp[:, b % 2, :, :], ALU.add
                                        ).then_inc(s["x0_ready"], 1)

            def low_weights(n):
                pool.wait_ge(s["w0_high"], n + 1)
                c = slice(4 * D * n, 4 * D * n + 4 * D)
                nc.gpsimd.tensor_tensor(WL[:, c], stage0[:, c], WH[:, c].bitcast(fp32), ALU.subtract
                                        ).then_inc(s["w0_low"], 1)

            def low_input(l, p):
                n = NP * l + p
                pool.wait_ge(s["xh_ready"], n + 1)
                nc.gpsimd.tensor_tensor(XL[:, p % 2, :], XT[:, cols(p)], XH[:, p % 2, :].bitcast(fp32), ALU.subtract
                                        ).then_inc(s["xl_ready"], 1)

            root(0, 0)
            root(0, 1)
            root(0, 2)
            norm(0)
            root(0, 3)
            for p in range(1, NP):
                norm(p)
            for n in range(3):
                low_weights(n)
            for b in range(B):
                if b == B - 3:
                    low_input(0, 0)
                if b + 3 <= B:
                    low_weights(b + 3)
                add_attention0(b)
                if b == 2:
                    root(1, 0)
                if b == 4:
                    root(1, 1)

            def low_part(u, source):
                pool.wait_ge(s["high_ready"], u + 1)
                if u >= 3:
                    pool.wait_ge(s["down_done"], u - 2)
                nc.gpsimd.tensor_tensor(hidl[:, u % 3, :], source, hidh[:, u % 3, :].bitcast(fp32), ALU.subtract
                                        ).then_inc(s["low_ready"], 1)

            for u in range(NP * STEPS0):
                p, i = divmod(u, STEPS0)
                low_part(u, act_out[:, u % 3, :] if i >= E * C0 else hidf0[:, u % 4, :])
                if p + 1 < NP and i == 5:
                    low_input(0, p + 1)
                if p >= 1 and i == 8:
                    root(2, p - 1)
                if p + 2 < NP and i == 4:
                    root(1, p + 2)

            def clear(w):
                if w == 0:
                    pool.wait_ge(s["down_done"], summed(NP))
                    pool.wait_ge(s["low_ready"], NP * STEPS0)
                else:
                    pool.wait_ge(s["w1_low"], 4 * w)
                if w < 2:
                    nc.gpsimd.memset(stage1[:, F1:FP], 0.0).then_inc(s["zeroed"], 1)
                else:
                    nc.gpsimd.memset(stage1[:, FP - D:FP], 0.0).then_inc(s["zeroed"], 1)

            def split(w, q):
                pool.wait_ge(s["stage_loaded"], 16 * (2, 4, 7)[w])
                c = slice(q * FP // 4, (q + 1) * FP // 4)
                d = slice(w * FP + q * FP // 4, w * FP + (q + 1) * FP // 4)
                nc.gpsimd.tensor_copy(WH[:, d], stage1[:, c]).then_inc(s["w1_high"], 1)
                pool.wait_ge(s["w1_high"], 4 * w + q + 1)
                nc.gpsimd.tensor_tensor(WL[:, d], stage1[:, c], WH[:, d].bitcast(fp32), ALU.subtract
                                        ).then_inc(s["w1_low"], 1)

            def queries(g):
                pool.wait_ge(s["rz_ready"], g + 1)
                pool.wait_ge(s["q1_sb"], g // GPP + 1)
                if g >= 2:
                    pool.wait_ge(s["c1_ps"], g - 1)
                q = qT[:, GT * g:GT * g + GT].rearrange("p (j d h) -> p j d h", j=HPG, d=DH)
                for h in range(2):
                    last = nc.gpsimd.tensor_tensor(
                        qs4[:, g % 2, :, h, :, :],
                        q[:, :, :, h].unsqueeze(2).broadcast_to([128, HPG, HPG, DH]),
                        rz1[:, g % 4, :, h].unsqueeze(2).unsqueeze(3).broadcast_to([128, HPG, HPG, DH]), ALU.mult)
                last.then_inc(s["qs_ready"], 1)

            def attention_residual(b):
                ts = slice(TPB * b, TPB * b + TPB)
                pool.wait_ge(ao_in[b], 16)
                nc.gpsimd.tensor_tensor(AO[:, ts, :], AO[:, ts, :],
                                        mrow1[:, b, :].unsqueeze(1).broadcast_to([128, TPB, D]), ALU.mult
                                        ).then_inc(s["gated"], 1)
                pool.wait_ge(s["gated"], b + 1)
                nc.gpsimd.tensor_tensor(X[:, ts, :], X[:, ts, :], AO[:, ts, :], ALU.add).then_inc(s["x1_ready"], 1)

            clear(0)
            for g in range(NG):
                if g == 3:
                    root(2, NP - 1)
                if g in (15, 15 + GPP):
                    root(3, (g - 15) // GPP)
                queries(g)
                if g == 8:
                    clear(1)
                if g == 18:
                    clear(2)
                for w, quarters in enumerate(((4, 5, 6, 7), (11, 13, 15, 17), (23, 25, 26, 27))):
                    if g in quarters:
                        split(w, quarters.index(g))
                for p in range(2):
                    i = g - GPP * p
                    if i in (10, 12):
                        attention_residual(2 * p + i // 2 - 5)
                    if i == 19:
                        low_input(1, p)
            for n in range(NP * C1):
                p, i = divmod(n, C1)
                low_part(NP * STEPS0 + n, hidf[:, n % 2, :])
                if p == 0 and i in (2, 4, 6, 8):
                    attention_residual(3 + i // 2)
                if p in (1, 2) and i == 3:
                    low_input(1, p + 1)
                if p in (0, 1) and i == 8:
                    root(3, p + 2)

        @block.vector
        def _(dve):
            v = nc.vector
            step = [0]

            def link(ins):
                step[0] += 1
                ins.then_inc(s["v_step"], 1)
                dve.wait_ge(s["v_step"], step[0])

            def guard(dst, gate, tmp):
                v.tensor_scalar(tmp, gate, 0.0, 2.0, ALU.is_ge, ALU.mult)
                link(v.scalar_tensor_tensor(out=gate, in0=gate, scalar=-1.0, in1=gate, op0=ALU.mult, op1=ALU.max))
                link(v.tensor_scalar(gate, gate, 0.25, None, ALU.max))
                return v.scalar_tensor_tensor(out=dst, in0=tmp, scalar=-1.0, in1=gate,
                                              op0=ALU.add, op1=ALU.mult)

            def pair(p):
                return slice(TPP * p, TPP * p + TPP)

            def ln_stats(k, p, half=None):
                ts = {None: tiles(p), 0: tiles(p)[0:2], 1: tiles(p)[2:4]}[half]
                if k == 1:
                    dve.wait_ge(s["x0_ready"], 2 * p + (1 if half == 0 else 2))
                if k == 3:
                    dve.wait_ge(s["x1_ready"], 2 * p + (1 if half == 0 else 2))
                for t in ts:
                    last = v.bn_stats(st[:, t, :], X[:, t, :])
                link(last)
                for t in ts:
                    last = v.bn_aggr(mv[:, k, t, :], st[:, t, :])
                link(last)
                if half == 0:
                    return
                v.tensor_scalar(ve[:, k, pair(p)], mv[:, k, pair(p), 1], EPS, None, ALU.add
                                ).then_inc(s[f"ve_ready{k}"], 1)

            def ln_apply(k, p, half=None):
                dve.wait_ge(s[f"rstd_ready{k}"], p + 1)
                if k >= 1:
                    dve.wait_ge(s[f"xt_ps{k - 1}"], p + 1)
                for t in {None: tiles(p), 0: tiles(p)[0:2], 1: tiles(p)[2:4]}[half]:
                    last = v.tensor_scalar(SC[:, t, :], X[:, t, :], mv[:, k, t, 0:1],
                                           rstd[:, k, t:t + 1], ALU.subtract, ALU.mult)
                if half != 0:
                    last.then_inc(s[f"xn_ready{k}"], 1)

            def router_logits(l, p):
                n, n9, ts = NP * l + p, E + l, half(p)
                dve.wait_ge(s["r_ps"], n + 1)
                R = P[:, MISC, 0:TPP * n9].rearrange("p (t e) -> p t e", e=n9)
                if l == 0:
                    link(v.tensor_tensor(lg[:, ts, 0:E], R, rb0[:, :].unsqueeze(1).broadcast_to([128, TPP, E]), ALU.add))
                else:
                    link(v.tensor_copy(lg[:, ts, :], R))
                link(v.reduce_max(nmr[:, ts], lg[:, ts, 0:E], AX.X))
                if l == 1:
                    v.tensor_scalar(ld[:, ts, E], lg[:, ts, E], -1.0, None, ALU.mult)
                v.tensor_tensor(ld[:, ts, 0:E], lg[:, ts, 0:E],
                                nmr[:, ts].unsqueeze(2).broadcast_to([128, TPP, E]), ALU.subtract
                                ).then_inc(s["rd_ready"], 1)

            def router_weights(l, p, part):
                n, n9, ts = NP * l + p, E + l, half(p)
                if part == 0:
                    dve.wait_ge(s["rex_ready"], n + 1)
                    for t in range(ts.start, ts.stop):
                        last = v.max(top[:, t, :], ex[:, t, 0:E])
                    link(last)
                    if l == 0:
                        v.reduce_sum(tden[:, ts], ex[:, ts, 0:E], AX.X)
                    else:
                        v.tensor_scalar(res[:, ts, E], ex[:, ts, E], 1.0, None, ALU.add)
                        v.reduce_sum(tden[:, ts], top[:, ts, 0:2], AX.X)
                    for t in range(ts.start, ts.stop):
                        last = v.max_index(tix[:, t, :], top[:, t, :], ex[:, t, 0:E])
                    link(last)
                if part == 1:
                    v.tensor_copy(tif[:, ts, :], tix[:, ts, 0:2])
                    if l == 1:
                        v.reciprocal(W[:, ts, E], res[:, ts, E])
                    link(v.reciprocal(trc[:, ts], tden[:, ts]))
                    for k in range(2):
                        v.tensor_tensor(oh[:, ts, k, :], iota[:, :].unsqueeze(1).broadcast_to([128, TPP, E]),
                                        tif[:, ts, k].unsqueeze(2).broadcast_to([128, TPP, E]), ALU.is_equal)
                    link(v.tensor_tensor(tw[:, ts, :], top[:, ts, 0:2],
                                         trc[:, ts].unsqueeze(2).broadcast_to([128, TPP, 2]), ALU.mult))
                if part == 2:
                    for k in range(2):
                        last = v.tensor_tensor(oh[:, ts, k, :], oh[:, ts, k, :],
                                               tw[:, ts, k].unsqueeze(2).broadcast_to([128, TPP, E]), ALU.mult)
                    link(last)
                    link(v.tensor_tensor(W[:, ts, 0:E], oh[:, ts, 0, :], oh[:, ts, 1, :], ALU.add))
                    link(v.tensor_copy(WP[:, ts, 0:n9], W[:, ts, 0:n9]))
                if part == 3:
                    link(v.tensor_tensor(res[:, ts, 0:n9], W[:, ts, 0:n9], WP[:, ts, 0:n9], ALU.subtract))
                    link(v.tensor_copy(WP[:, ts, n9:2 * n9], res[:, ts, 0:n9]))
                    v.tensor_tensor(WP[:, ts, 2 * n9:3 * n9], res[:, ts, 0:n9], WP[:, ts, n9:2 * n9],
                                    ALU.subtract).then_inc(s["w_ready"], 1)

            def gate_experts(l, p):
                n = NP * l + p
                dve.wait_ge(s["down_done"], summed(n + 1))
                if n >= 2:
                    dve.wait_ge(s["z_ps"], n - 1)
                bank = bank_y0[p] if l == 0 else bank_y1
                for h in range(2):
                    b = 2 * p + h
                    last = v.tensor_scalar(yT[:, n % 2, h * S:(h + 1) * S], P[:, bank, h * S:(h + 1) * S],
                                           sb2[:, :] if l == 0 else 0.0, mcol[:, l, 5, b:b + 1], ALU.add, ALU.mult)
                last.then_inc(s["y_sb"], 1)

            def add_experts(l, p):
                n = NP * l + p
                dve.wait_ge(s["z_ps"], n + 1)
                v.tensor_tensor(X[:, pair(p), :], X[:, pair(p), :],
                                P[:, MISC, :].rearrange("p (t d) -> p t d", d=D), ALU.add
                                ).then_inc(s["z_read"], 1)
                dve.wait_ge(s["z_read"], n + 1)

            def kv(*ts):
                for t in ts:
                    n = t // 2
                    dve.wait_ge(s["kv_ps"], n + 1)
                    if t >= KVR:
                        dve.wait_ge(kv_out[t % KVR], 16 * (t // KVR))
                    ps = P[:, MISC, (t % 2) * 2 * D:(t % 2) * 2 * D + 2 * D]
                    v.tensor_tensor(kvf[:, t % 2, 0, :], ps[:, 0:D], b1v[:, :], ALU.add)
                    link(v.scalar_tensor_tensor(out=kvf[:, t % 2, 1, :], in0=ps[:, D:2 * D],
                                                scalar=temp[:, t % 2:t % 2 + 1], in1=b1kt[:, t % 2, :],
                                                op0=ALU.mult, op1=ALU.add))
                    link(v.tensor_copy(kvs[:, t % KVR, 0:4:2, :], kvf[:, t % 2, :, :]))
                    v.tensor_tensor(kvs[:, t % KVR, 1:4:2, :], kvf[:, t % 2, :, :],
                                    kvs[:, t % KVR, 0:4:2, :].bitcast(fp32), ALU.subtract
                                    ).then_inc(s["kvs_ready"], 1)

            def modulation(l):
                dve.wait_ge(s["mod_ps"], l + 1)
                v.tensor_copy(mcol[:, l, :, :], P[:, bank_mod[l], 0:6 * B].rearrange("p (m b) -> p m b", m=6)
                              ).then_inc(s["mod_sb"], 1)
                dve.wait_ge(s["mod_sb"], l + 1)
                for m in (1, 4):
                    last = v.tensor_scalar(mcol[:, l, m, :], mcol[:, l, m, :], 1.0, None, ALU.add)
                last.then_inc(s["mod_done"], 1)
                guard(mcol[:, l, 2:6:3, :], mcol[:, l, 2:6:3, :], gtmc[:, :, :]).then_inc(s["gates_ready"], 1)
                dve.wait_ge(s["gates_ready"], l + 1)

            def squares_sum(p):
                dve.wait_ge(s["ss_ps"], p + 1)
                v.tensor_copy(ss[:, pair(p)], P[:, bank_ss[p], 0:TPP]).then_inc(s["ss_ready"], 1)

            def norms(p):
                dve.wait_ge(s["nrm_ready"], p + 1)
                link(v.tensor_scalar(rn[:, pair(p)], nrm[:, pair(p)], 1e-9, None, ALU.add))
                link(v.reciprocal(rn[:, pair(p)], rn[:, pair(p)]))
                if p >= 2:
                    dve.wait_ge(s["rn_ps"], p - 1)
                v.tensor_tensor(dg[:, p % 2, :, :], ident[:, :].unsqueeze(1).broadcast_to([128, TPP, D]),
                                rn[:, pair(p)].unsqueeze(2).broadcast_to([128, TPP, D]), ALU.mult
                                ).then_inc(s["dg_ready"], 1)

            def unit_input(p):
                dve.wait_ge(s["rn_ps"], p + 1)
                v.tensor_tensor(XT[:, cols(p)], XT[:, cols(p)], P[:, bank_rn[p], :], ALU.mult
                                ).then_inc(s["xt_sb0"], 1)

            def values(p):
                dve.wait_ge(s["v0_ps"], p + 1)
                v.tensor_tensor(V[:, pair(p), :],
                                P[:, bank_v0[p], :].rearrange("p (t d) -> p t d", d=D),
                                b0v[:, :].unsqueeze(1).broadcast_to([128, TPP, D]), ALU.add).then_inc(s["v0_sb"], 1)

            def maxima0(b):
                dve.wait_ge(s["s0_ps"], b + 1)
                ts = slice(TPB * b, TPB * b + TPB)
                link(v.reduce_max(nm0[:, ts], P[:, bank_s0(b), :].rearrange("p (i t) -> p i t", i=TPB), AX.X))
                v.tensor_scalar(nms0[:, ts], nm0[:, ts], -(D ** -0.5), None, ALU.mult).then_inc(s["nm0_ready"], 1)

            def context0(b):
                dve.wait_ge(s["c0_ps"], b + 1)
                ts = slice(TPB * b, TPB * b + TPB)
                link(v.reciprocal(nz[:, ts], Z0[:, ts]))
                link(v.tensor_tensor(nz[:, ts], nz[:, ts], nrm[:, ts], ALU.mult))
                dve.wait_ge(s["gate_sb"], 2)
                if b >= 2:
                    dve.wait_ge(s["x0_ready"], b - 1)
                for i in range(TPB):
                    t = TPB * b + i
                    last = v.scalar_tensor_tensor(out=ctmp[:, b % 2, i, :], in0=P[:, bank_c0(b), i * D:(i + 1) * D],
                                                  scalar=nz[:, t:t + 1], in1=mrow0[:, b, :],
                                                  op0=ALU.mult, op1=ALU.mult)
                last.then_inc(s["c0_read"], 1)

            def statistics0(p):
                dve.wait_ge(ld_x[p], 16)
                ln_stats(0, p)

            statistics0(0)
            ln_apply(0, 0)
            statistics0(1)
            modulation(0)
            ln_apply(0, 1)
            statistics0(2)
            squares_sum(0)
            ln_apply(0, 2)
            norms(0)
            statistics0(3)
            squares_sum(1)
            ln_apply(0, 3)
            unit_input(0)
            norms(1)
            squares_sum(2)
            dve.wait_ge(s["ld_w0"], 16 * N_LD["ld_w0"])
            values(0)
            unit_input(1)
            squares_sum(3)
            norms(2)
            norms(3)
            values(1)
            for b in range(B + 4):
                if b < B:
                    maxima0(b)
                if b == 0:
                    unit_input(2)
                    modulation(1)
                if b == 2:
                    unit_input(3)
                if b in (3, 4):
                    values(b - 1)
                if b >= 4:
                    context0(b - 4)
                if b == 6:
                    ln_stats(1, 0)
                if b == 7:
                    ln_apply(1, 0)
                if b == 3:
                    dve.wait_ge(s["ld_b"], 16 * N_LD["ld_b"])
                    link(v.tensor_copy(dbp[:, 0, :], db0[:, :]))
                    link(v.tensor_tensor(dbr[:, :], db0[:, :], dbp[:, 0, :], ALU.subtract))
                    link(v.tensor_copy(dbp[:, 1, :], dbr[:, :]))
                    v.tensor_tensor(dbp[:, 2, :], dbr[:, :], dbp[:, 1, :], ALU.subtract).then_inc(s["const_done"], 1)
                if b == 8:
                    ln_stats(1, 1)
                if b == 9:
                    router_logits(0, 0)
                if b >= 10:
                    router_weights(0, 0, 2 * b - 20)
                    router_weights(0, 0, 2 * b - 19)
            ln_apply(1, 1)

            dve.wait_ge(s["x0_ready"], B)
            for u in range(NP * STEPS0):
                p, i = divmod(u, STEPS0)
                if i < E * C0:
                    dve.wait_ge(s["bc_ps"], p * E + i // C0 + 1)
                    dve.wait_ge(s["act_ready"], u + 1)
                    if u >= 4:
                        dve.wait_ge(s["low_ready"], u - 3)
                    v.tensor_tensor(hidf0[:, u % 4, :], act_out[:, u % 3, :], P[:, bank_bc(p * E + i // C0), :],
                                    ALU.mult).then_inc(s["bc_read"], 1)
                if p + 1 < NP:
                    if i == 7:
                        router_logits(0, p + 1)
                    if i in (9, 12, 13, 14):
                        router_weights(0, p + 1, (9, 12, 13, 14).index(i))
                if p + 2 < NP:
                    if i in (0, 4):
                        ln_stats(1, p + 2, i // 4)
                    if i in (15, 16):
                        ln_apply(1, p + 2, i - 15)
                if p >= 1:
                    if i == 3:
                        gate_experts(0, p - 1)
                    if i == 5:
                        add_experts(0, p - 1)
                    if i in (6, 8):
                        ln_stats(2, p - 1, i // 2 - 3)
                    if i in (10, 11):
                        ln_apply(2, p - 1, i - 10)
                    if i == 17 and p == 1:
                        dve.wait_ge(s["ld_w1"], 16 * N_LD["ld_w1"])
                        for k in range(2):
                            last = v.tensor_scalar(b1kt[:, k, :], b1k, temp[:, k:k + 1], None, ALU.mult)
                        link(last)
                    if i == 17:
                        kv(TPP * (p - 1), TPP * (p - 1) + 1)
                if p >= 2 and i in (1, 2):
                    kv(TPP * (p - 2) + 1 + i)
            def maxima(g, h):
                bank = bank_s1(g, 2 * h)
                dve.wait_ge(s["s1_ps"], HPG * g + 2 * h + 2)
                v.tensor_reduce(nm1[:, g % 4, 2 * h:2 * h + 2, :],
                                P[:, bank:bank + 2, :].rearrange("p j (h s) -> p (j h) s", h=2),
                                AX.X, ALU.max, negate=True).then_inc(s["nm1_ready"], 1)

            def denominators(g):
                dve.wait_ge(s["e1_ready"], HPG * (g + 1))
                if g >= 4:
                    dve.wait_ge(s["qs_ready"], g - 3)
                v.reciprocal(rz1[:, g % 4, :, :], Z1[:, g % 4, :, :]).then_inc(s["rz_ready"], 1)

            def outputs(g):
                b = g // GPB
                dve.wait_ge(s["c1_ps"], g + 1)
                if b >= 2 and g % GPB == 0:
                    dve.wait_ge(ao_out[b - 2], 16 * HPG)
                v.tensor_copy(O[:, b % 2, g % GPB, :], P[:, BANK_C1, 0:S]).then_inc(s["o1_ready"], 1)

            maxima(0, 0)
            maxima(0, 1)
            gate_experts(0, NP - 1)
            for g in range(NG):
                if g >= 3:
                    outputs(g - 3)
                if g + 1 < NG:
                    maxima(g + 1, 0)
                if g >= 1:
                    denominators(g - 1)
                if g < 2:
                    kv(2 * TPP + 2 + g)
                if g == 2:
                    add_experts(0, NP - 1)
                if g in (2, 3):
                    ln_stats(2, NP - 1, g - 2)
                if g == 4:
                    ln_apply(2, NP - 1)
                if g in (10, 11, 13, 14):
                    kv((NP - 1) * TPP + (10, 11, 13, 14).index(g))
                for p in range(2):
                    i = g - GPP * p
                    if i == 15:
                        ln_stats(3, p)
                    if i == 16:
                        ln_apply(3, p)
                    if i == 21:
                        router_logits(1, p)
                    if 22 <= i < 26:
                        router_weights(1, p, i - 22)
                if g + 1 < NG:
                    maxima(g + 1, 1)
            denominators(NG - 1)
            outputs(NG - 3)
            router_weights(1, 1, 2)
            outputs(NG - 2)
            router_weights(1, 1, 3)
            outputs(NG - 1)

            base = NP * STEPS0
            for n in range(NP * C1):
                p, i = divmod(n, C1)
                dve.wait_ge(s["u_ps"], n + 1)
                dve.wait_ge(s["gact_ready"], n + 1)
                v.tensor_tensor(gu[:, n % 2, :], act_out[:, n % 3, :], P[:, bank_u(n), :], ALU.mult
                                ).then_inc(s["u_read"], 1)
                dve.wait_ge(s["u_read"], n + 1)
                dve.wait_ge(s["bc_ps"], NP * E + n + 1)
                if n >= 2:
                    dve.wait_ge(s["low_ready"], base + n - 1)
                v.tensor_tensor(hidf[:, n % 2, :], gu[:, n % 2, :], P[:, bank_bc(n), :],
                                ALU.mult).then_inc(s["bc_read"], 1)
                if p in (1, 2):
                    if i in (0, 1):
                        ln_apply(3, p + 1, i)
                    if i == 4:
                        router_logits(1, p + 1)
                    if i in (6, 8, 9, 10):
                        router_weights(1, p + 1, (6, 8, 9, 10).index(i))
                if p in (0, 1) and i in (5, 7):
                    ln_stats(3, p + 2, i // 2 - 2)
                if p >= 1:
                    if i == 3:
                        gate_experts(1, p - 1)
                    if i == 7:
                        add_experts(1, p - 1)
            gate_experts(1, NP - 1)
            add_experts(1, NP - 1)

        @block.scalar
        def _(act):
            sc = nc.scalar
            act.wait_ge(s["ld_c"], 16 * N_LD["ld_c"])
            sc.activation(scT[:, 0, :], cT[:, 0, :], ACT.Silu).then_inc(s["silu_done"], 1)
            act.wait_ge(s["ld_m1"], 16 * N_LD["ld_m1"])
            sc.activation(scT[:, 1, :], cT[:, 1, :], ACT.Silu).then_inc(s["silu_done"], 1)
            sc.activation(identb[:, :], ident[:, :], ACT.Copy).then_inc(s["identb_done"], 1)

            def modulate0(p):
                act.wait_ge(s["xt_ps0"], p + 1)
                act.wait_ge(s["mod_done"], 1)
                for h in range(2):
                    b = 2 * p + h
                    last = sc.activation(XT[:, b * S:(b + 1) * S], P[:, bank_xt0[p], h * S:(h + 1) * S],
                                         ACT.Identity, bias=mcol[:, 0, 0, b:b + 1], scale=mcol[:, 0, 1, b:b + 1])
                last.then_inc(s["hh_ready"], 1)
                act.wait_ge(s["hh_ready"], 2 * p + 1)
                sc.activation(HH[:, cols(p)], XT[:, cols(p)], ACT.Square).then_inc(s["hh_ready"], 1)

            def high_weights(n):
                c = slice(4 * D * n, 4 * D * n + 4 * D)
                sc.activation(WH[:, c], stage0[:, c], ACT.Copy).then_inc(s["w0_high"], 1)

            def queries0(p):
                act.wait_ge(s["q0_ps"], p + 1)
                sc.activation(qT[:, cols(p)], P[:, bank_q0[p], :], ACT.Identity, bias=b0q[:, :]).then_inc(s["q0_sb"], 1)

            def anomaly_queries(p):
                act.wait_ge(s["tq_ps"], p + 1)
                sc.activation(tqT[:, cols(p)], P[:, bank_tq[p], :], ACT.Copy).then_inc(s["tq_sb"], 1)

            def gate_rows(h):
                act.wait_ge(s["gate_ps"], h + 1)
                sc.activation((mrow0, mrow1)[h // 2][:, 4 * (h % 2):4 * (h % 2) + 4, :],
                              P[:, bank_gate[h], :].rearrange("p (b d) -> p b d", d=D), ACT.Copy
                              ).then_inc(s["gate_sb"], 1)

            def modulate(k, p):
                l, m = ((0, 3), (1, 0), (1, 3))[k - 1]
                act.wait_ge(s[f"xt_ps{k}"], p + 1)
                for h in range(2):
                    b = 2 * p + h
                    last = sc.activation(XT[:, b * S:(b + 1) * S], P[:, MISC, h * S:(h + 1) * S], ACT.Identity,
                                         bias=mcol[:, l, m, b:b + 1], scale=mcol[:, l, m + 1, b:b + 1])
                last.then_inc(s[f"xt_sb{k}"], 1)

            def high_input(l, p):
                act.wait_ge(s[f"xt_sb{(1, 3)[l]}"], p + 1)
                if p >= 2:
                    act.wait_ge(s[("up_ps", "u_ps")[l]], (p - 1) * (STEPS0, C1)[l])
                sc.activation(XH[:, p % 2, :], XT[:, cols(p)], ACT.Copy).then_inc(s["xh_ready"], 1)

            def router_exp(l, p):
                act.wait_ge(s["rd_ready"], NP * l + p + 1)
                sc.activation(ex[:, half(p), 0:E + l], ld[:, half(p), 0:E + l], ACT.Exp).then_inc(s["rex_ready"], 1)

            def weights_out(l, p):
                n, r = NP * l + p, 3 * (E + l)
                act.wait_ge(s["wt_ps"], n + 1)
                sc.activation(WPT[0:r, p % 2, :], P[0:r, MISC, 0:PT // 2].bitcast(bf16), ACT.Copy
                              ).then_inc(s["wt_sb"], 1)

            for p in range(NP):
                modulate0(p)
                if p == 2:
                    act.wait_ge(s["ld_b"], 16 * N_LD["ld_b"])
                    sc.activation(sel0[:, :], sel0f, ACT.Copy).then_inc(s["sel_done"], 1)
                    sc.activation(sel1[:, :], sel1f.bitcast(fp32), ACT.Copy).then_inc(s["sel_done"], 1)
            act.wait_ge(s["ld_w0"], 16 * N_LD["ld_w0"])
            queries0(0)
            act.wait_ge(s["ld_f0"], 16 * N_LD["ld_f0"])
            high_weights(0)
            high_weights(1)
            anomaly_queries(0)
            queries0(1)
            high_weights(2)
            for b in range(B + 3):
                if b == 1:
                    anomaly_queries(1)
                if b < B:
                    act.wait_ge(s["nm0_ready"], b + 1)
                    for i in range(TPB):
                        t = TPB * b + i
                        sc.activation(PR[:, t, :], P[:, bank_s0(b), i * S:(i + 1) * S], ACT.Exp,
                                      bias=nms0[:, t:t + 1], scale=D ** -0.5,
                                      accum_out=Z0[:, t:t + 1]).then_inc(s["p0_ready"], 1)
                if b in (1, 3):
                    queries0(2 + b // 2)
                if b in (0, 1):
                    gate_rows(b)
                if b == 6:
                    gate_rows(2)
                    gate_rows(3)
                if b in (2, 4):
                    anomaly_queries(1 + b // 2)
                if b + 3 <= B:
                    high_weights(b + 3)
                if 2 <= b < B + 2:
                    act.wait_ge(s["pt_ps"], b - 1)
                    sc.activation(PRT[:, b - 2, :, :], P[:, bank_pt(b - 2), :].rearrange("p (j q) -> p j q", j=TPB),
                                  ACT.Copy).then_inc(s["pt_sb"], 1)
                if b == 8:
                    modulate(1, 0)
                    high_input(0, 0)
                if b == 10:
                    router_exp(0, 0)

            def queries_out(p):
                act.wait_ge(s["q1_ps"], p + 1)
                sc.activation(qT[:, cols(p)], P[:, MISC, :], ACT.Identity, bias=b1q[:, :]).then_inc(s["q1_sb"], 1)

            def high_part(u, source):
                if u >= 3:
                    act.wait_ge(s["down_done"], u - 2)
                sc.activation(hidh[:, u % 3, :], source, ACT.Copy).then_inc(s["high_ready"], 1)

            act.wait_ge(s["ld_b"], 16 * N_LD["ld_b"])
            act.wait_ge(s["ld_w1"], 16 * N_LD["ld_w1"])

            def high0(u):
                p, i = divmod(u, STEPS0)
                if i < E * C0:
                    act.wait_ge(s["bc_read"], p * E * C0 + i + 1)
                    high_part(u, hidf0[:, u % 4, :])
                else:
                    act.wait_ge(s["act_ready"], u + 1)
                    high_part(u, act_out[:, u % 3, :])

            for u in range(NP * STEPS0):
                p, i = divmod(u, STEPS0)
                act.wait_ge(s["up_ps"], u + 1)
                if u >= 3:
                    pp, ii = divmod(u - 3, STEPS0)
                    if ii < E * C0:
                        act.wait_ge(s["bc_read"], pp * E * C0 + ii + 1)
                    else:
                        act.wait_ge(s["low_ready"], u - 2)
                sc.activation(act_out[:, u % 3, :], P[:, bank_up(u), :], ACT.Gelu,
                              bias=ub0[:, i // C0, i % C0:i % C0 + 1]).then_inc(s["act_ready"], 1)
                if u == 1:
                    weights_out(0, 0)
                if u >= 1:
                    high0(u - 1)
                if p + 1 < NP:
                    if i == 4:
                        modulate(1, p + 1)
                    if i == 5:
                        high_input(0, p + 1)
                    if i == 8:
                        router_exp(0, p + 1)
                    if i == 16:
                        weights_out(0, p + 1)
                if p >= 1:
                    if i == 13:
                        modulate(2, p - 1)
                    if i == 14:
                        queries_out(p - 1)
            high0(NP * STEPS0 - 1)

            for g in range(NG):
                for j in range(HPG):
                    act.wait_ge(s["nm1_ready"], 2 * g + j // 2 + 1)
                    if g >= 4 and j == 0:
                        act.wait_ge(s["c1_ps"], g - 3)
                    for h in range(2):
                        last = sc.activation(ex1(g, j)[:, h * S:(h + 1) * S],
                                             P[:, bank_s1(g, j), h * S:(h + 1) * S],
                                             ACT.Exp, bias=nm1[:, g % 4, j, h:h + 1], accum_out=Z1[:, g % 4, j, h:h + 1])
                    last.then_inc(s["e1_ready"], 1)
                    if j == HPG - 1:
                        if g == 5:
                            modulate(2, NP - 1)
                        if g == 7:
                            queries_out(NP - 1)
                        if g in (18, 18 + GPP):
                            modulate(3, (g - 18) // GPP)
                            high_input(1, (g - 18) // GPP)
                for p in range(2):
                    i = g - GPP * p
                    if i == 21:
                        router_exp(1, p)
                    if i == 27:
                        weights_out(1, p)

            base = NP * STEPS0

            def high1(n):
                act.wait_ge(s["bc_read"], NP * E * C0 + n + 1)
                high_part(base + n, hidf[:, n % 2, :])

            for n in range(NP * C1):
                p, i = divmod(n, C1)
                act.wait_ge(s["g_ps"], n + 1)
                if n >= 3:
                    act.wait_ge(s["u_read"], n - 2)
                else:
                    act.wait_ge(s["low_ready"], base)
                sc.activation(act_out[:, n % 3, :], P[:, bank_g(n), :], ACT.Silu).then_inc(s["gact_ready"], 1)
                if n >= 1:
                    high1(n - 1)
                if n == 2:
                    weights_out(1, 1)
                if p in (1, 2):
                    if i == 2:
                        modulate(3, p + 1)
                    if i == 3:
                        high_input(1, p + 1)
                    if i == 5:
                        router_exp(1, p + 1)
                    if i == 11:
                        weights_out(1, p + 1)
            high1(NP * C1 - 1)

        @block.tensor
        def _(pe):
            mm = nc.tensor.matmul
            reader = {}

            def claim(bank, who, value):
                if bank in reader:
                    pe.wait_ge(*reader[bank])
                reader[bank] = (s[who], value)

            def split_mm(bank, w, m, xh, xl, start, stop):
                mm(P[:, bank, :], WH[:, w:w + m], xh, start=start, stop=False)
                mm(P[:, bank, :], WL[:, w:w + m], xh, start=False, stop=False)
                return mm(P[:, bank, :], WH[:, w:w + m], xl, start=False, stop=stop)

            def modulation(l):
                pe.wait_ge(s["silu_done"], l + 1)
                claim(bank_mod[l], "mod_sb", l + 1)
                for m in range(6):
                    last = mm(P[:, bank_mod[l], m * B:(m + 1) * B], wmod[:, l, m * D:(m + 1) * D],
                              scT[:, l, :], start=True, stop=True)
                last.then_inc(s["mod_ps"], 1)

            def transpose_tokens(k, p, bank):
                pe.wait_ge(s[f"xn_ready{k}"], p + 1)
                claim(bank, f"xt_sb{k}", p + 1)
                for i, t in enumerate(tiles(p)):
                    last = nc.tensor.transpose(P[:, bank, i * D:(i + 1) * D], SC[:, t, :], ident[:, :])
                last.then_inc(s[f"xt_ps{k}"], 1)

            def transpose0(p):
                transpose_tokens(0, p, bank_xt0[p])
                reader[bank_xt0[p]] = (s["hh_ready"], 2 * p + 1)

            def gate_rows(h):
                pe.wait_ge(s["gates_ready"], h // 2 + 1)
                claim(bank_gate[h], "gate_sb", h + 1)
                for i in range(4):
                    last = mm(P[:, bank_gate[h], i * D:(i + 1) * D],
                              mcol[:, h // 2, 2, 4 * (h % 2) + i:4 * (h % 2) + i + 1].broadcast_to([128, 128]),
                              ident[:, :], start=True, stop=True)
                last.then_inc(s["gate_ps"], 1)

            def squares_sum(p):
                pe.wait_ge(s["pool_const"], 3)
                pe.wait_ge(s["hh_ready"], 2 * p + 2)
                claim(bank_ss[p], "ss_ready", p + 1)
                for i, t in enumerate(tiles(p)):
                    last = mm(P[:, bank_ss[p], i:i + 1], HH[:, t * D:(t + 1) * D], ones[:, 0:1], start=True, stop=True)
                last.then_inc(s["ss_ps"], 1)

            def norms(p):
                pe.wait_ge(s["dg_ready"], p + 1)
                claim(bank_rn[p], "xt_sb0", p + 1)
                mm(P[:, bank_rn[p], :], ones[:, :], dg[:, p % 2, :, :].rearrange("p t d -> p (t d)"),
                   start=True, stop=True).then_inc(s["rn_ps"], 1)

            def project_q0(p):
                pe.wait_ge(s["xt_sb0"], p + 1)
                claim(bank_q0[p], "q0_sb", p + 1)
                mm(P[:, bank_q0[p], :], w0q[:, :], XT[:, cols(p)], start=True, stop=True).then_inc(s["q0_ps"], 1)

            def project_v0(p):
                claim(bank_v0[p], "v0_sb", p + 1)
                for i, t in enumerate(tiles(p)):
                    last = mm(P[:, bank_v0[p], i * D:(i + 1) * D], XT[:, t * D:(t + 1) * D], w0v[:, :],
                              start=True, stop=True)
                last.then_inc(s["v0_ps"], 1)

            def anomaly_queries(p):
                pe.wait_ge(s["q0_sb"], p + 1)
                claim(bank_tq[p], "tq_sb", p + 1)
                mm(P[:, bank_tq[p], :], w0a[:, :], qT[:, cols(p)], start=True, stop=True).then_inc(s["tq_ps"], 1)

            def scores0(b):
                pe.wait_ge(s["tq_sb"], b // 2 + 1)
                claim(bank_s0(b), "p0_ready", TPB * (b + 1))
                for i in range(TPB):
                    t = TPB * b + i
                    last = mm(P[:, bank_s0(b), i * S:(i + 1) * S], qT[:, t * D:(t + 1) * D],
                              tqT[:, b * S:(b + 1) * S], start=True, stop=True)
                last.then_inc(s["s0_ps"], 1)

            def transpose_numerators(b):
                pe.wait_ge(s["p0_ready"], TPB * (b + 1))
                claim(bank_pt(b), "pt_sb", b + 1)
                for j in range(TPB):
                    for i in range(TPB):
                        last = nc.tensor.transpose(P[:, bank_pt(b), j * S + i * D:j * S + (i + 1) * D],
                                                   PR[:, TPB * b + i, j * D:(j + 1) * D], ident[:, :])
                last.then_inc(s["pt_ps"], 1)

            def context0(b):
                pe.wait_ge(s["pt_sb"], b + 1)
                pe.wait_ge(s["v0_sb"], b // 2 + 1)
                claim(bank_c0(b), "c0_read", b + 1)
                for i in range(TPB):
                    for j in range(TPB):
                        last = mm(P[:, bank_c0(b), i * D:(i + 1) * D], PRT[:, b, j, i * D:(i + 1) * D],
                                  V[:, TPB * b + j, :], start=(j == 0), stop=(j == TPB - 1))
                last.then_inc(s["c0_ps"], 1)

            def route(l, p):
                n, n9, k = NP * l + p, E + l, (1, 3)[l]
                pe.wait_ge(s[f"xt_sb{k}"], p + 1)
                claim(MISC, "rd_ready", n + 1)
                for i, t in enumerate(tiles(p)):
                    last = mm(P[:, MISC, i * n9:(i + 1) * n9], XT[:, t * D:(t + 1) * D],
                              (rw0, rw1)[l][:, :], start=True, stop=True)
                last.then_inc(s["r_ps"], 1)

            def weights_back(l, p):
                n, n9 = NP * l + p, E + l
                pe.wait_ge(s["w_ready"], n + 1)
                claim(MISC, "wt_sb", n + 1)
                for i, t in enumerate(tiles(p)):
                    last = nc.tensor.transpose(P[0:3 * n9, MISC, 0:PT // 2].bitcast(bf16)[:, i * D:(i + 1) * D],
                                               WP[:, TPP * (p % 2) + i, 0:3 * n9], identb[:, :])
                last.then_inc(s["wt_ps"], 1)

            def tokens_back(l, p):
                n = NP * l + p
                pe.wait_ge(s["y_sb"], n + 1)
                claim(MISC, "z_read", n + 1)
                for i in range(TPP):
                    last = nc.tensor.transpose(P[:, MISC, i * D:(i + 1) * D], yT[:, n % 2, i * D:(i + 1) * D],
                                               ident[:, :])
                last.then_inc(s["z_ps"], 1)

            def project_q(p):
                pe.wait_ge(s["xt_sb2"], p + 1)
                claim(MISC, "q1_sb", p + 1)
                mm(P[:, MISC, :], w1q[:, :], XT[:, cols(p)], start=True, stop=True).then_inc(s["q1_ps"], 1)

            def project_kv(n):
                claim(MISC, "kvs_ready", 2 * n + 2)
                for i in range(2):
                    t = 2 * n + i
                    last = mm(P[:, MISC, i * 2 * D:(i + 1) * 2 * D], XT[:, t * D:(t + 1) * D],
                              w1vk[:, :], start=True, stop=True)
                last.then_inc(s["kv_ps"], 1)

            modulation(0)
            transpose0(0)
            transpose0(1)
            squares_sum(0)
            transpose0(2)
            norms(0)
            squares_sum(1)
            transpose0(3)
            pe.wait_ge(s["ld_w0"], 16 * N_LD["ld_w0"])
            project_q0(0)
            squares_sum(2)
            project_v0(0)
            norms(1)
            anomaly_queries(0)
            squares_sum(3)
            project_q0(1)
            project_v0(1)
            modulation(1)
            for b in range(B + 3):
                if b < B:
                    scores0(b)
                if b == 0:
                    anomaly_queries(1)
                    norms(2)
                if b == 1:
                    project_q0(2)
                    norms(3)
                if b in (0, 1):
                    gate_rows(b)
                if b == 6:
                    gate_rows(2)
                    gate_rows(3)
                if b == 2:
                    project_v0(2)
                if b == 3:
                    project_q0(3)
                if 2 <= b < B + 2:
                    transpose_numerators(b - 2)
                if b in (2, 4):
                    anomaly_queries(1 + b // 2)
                if b == 3:
                    project_v0(3)
                if b >= 3:
                    context0(b - 3)
                if b == 8:
                    transpose_tokens(1, 0, MISC)
                if b == 9:
                    route(0, 0)
            pe.wait_ge(s["identb_done"], 1)

            pe.wait_ge(s["w0_low"], -(-STEPS0 // 4))
            pe.wait_ge(s["const_done"], 1)
            pe.wait_ge(s["sel_done"], 2)
            pe.wait_ge(s["ld_w1"], 16 * N_LD["ld_w1"])

            def down0(u):
                p, i = divmod(u, STEPS0)
                if u == 0:
                    pe.wait_ge(s["w0_low"], 2 * STEPS0 // 4)
                if i == 0:
                    claim(bank_y0[p], "y_sb", p + 1)
                    for n in range(3):
                        mm(P[:, bank_y0[p], :], dbp[:, n, :], WPT[0:3 * E, p % 2, :], start=(n == 0), stop=False)
                pe.wait_ge(s["high_ready"], u + 1)
                pe.wait_ge(s["low_ready"], u + 1)
                last = split_mm(bank_y0[p], (STEPS0 + i) * D, D, hidh[:, u % 3, :], hidl[:, u % 3, :],
                                False, i == STEPS0 - 1)
                last.then_inc(s["down_done"], 1)

            for u in range(NP * STEPS0):
                p, i = divmod(u, STEPS0)
                if i == 0:
                    pe.wait_ge(s["xl_ready"], p + 1)
                claim(bank_up(u), "act_ready", u + 1)
                split_mm(bank_up(u), i * D, D, XH[:, p % 2, :], XL[:, p % 2, :], True, True
                         ).then_inc(s["up_ps"], 1)
                if u == 1:
                    weights_back(0, 0)
                if i == 0 and p >= 1 or u == 2:
                    pe.wait_ge(s["wt_sb"], p + 1)
                for e in [0, 1] if u == 2 else [i // C0] if i % C0 == 0 and 0 < u and i < E * C0 else []:
                    m = p * E + e
                    claim(bank_bc(m), "bc_read", (m + 1) * C0)
                    mm(P[:, bank_bc(m), :], sel0[:, e * D:(e + 1) * D], WPT[0:3 * E, p % 2, :],
                       start=True, stop=True).then_inc(s["bc_ps"], 1)
                if u >= LAG:
                    down0(u - LAG)
                if p + 1 < NP:
                    if i == 4:
                        transpose_tokens(1, p + 1, MISC)
                    if i == 7:
                        route(0, p + 1)
                    if i == 16:
                        weights_back(0, p + 1)
                if p >= 1:
                    if i == 5:
                        tokens_back(0, p - 1)
                    if i == 13:
                        transpose_tokens(2, p - 1, MISC)
                    if i == 14:
                        project_q(p - 1)
                    if i == 17:
                        project_kv(2 * p - 2)
                if p >= 2 and i == 1:
                    project_kv(2 * p - 3)
            def scores(g, half):
                p = g // GPP
                if g % GPP == 0:
                    pe.wait_ge(kv_in[p], 16 * 6 * HPG)
                for j in (2 * half, 2 * half + 1):
                    claim(bank_s1(g, j), "e1_ready", HPG * g + j + 1)
                    for h in range(2):
                        last = mm(P[:, bank_s1(g, j), h * S:(h + 1) * S],
                                  KS[32 * j:32 * j + 3 * DH, p % 2, g % GPP, h * D:(h + 1) * D],
                                  VS[32 * j:32 * j + 3 * DH, p % 2, g % GPP, :], start=True, stop=True)
                    last.then_inc(s["s1_ps"], 1)

            def context(g, h):
                if h == 0:
                    claim(BANK_C1, "o1_ready", g + 1)
                    pe.wait_ge(s["qs_ready"], g + 1)
                for j in range(HPG):
                    last = mm(P[32 * j:32 * j + 32, BANK_C1, 0:S],
                              qs4[:, g % 2, j, h, :, :].rearrange("p r d -> p (r d)"),
                              ex1(g, j)[:, h * S:(h + 1) * S], start=(h == 0), stop=(h == 1))
                if h == 1:
                    last.then_inc(s["c1_ps"], 1)

            scores(0, 0)
            down0(NP * STEPS0 - 4)
            down0(NP * STEPS0 - 3)
            scores(0, 1)
            down0(NP * STEPS0 - 2)
            scores(1, 0)
            down0(NP * STEPS0 - 1)
            project_kv(2 * NP - 3)
            for g in range(NG):
                for half in range(2):
                    if g + 1 < NG and (g, half) != (0, 0):
                        scores(g + 1, half)
                    if g >= 2:
                        context(g - 2, half)
                if g == 1:
                    tokens_back(0, NP - 1)
                if g == 4:
                    transpose_tokens(2, NP - 1, MISC)
                if g == 6:
                    project_q(NP - 1)
                if g in (8, 11):
                    project_kv(2 * NP - 2 + g // 11)
                if g == 9:
                    pe.wait_ge(s["ld_r1"], 16 * N_LD["ld_r1"])
                for p in range(2):
                    i = g - GPP * p
                    if i == 17:
                        transpose_tokens(3, p, MISC)
                    if i == 19:
                        route(1, p)
                    if i == 26:
                        weights_back(1, p)
            for half in range(2):
                context(NG - 2, half)
            pe.wait_ge(s["w1_low"], 12)

            def gate_up(n):
                p, i = divmod(n, C1)
                if i == 0:
                    pe.wait_ge(s["xl_ready"], NP + p + 1)
                claim(bank_u(n), "u_read", n + 1)
                split_mm(bank_u(n), FP + i * D, D, XH[:, p % 2, :], XL[:, p % 2, :], True, True).then_inc(s["u_ps"], 1)
                claim(bank_g(n), "gact_ready", n + 1)
                split_mm(bank_g(n), i * D, D, XH[:, p % 2, :], XL[:, p % 2, :], True, True).then_inc(s["g_ps"], 1)

            gate_up(0)
            for half in range(2):
                context(NG - 1, half)

            base = NP * STEPS0

            def down1(n):
                p, i = divmod(n, C1)
                u = base + n
                if i == 0:
                    claim(bank_y1, "y_sb", NP + p + 1)
                pe.wait_ge(s["high_ready"], u + 1)
                pe.wait_ge(s["low_ready"], u + 1)
                last = split_mm(bank_y1, 2 * FP + i * D, D, hidh[:, u % 3, :], hidl[:, u % 3, :],
                                i == 0, i == C1 - 1)
                last.then_inc(s["down_done"], 1)

            for n in range(NP * C1):
                p, i = divmod(n, C1)
                if n >= 1:
                    gate_up(n)
                if i == 0:
                    pe.wait_ge(s["wt_sb"], NP + p + 1)
                claim(bank_bc(n), "bc_read", NP * E * C0 + n + 1)
                mm(P[:, bank_bc(n), :], sel1[:, i * D:(i + 1) * D], WPT[:, p % 2, :], start=True, stop=True
                   ).then_inc(s["bc_ps"], 1)
                if n >= LAG:
                    down1(n - LAG)
                if n == 2:
                    weights_back(1, 1)
                if p in (1, 2):
                    if i == 2:
                        transpose_tokens(3, p + 1, MISC)
                    if i == 4:
                        route(1, p + 1)
                    if i == 11:
                        weights_back(1, p + 1)
                if p >= 1 and i == 7:
                    tokens_back(1, p - 1)
            for n in range(NP * C1 - LAG, NP * C1):
                down1(n)
            tokens_back(1, NP - 1)


bank_xt0 = [4, 5, 6, 7]
bank_ss = [0, 1, 2, 3]
bank_rn = [4, 5, 6, 5]
bank_q0 = [0, 1, 7, 5]
bank_v0 = [2, 3, 6, 7]
bank_tq = [4, 5, 7, 6]
bank_mod = [0, 2]
bank_gate = [7, 4, 6, 7]
MISC = 7
BANK_C1 = 6
bank_y0 = [5, 6, 5, 6]
bank_y1 = 5


def bank_up(u):
    return u % 3


def bank_bc(m):
    return 3 + m % 2


def bank_s0(b):
    return b % 2


def bank_pt(b):
    return 2 + b % 2


def bank_c0(b):
    return 4 + b % 2


def bank_s1(g, j):
    return 2 * ((2 * g + j // 2) % 3) + j % 2


def bank_g(n):
    return n % 2


def bank_u(n):
    return (2, 6)[n % 2]


_NAMED = ["L0_wmod", "L1_wmod", "L0_attn_anomaly_matrix", "L0_attn_bq", "L0_attn_bv",
          "L0_ffn_router_w", "L0_ffn_router_b", "L0_ffn_sw1", "L0_ffn_sw2", "L0_ffn_sb2",
          "L0_ffn_rw1", "L0_ffn_rw2", "L0_ffn_rb2", "L1_attn_Wq", "L1_attn_Wk", "L1_attn_Wv",
          "L1_attn_bq", "L1_attn_bk", "L1_attn_bv", "L1_ffn_w_gate", "L1_ffn_w_up",
          "L1_ffn_w_down", "L1_ffn_sw_gate", "L1_ffn_sw_up", "L1_ffn_sw_down"]


def kernel(**inputs):
    import numpy as np
    import concourse.bacc as bacc
    from concourse.bass_utils import run_bass_kernel_spmd as run

    arrays = {n: np.ascontiguousarray(inputs[n]) for n in _NAMED}

    def put(name, array):
        arrays[name] = np.ascontiguousarray(array)

    put("x", np.asarray(inputs["L0_attn_hidden_states"]).reshape(TOK, D))
    put("c0T", np.asarray(inputs["L0_c"]).T)
    put("c1T", np.asarray(inputs["L1_c"]).T)
    put("WqT0", np.asarray(inputs["L0_attn_Wq"]).T)
    put("WvT0", np.asarray(inputs["L0_attn_Wv"]).T)
    ub = np.concatenate([np.asarray(inputs["L0_ffn_rb1"]), np.asarray(inputs["L0_ffn_sb1"])[None]])
    put("ub0T", ub.reshape((E + 1) * C0, D).T)
    put("tempT", np.repeat(np.asarray(inputs["L1_attn_temperature"]).reshape(2, HEADS // 2), 2 * DH, axis=1).T)
    put("gate_wT", np.asarray(inputs["L1_ffn_gate_w"]).T)
    put("shared_gateT", np.asarray(inputs["L1_ffn_shared_gate_w"]).T)
    put("ident", np.eye(128, dtype=np.float32))
    put("iota", np.arange(E, dtype=np.float32))
    put("sel0", np.tile(np.repeat(np.eye(E, dtype=np.float32), D, axis=1), (3, 1)))
    sel1 = np.tile(np.repeat(np.eye(E + 1, dtype=np.float32), H1, axis=1), (3, 1))
    put("sel1", np.pad(sel1, ((0, 0), (0, FP - F1))))

    nc = bacc.Bacc("TRN2", target_bir_lowering=False, num_devices=1)
    aps = {n: nc.dram_tensor(f"in_{n}", v.shape, mybir.dt.float32, kind="ExternalInput").ap()
           for n, v in arrays.items()}
    out = nc.dram_tensor("out", (TOK, D), mybir.dt.float32, kind="ExternalOutput").ap()
    scratch = {"kv": nc.dram_tensor("kv_parts", (4, TOK, D), mybir.dt.float32, kind="Internal").ap(),
               "ao": nc.dram_tensor("attention_rows", (TOK, D), mybir.dt.float32, kind="Internal").ap()}
    two_block_adaln(nc, aps, out, scratch)
    r = run(nc, [{f"in_{n}": v for n, v in arrays.items()}], core_ids=[0])
    return r.results[0]["out"].reshape(B, S, D)
```
